# Optimizing a Trainium2 kernel written in Bass

```python
import numpy as np
import jax
import jax.numpy as jnp

def _softmax(x, axis=-1):
    return jax.nn.softmax(x, axis=axis)

def _gelu(x):
    return jax.nn.gelu(x, approximate=True)

def _silu(x):
    return jax.nn.silu(x)

def _sigmoid(x):
    return jax.nn.sigmoid(x)

def _layernorm(x, axis=-1, eps=1e-05):
    m = jnp.mean(x, axis=axis, keepdims=True)
    v = jnp.var(x, axis=axis, keepdims=True)
    return (x - m) / jnp.sqrt(v + eps)

def _scatter_add(tgt, idx, src, axis=0):
    return tgt.at[idx].add(src)

def _segment_sum(src, seg, n):
    return jax.ops.segment_sum(src, seg, n)
kernel_name = 'mk_xattn_ffn_d2_seqx_r4_af2aaa'

def setup_inputs(seed: int=0):
    np.random.seed(seed)
    _w = jnp.asarray

    def _rec_inputs():
        import jax
        import jax.numpy as jnp
        _rk = jax.random.key(seed)
        x = 7.22e-05 + 1 * jax.random.normal(jax.random.fold_in(_rk, 1), (16, 100, 256), jnp.float32)
        _lenS = 100 - jax.random.randint(jax.random.fold_in(_rk, 7), (16,), 0, max(1, 100 // 4) + 1, jnp.int32)
        _lenS2 = 361 - jax.random.randint(jax.random.fold_in(_rk, 8), (16,), 0, max(1, 361 // 4) + 1, jnp.int32)
        _ctx_1024P = jax.random.normal(jax.random.fold_in(_rk, 11), (16, 16, 256), jnp.float32)
        _ctx_1024c = jax.random.dirichlet(jax.random.fold_in(_rk, 511), 0.3 * jnp.ones((16,), jnp.float32), (16, 361))
        _ctx_1024t = jnp.einsum('bsk,bkd->bsd', _ctx_1024c, _ctx_1024P)
        _ctx_1024t = _ctx_1024t * jax.lax.rsqrt(jnp.mean(jnp.square(_ctx_1024t)) + 1e-12) * 0.953939
        ctx_1024 = 2.81802e-05 + 1.00001 * (_ctx_1024t + 0.3 * jax.random.normal(jax.random.fold_in(_rk, 611), (16, 361, 256), jnp.float32))
        _validS = jnp.arange(100)[None, :] < _lenS[:, None]
        _validS2 = jnp.arange(361)[None, :] < _lenS2[:, None]
        _causal = jnp.tril(jnp.ones((100, 100), dtype=bool))
        mask_BxS2_ik1 = jnp.where(jnp.broadcast_to(_validS2[:, :], (16, 361)), 1, 0).astype(jnp.int32)
        return (x, ctx_1024, mask_BxS2_ik1)
    x, ctx_1024, mask_BxS2_ik1 = _rec_inputs()

    def _L0_xattn_setup():
        import jax, jax.numpy as jnp
        import numpy as np
        B, T, S, D = (4, 512, 1024, 256)
        TOP_K = 32

        def _read(query, mem_state, top_k, Wq, bq, Wk, bk, Wv, bv, Wo, bo):
            b, t, d = query.shape
            s = mem_state.shape[1]
            scale = 1.0 / np.sqrt(d)
            q = query @ Wq.T + bq
            k = mem_state @ Wk.T + bk
            v = mem_state @ Wv.T + bv
            scores = jnp.einsum('btd,bsd->bts', q, k) * scale
            if top_k < s:
                vals, idx = jax.lax.top_k(scores, top_k)
                b_ix = jnp.arange(b)[:, None, None]
                t_ix = jnp.arange(t)[None, :, None]
                masked = jnp.full_like(scores, -jnp.inf)
                scores = masked.at[b_ix, t_ix, idx].set(vals)
            attn = jax.nn.softmax(scores, axis=-1)
            ctx = jnp.einsum('bts,bsd->btd', attn, v)
            return ctx @ Wo.T + bo
        key = jax.random.key(seed)
        ks = jax.random.split(key, 12)
        std = 0.02
        inp = {'query': jax.random.normal(ks[0], (B, T, D), dtype=jnp.float32), 'mem_state': jax.random.normal(ks[1], (B, S, D), dtype=jnp.float32), 'top_k': TOP_K, 'Wq': jax.random.normal(ks[2], (D, D), dtype=jnp.float32) * std, 'bq': jnp.zeros((D,), dtype=jnp.float32), 'Wk': jax.random.normal(ks[3], (D, D), dtype=jnp.float32) * std, 'bk': jnp.zeros((D,), dtype=jnp.float32), 'Wv': jax.random.normal(ks[4], (D, D), dtype=jnp.float32) * std, 'bv': jnp.zeros((D,), dtype=jnp.float32), 'Wo': jax.random.normal(ks[5], (D, D), dtype=jnp.float32) * std, 'bo': jnp.zeros((D,), dtype=jnp.float32)}
        return inp
    _L0_xattn_all = _L0_xattn_setup()
    _L0_xattn_in = {k: v for k, v in _L0_xattn_all.items() if k in ('Wq', 'bq', 'Wk', 'bk', 'Wv', 'bv', 'Wo', 'bo')}
    del _L0_xattn_all

    def _L0_ffn_setup():
        import jax, jax.numpy as jnp
        import numpy as np
        S_LEN, BATCH, HIDDEN = (512, 2, 256)
        N_HEADS, N_KV = (16, 8)
        N_EXP, TOP_K, CAP_F = (8, 2, 1.25)
        FFN = 1024
        HEAD_DIM = HIDDEN // N_HEADS
        Q_PER_KV = N_HEADS // N_KV
        EPS = 1e-05
        NEG = -1000000000.0

        def _ln(x, w, b):
            mu = jnp.mean(x, -1, keepdims=True)
            var = jnp.var(x, -1, keepdims=True)
            return (x - mu) * jax.lax.rsqrt(var + EPS) * w + b

        def _forward(hidden_states, ln1_weight, ln1_bias, ln2_weight, ln2_bias, qkv_weight, proj_weight, router_weight, moe_w1, moe_w2):
            S, B, H = hidden_states.shape
            ln1 = _ln(hidden_states, ln1_weight, ln1_bias)
            qkv = (ln1 @ qkv_weight.T).reshape(S, B, N_KV, (Q_PER_KV + 2) * HEAD_DIM)
            q_dim = Q_PER_KV * HEAD_DIM
            q = qkv[..., :q_dim].reshape(S, B, N_HEADS, HEAD_DIM)
            k = jnp.repeat(qkv[..., q_dim:q_dim + HEAD_DIM], Q_PER_KV, axis=2)
            v = jnp.repeat(qkv[..., q_dim + HEAD_DIM:], Q_PER_KV, axis=2)
            scores = jnp.einsum('sbhd,tbhd->bhst', q, k) / jnp.sqrt(jnp.float32(HEAD_DIM))
            causal = jnp.tril(jnp.ones((S, S), bool))
            attn = jax.nn.softmax(jnp.where(causal[None, None], scores, NEG), axis=-1)
            attn_out = jnp.einsum('bhst,tbhd->sbhd', attn, v).reshape(S, B, H)
            hidden_after_attn = hidden_states + attn_out @ proj_weight.T
            x = _ln(hidden_after_attn, ln2_weight, ln2_bias).reshape(-1, H)
            N = S * B
            probs = jax.nn.softmax(x.astype(jnp.float32) @ router_weight, axis=-1)
            top_p, top_i = jax.lax.top_k(probs, TOP_K)
            top_p = top_p / jnp.sum(top_p, -1, keepdims=True)
            flat_exp = top_i.reshape(-1)
            order = jnp.argsort(flat_exp)
            sorted_exp = flat_exp[order]
            counts = jnp.bincount(sorted_exp, length=N_EXP)
            offsets = jnp.concatenate([jnp.zeros((1,), counts.dtype), jnp.cumsum(counts)])
            within = jnp.arange(N * TOP_K) - offsets[sorted_exp]
            cap = int(np.ceil(N * TOP_K / N_EXP * CAP_F))
            keep = within < cap
            slot = jnp.where(keep, sorted_exp * cap + within, N_EXP * cap)
            tok_id = order // TOP_K
            padded_tokens = jnp.zeros((N_EXP * cap + 1, H), x.dtype).at[slot].set(x[tok_id])[:-1]
            padded_probs = jnp.zeros((N_EXP * cap + 1,), jnp.float32).at[slot].set(top_p.reshape(-1)[order])[:-1]
            padded_ids = jnp.zeros((N_EXP * cap + 1,), jnp.int32).at[slot].set(tok_id.astype(jnp.int32))[:-1]
            exp_in = padded_tokens.reshape(N_EXP, cap, H)
            act = jax.nn.gelu(jnp.einsum('ech,ehf->ecf', exp_in, moe_w1), approximate=False)
            exp_out = jnp.einsum('ecf,efh->ech', act, moe_w2).reshape(N_EXP * cap, H)
            weighted = exp_out * padded_probs[:, None].astype(exp_out.dtype)
            moe = jnp.zeros((N, H), exp_out.dtype).at[padded_ids].add(weighted)
            return hidden_after_attn + moe.reshape(S, B, H)
        ks = jax.random.split(jax.random.key(seed), 6)
        qkv_out = N_KV * (Q_PER_KV + 2) * HEAD_DIM
        sc = 0.02
        return {'hidden_states': jax.random.normal(ks[0], (S_LEN, BATCH, HIDDEN), jnp.float32), 'ln1_weight': jnp.ones((HIDDEN,), jnp.float32), 'ln1_bias': jnp.zeros((HIDDEN,), jnp.float32), 'ln2_weight': jnp.ones((HIDDEN,), jnp.float32), 'ln2_bias': jnp.zeros((HIDDEN,), jnp.float32), 'qkv_weight': jax.random.normal(ks[1], (qkv_out, HIDDEN), jnp.float32) * sc, 'proj_weight': jax.random.normal(ks[2], (HIDDEN, HIDDEN), jnp.float32) * sc, 'router_weight': jax.random.normal(ks[3], (HIDDEN, N_EXP), jnp.float32) * sc, 'moe_w1': jax.random.normal(ks[4], (N_EXP, HIDDEN, FFN), jnp.float32) * sc, 'moe_w2': jax.random.normal(ks[5], (N_EXP, FFN, HIDDEN), jnp.float32) * sc}
    _L0_ffn_all = _L0_ffn_setup()
    _L0_ffn_in = {k: v for k, v in _L0_ffn_all.items() if k in ('ln1_weight', 'ln1_bias', 'ln2_weight', 'ln2_bias', 'qkv_weight', 'proj_weight', 'router_weight', 'moe_w1', 'moe_w2')}
    del _L0_ffn_all

    def _L1_xattn_setup():
        import jax, jax.numpy as jnp
        import numpy as np
        MASK_FILL = -99999.0
        key = jax.random.key(seed)
        k1, k2, k3, k4, k5, k6, k7 = jax.random.split(key, 7)
        B, S, H = (8, 512, 256)
        query = jax.random.normal(k1, (B, S, H), dtype=jnp.float32)
        key_t = jax.random.normal(k2, (B, S, H), dtype=jnp.float32)
        value = jax.random.normal(k3, (B, S, H), dtype=jnp.float32)
        mask = jax.random.randint(k4, (B, S), 0, 2, dtype=jnp.int32)
        s = 1.0 / np.sqrt(H)
        Wq = jax.random.uniform(k5, (H, H), dtype=jnp.float32, minval=-s, maxval=s)
        Wk = jax.random.uniform(k6, (H, H), dtype=jnp.float32, minval=-s, maxval=s)
        Wv = jax.random.uniform(k7, (H, H), dtype=jnp.float32, minval=-s, maxval=s)
        return {'query': query, 'key': key_t, 'value': value, 'Wq': Wq, 'Wk': Wk, 'Wv': Wv, 'mask': mask}
    _L1_xattn_all = _L1_xattn_setup()
    _L1_xattn_in = {k: v for k, v in _L1_xattn_all.items() if k in ('Wq', 'Wk', 'Wv')}
    del _L1_xattn_all

    def _L1_ffn_setup():
        import jax, jax.numpy as jnp
        import numpy as np
        key = jax.random.key(seed)
        ks = jax.random.split(key, 6)
        B, L, D, E = (4, 512, 256, 4)
        H = 4 * D
        x = jax.random.normal(ks[0], (B, L, D), dtype=jnp.float32)
        rW1 = jax.random.normal(ks[1], (D, 2 * D), dtype=jnp.float32) * (2.0 / D) ** 0.5
        rb1 = jnp.zeros((2 * D,), dtype=jnp.float32)
        rW2 = jax.random.normal(ks[2], (2 * D, E), dtype=jnp.float32) * (2.0 / (2 * D)) ** 0.5
        rb2 = jnp.zeros((E,), dtype=jnp.float32)
        We1 = jax.random.normal(ks[3], (E, D, H), dtype=jnp.float32) * (2.0 / D) ** 0.5
        be1 = jnp.zeros((E, H), dtype=jnp.float32)
        We2 = jax.random.normal(ks[4], (E, H, D), dtype=jnp.float32) * (2.0 / H) ** 0.5
        be2 = jnp.zeros((E, D), dtype=jnp.float32)
        return {'x': x, 'rW1': rW1, 'rb1': rb1, 'rW2': rW2, 'rb2': rb2, 'We1': We1, 'be1': be1, 'We2': We2, 'be2': be2}
    _L1_ffn_all = _L1_ffn_setup()
    _L1_ffn_in = {k: v for k, v in _L1_ffn_all.items() if k in ('rW1', 'rb1', 'rW2', 'rb2', 'We1', 'be1', 'We2', 'be2')}
    del _L1_ffn_all
    return {'x': x, 'ctx_1024': ctx_1024, 'mask_BxS2_ik1': mask_BxS2_ik1, 'L0_xattn_Wq': _L0_xattn_in['Wq'], 'L0_xattn_bq': _L0_xattn_in['bq'], 'L0_xattn_Wk': _L0_xattn_in['Wk'], 'L0_xattn_bk': _L0_xattn_in['bk'], 'L0_xattn_Wv': _L0_xattn_in['Wv'], 'L0_xattn_bv': _L0_xattn_in['bv'], 'L0_xattn_Wo': _L0_xattn_in['Wo'], 'L0_xattn_bo': _L0_xattn_in['bo'], 'L0_ffn_ln1_weight': _L0_ffn_in['ln1_weight'], 'L0_ffn_ln1_bias': _L0_ffn_in['ln1_bias'], 'L0_ffn_ln2_weight': _L0_ffn_in['ln2_weight'], 'L0_ffn_ln2_bias': _L0_ffn_in['ln2_bias'], 'L0_ffn_qkv_weight': _L0_ffn_in['qkv_weight'], 'L0_ffn_proj_weight': _L0_ffn_in['proj_weight'], 'L0_ffn_router_weight': _L0_ffn_in['router_weight'], 'L0_ffn_moe_w1': _L0_ffn_in['moe_w1'], 'L0_ffn_moe_w2': _L0_ffn_in['moe_w2'], 'L1_xattn_Wq': _L1_xattn_in['Wq'], 'L1_xattn_Wk': _L1_xattn_in['Wk'], 'L1_xattn_Wv': _L1_xattn_in['Wv'], 'L1_ffn_rW1': _L1_ffn_in['rW1'], 'L1_ffn_rb1': _L1_ffn_in['rb1'], 'L1_ffn_rW2': _L1_ffn_in['rW2'], 'L1_ffn_rb2': _L1_ffn_in['rb2'], 'L1_ffn_We1': _L1_ffn_in['We1'], 'L1_ffn_be1': _L1_ffn_in['be1'], 'L1_ffn_We2': _L1_ffn_in['We2'], 'L1_ffn_be2': _L1_ffn_in['be2']}

def reference(x, ctx_1024, mask_BxS2_ik1, L0_xattn_Wq, L0_xattn_bq, L0_xattn_Wk, L0_xattn_bk, L0_xattn_Wv, L0_xattn_bv, L0_xattn_Wo, L0_xattn_bo, L0_ffn_ln1_weight, L0_ffn_ln1_bias, L0_ffn_ln2_weight, L0_ffn_ln2_bias, L0_ffn_qkv_weight, L0_ffn_proj_weight, L0_ffn_router_weight, L0_ffn_moe_w1, L0_ffn_moe_w2, L1_xattn_Wq, L1_xattn_Wk, L1_xattn_Wv, L1_ffn_rW1, L1_ffn_rb1, L1_ffn_rW2, L1_ffn_rb2, L1_ffn_We1, L1_ffn_be1, L1_ffn_We2, L1_ffn_be2):
    import jax
    import jax.numpy as jnp

    def _L0_xattn_ref(query, mem_state, top_k, Wq, bq, Wk, bk, Wv, bv, Wo, bo):
        import jax, jax.numpy as jnp
        import numpy as np
        B, T, S, D = (4, 512, 1024, 256)
        TOP_K = 32

        def _read(query, mem_state, top_k, Wq, bq, Wk, bk, Wv, bv, Wo, bo):
            b, t, d = query.shape
            s = mem_state.shape[1]
            scale = 1.0 / np.sqrt(d)
            q = query @ Wq.T + bq
            k = mem_state @ Wk.T + bk
            v = mem_state @ Wv.T + bv
            scores = jnp.einsum('btd,bsd->bts', q, k) * scale
            if top_k < s:
                vals, idx = jax.lax.top_k(scores, top_k)
                b_ix = jnp.arange(b)[:, None, None]
                t_ix = jnp.arange(t)[None, :, None]
                masked = jnp.full_like(scores, -jnp.inf)
                scores = masked.at[b_ix, t_ix, idx].set(vals)
            attn = jax.nn.softmax(scores, axis=-1)
            ctx = jnp.einsum('bts,bsd->btd', attn, v)
            return ctx @ Wo.T + bo
        return _read(query, mem_state, top_k, Wq, bq, Wk, bk, Wv, bv, Wo, bo)

    def _L0_ffn_ref(hidden_states, ln1_weight, ln1_bias, ln2_weight, ln2_bias, qkv_weight, proj_weight, router_weight, moe_w1, moe_w2):
        import jax, jax.numpy as jnp
        import numpy as np
        S_LEN, BATCH, HIDDEN = (512, 2, 256)
        N_HEADS, N_KV = (16, 8)
        N_EXP, TOP_K, CAP_F = (8, 2, 1.25)
        FFN = 1024
        HEAD_DIM = HIDDEN // N_HEADS
        Q_PER_KV = N_HEADS // N_KV
        EPS = 1e-05
        NEG = -1000000000.0

        def _ln(x, w, b):
            mu = jnp.mean(x, -1, keepdims=True)
            var = jnp.var(x, -1, keepdims=True)
            return (x - mu) * jax.lax.rsqrt(var + EPS) * w + b

        def _forward(hidden_states, ln1_weight, ln1_bias, ln2_weight, ln2_bias, qkv_weight, proj_weight, router_weight, moe_w1, moe_w2):
            S, B, H = hidden_states.shape
            ln1 = _ln(hidden_states, ln1_weight, ln1_bias)
            qkv = (ln1 @ qkv_weight.T).reshape(S, B, N_KV, (Q_PER_KV + 2) * HEAD_DIM)
            q_dim = Q_PER_KV * HEAD_DIM
            q = qkv[..., :q_dim].reshape(S, B, N_HEADS, HEAD_DIM)
            k = jnp.repeat(qkv[..., q_dim:q_dim + HEAD_DIM], Q_PER_KV, axis=2)
            v = jnp.repeat(qkv[..., q_dim + HEAD_DIM:], Q_PER_KV, axis=2)
            scores = jnp.einsum('sbhd,tbhd->bhst', q, k) / jnp.sqrt(jnp.float32(HEAD_DIM))
            causal = jnp.tril(jnp.ones((S, S), bool))
            attn = jax.nn.softmax(jnp.where(causal[None, None], scores, NEG), axis=-1)
            attn_out = jnp.einsum('bhst,tbhd->sbhd', attn, v).reshape(S, B, H)
            hidden_after_attn = hidden_states + attn_out @ proj_weight.T
            x = _ln(hidden_after_attn, ln2_weight, ln2_bias).reshape(-1, H)
            N = S * B
            probs = jax.nn.softmax(x.astype(jnp.float32) @ router_weight, axis=-1)
            top_p, top_i = jax.lax.top_k(probs, TOP_K)
            top_p = top_p / jnp.sum(top_p, -1, keepdims=True)
            flat_exp = top_i.reshape(-1)
            order = jnp.argsort(flat_exp)
            sorted_exp = flat_exp[order]
            counts = jnp.bincount(sorted_exp, length=N_EXP)
            offsets = jnp.concatenate([jnp.zeros((1,), counts.dtype), jnp.cumsum(counts)])
            within = jnp.arange(N * TOP_K) - offsets[sorted_exp]
            cap = int(np.ceil(N * TOP_K / N_EXP * CAP_F))
            keep = within < cap
            slot = jnp.where(keep, sorted_exp * cap + within, N_EXP * cap)
            tok_id = order // TOP_K
            padded_tokens = jnp.zeros((N_EXP * cap + 1, H), x.dtype).at[slot].set(x[tok_id])[:-1]
            padded_probs = jnp.zeros((N_EXP * cap + 1,), jnp.float32).at[slot].set(top_p.reshape(-1)[order])[:-1]
            padded_ids = jnp.zeros((N_EXP * cap + 1,), jnp.int32).at[slot].set(tok_id.astype(jnp.int32))[:-1]
            exp_in = padded_tokens.reshape(N_EXP, cap, H)
            act = jax.nn.gelu(jnp.einsum('ech,ehf->ecf', exp_in, moe_w1), approximate=False)
            exp_out = jnp.einsum('ecf,efh->ech', act, moe_w2).reshape(N_EXP * cap, H)
            weighted = exp_out * padded_probs[:, None].astype(exp_out.dtype)
            moe = jnp.zeros((N, H), exp_out.dtype).at[padded_ids].add(weighted)
            return hidden_after_attn + moe.reshape(S, B, H)
        return _forward(hidden_states, ln1_weight, ln1_bias, ln2_weight, ln2_bias, qkv_weight, proj_weight, router_weight, moe_w1, moe_w2)

    def _L1_xattn_ref(query, key, value, Wq, Wk, Wv, mask):
        import jax, jax.numpy as jnp
        import numpy as np
        MASK_FILL = -99999.0
        q = jnp.einsum('bsh,oh->bso', query, Wq)
        k = jnp.einsum('bsh,oh->bso', key, Wk)
        v = jnp.einsum('bsh,oh->bso', value, Wv)
        score = jnp.einsum('bqh,bkh->bqk', q, k)
        m = mask[:, None, :]
        score = jnp.where(m == 0, jnp.float32(MASK_FILL), score)
        attn = jax.nn.softmax(score, axis=-1)
        context = jnp.einsum('bqk,bkh->bqh', attn, v)
        return context

    def _L1_ffn_ref(x, rW1, rb1, rW2, rb2, We1, be1, We2, be2):
        import jax, jax.numpy as jnp
        import numpy as np
        E = We1.shape[0]
        top_k = min(2, E)
        rh = jax.nn.gelu(x @ rW1 + rb1, approximate=False)
        router_logits = rh @ rW2 + rb2
        router_probs = jax.nn.softmax(router_logits, axis=-1)
        expert_weights, expert_indices = jax.lax.top_k(router_probs, top_k)
        one_hot = jax.nn.one_hot(expert_indices, E, dtype=x.dtype)
        token_mask = one_hot.sum(axis=2)
        combine_w = (one_hot * expert_weights[..., None]).sum(axis=2)
        out = jnp.zeros_like(x)
        for e in range(E):
            xi = x * token_mask[..., e:e + 1]
            h = jax.nn.gelu(xi @ We1[e] + be1[e], approximate=False)
            yo = h @ We2[e] + be2[e]
            out = out + yo * combine_w[..., e:e + 1]
        return out
    x = x + _L0_xattn_ref(_layernorm(x, axis=-1), ctx_1024, 32, L0_xattn_Wq, L0_xattn_bq, L0_xattn_Wk, L0_xattn_bk, L0_xattn_Wv, L0_xattn_bv, L0_xattn_Wo, L0_xattn_bo)
    x = x + _L0_ffn_ref(_layernorm(x, axis=-1), L0_ffn_ln1_weight, L0_ffn_ln1_bias, L0_ffn_ln2_weight, L0_ffn_ln2_bias, L0_ffn_qkv_weight, L0_ffn_proj_weight, L0_ffn_router_weight, L0_ffn_moe_w1, L0_ffn_moe_w2)
    x = x + _L1_xattn_ref(_layernorm(x, axis=-1), ctx_1024, ctx_1024, L1_xattn_Wq, L1_xattn_Wk, L1_xattn_Wv, mask_BxS2_ik1)
    x = x + _L1_ffn_ref(_layernorm(x, axis=-1), L1_ffn_rW1, L1_ffn_rb1, L1_ffn_rW2, L1_ffn_rb2, L1_ffn_We1, L1_ffn_be1, L1_ffn_We2, L1_ffn_be2)
    return x

_drawn_inputs = setup_inputs


def setup_inputs(seed=0):
    import zlib

    import numpy as np

    out = dict(_drawn_inputs(seed))
    spreads = {'L0_xattn_bq': (0.0, 0.1),
     'L0_xattn_bk': (0.0, 0.8),
     'L0_xattn_bv': (0.0, 0.1),
     'L0_xattn_bo': (0.0, 0.1),
     'L0_ffn_ln1_weight': (1.0, 0.6),
     'L0_ffn_ln1_bias': (0.0, 0.544),
     'L0_ffn_ln2_weight': (1.0, 0.54),
     'L0_ffn_ln2_bias': (0.0, 0.33),
     'L1_ffn_rb1': (0.0, 0.1),
     'L1_ffn_rb2': (0.0, 0.1),
     'L1_ffn_be1': (0.0, 0.27),
     'L1_ffn_be2': (0.0, 0.1)}
    factors = {}
    for name, (base, spread) in spreads.items():
        noise = np.random.default_rng([zlib.crc32(name.encode()), seed]).standard_normal(out[name].shape)
        drawn = base * np.exp(spread * noise) if base else spread * noise
        out[name] = jnp.asarray(drawn.astype(out[name].dtype))
    for name, factor in factors.items():
        out[name] = (out[name] * factor).astype(out[name].dtype)
    return out
```

```python
from contextlib import ExitStack, contextmanager

import numpy as np

import concourse.bass as bass
import concourse.mybir as mybir

F32 = mybir.dt.float32
F32R = mybir.dt.float32r
I32 = mybir.dt.int32
U32 = mybir.dt.uint32
ALU = mybir.AluOpType
ACT = mybir.ActivationFunctionType
AX = mybir.AxisListType

S, B, D = 16, 100, 256
CTX = 361
P = 128
DC = D // P
CK = [128, 128, CTX - 256]
G, HD, T = 8, 16, 16
QJ = 2
FFN = 1024
FC = FFN // P
E0, CAP = 8, 500
ROWS0, SUB0 = 125, 4
E1 = 4
ROWS1, SUB1 = 128, 3
TILE1 = ROWS1 * SUB1
TILES1 = (2 * S * B + E1 * (TILE1 - 1)) // TILE1
RH = 2 * D
TOPK = 32
EPS = 1e-5
GONE = -3.0e38
NEG = -1.0e30
CREDIT = 2


def done(s):
    return s + 1 + CREDIT


def reuse(s):
    return s - 1 + CREDIT


@contextmanager
def semaphores(nc):
    own = []

    def allocate(name):
        own.append(nc.alloc_semaphore(name))
        return own[-1]

    yield allocate
    nc.clear_and_free_semaphores(own)
    nc.all_engine_barrier()


def carry(eng, passed):
    eng.sem_inc(passed, 1)


class Batch:

    def __init__(self, first, loop=0):
        self.first, self.loop = first, loop
        self.s, self.u, self.h = first + 2 * loop, first % 2, first // 2 + loop
        self.looped = not isinstance(loop, int)
        self.loaded = 16 * self.h + 16

    def plus(self, d):
        return Batch(self.first + d, self.loop)


def pipeline(eng, stages, count=S):
    least, most = min(o for _, o in stages), max(o for _, o in stages)
    start = max(-least, 0)
    pairs = (count - most - start) // 2

    def step(n, loop=0, full=False):
        for stage, offset in stages:
            if full or 0 <= n + offset < count:
                stage(Batch(n + offset, loop))

    for n in range(-most, start):
        step(n)
    with eng.Fori(0, pairs) as i:
        step(start, i, True)
        step(start + 1, i, True)
    for n in range(start + 2 * pairs, count - least):
        step(n)


def first_cross_attention(nc, io, keep):
    with ExitStack() as ctx:
        sb = lambda name, shape, dt=F32: ctx.enter_context(nc.sbuf_tensor(name, shape, dt))
        own = ctx.enter_context(semaphores(nc))
        sem = lambda name: own(name)
        psum = lambda name: ctx.enter_context(nc.psum_tensor(name, [P, 512], F32))

        w_a = sb("w_a", [P, DC, 4 * D])
        wq, wk, wv, woT = (w_a[:, :, k * D:(k + 1) * D] for k in range(4))
        wqkvT = sb("wqkvT", [P, DC, 4 * P])
        rows_sb = sb("rows_a", [1, D])
        ones = sb("ones_a", [1, P])
        A = sb("A", [P, DC, D])
        wqbk = sb("wqbk", [P, DC])
        Wov = sb("Wov", [P, DC, D])
        bqWk = sb("bqWk", [P, DC])
        bcast = sb("bcast", [P, 2, DC, P])
        qbk0 = sb("qbk0", [P, 1])
        orow = sb("orow", [P, D])

        ctxT = sb("ctxT", [P, 2, DC, CTX])
        ctxN = sb("ctxN", [P, 2, 3, D])
        st = sb("st", [P, 2, 2, 6])
        mv = sb("mv", [P, 2, 2, 2])
        ve = sb("ve", [P, 2, 3])
        rs = sb("rs", [P, 2, 3])
        v2 = sb("v2", [P, 2])
        y = sb("y", [P, 2, D])
        yT = sb("yT", [P, 2, DC, B])
        qT = sb("qT", [P, 2, DC, B])
        qb = sb("qb", [P, 2])
        sc = sb("sc", [P, 2, CTX])
        left = sb("left", [P, CTX])
        top = sb("top", [P, 2, 8])
        best = sb("best", [P, 2, 8])
        nmax = sb("nmax", [P, 2])
        ex = sb("ex", [P, 2, CTX])
        pr = sb("pr", [P, 2, CTX])
        psums = sb("psums", [P, 2])
        pinv = sb("pinv", [P, 2])
        prT = sb("prT", [P, 2, 3, B])
        avT = sb("avT", [P, 2, DC, B])
        z = sb("z", [P, 2, D])
        zT = sb("zT", [P, 2, DC, B])
        V = sb("V", [P, 2, P])

        ps_t, ps_q = psum("ps_t"), psum("ps_q")
        ps_s = [psum("ps_s0"), psum("ps_s1")]
        ps_p, ps_av, ps_o, ps_qkv = psum("ps_p"), psum("ps_av"), psum("ps_o"), psum("ps_qkv")

        ld_w, ld_x, ld_rows, ld_qkv = sem("ld_w"), sem("ld_x"), sem("ld_rows"), sem("ld_qkv")
        ld_ct = [sem("ld_ct0"), sem("ld_ct1")]
        ld_cn = [sem("ld_cn0"), sem("ld_cn1")]
        st_v = [sem("st_v0"), sem("st_v1")]
        fold_in, folded, fold_out = sem("fold_in"), sem("folded"), sem("fold_out")
        s_yT, s_q, s_sc, s_prT, s_av, s_out, s_zT, s_qkv = pe_sems = [
            sem(n) for n in ("yT_ps", "q_ps", "sc_ps", "prT_ps", "av_ps", "out_ps", "zT_ps", "qkv_ps")]
        a_yT, a_q, a_sc, a_ex, a_prT, a_av, a_zT, a_qkv = act_sems = [
            sem(n) for n in ("yT_sb", "q_sb", "sc_sb", "exp_sb", "prT_sb", "av_sb", "zT_sb", "qkv_sb")]
        d_st, d_mv, d_y, d_top, d_max, d_left, d_pr, d_inv, d_x1, d_st1, d_mv1, d_y1, d_v2, d_z = dve_sems = [
            sem(n) for n in ("st", "mv_r", "y_r", "top_r", "max_r", "left_r", "pr_r", "inv_r", "x1_r",
                             "st1_r", "mv1_r", "y1_r", "v2_r", "z_r")]
        g_ve, g_rs, g_row, g_ve1, g_rs1, g_ve2, g_rs2 = pool_sems = [
            sem(n) for n in ("ve_r", "rs_r", "row_r", "ve1_r", "rs1_r", "ve2_r", "rs2_r")]
        g_const = sem("g_const_a")
        passed = sem("passed")

        X, Y1, Q, K = keep.X, keep.Y1, keep.Q, keep.K
        ident, half = keep.ident, keep.half
        col = keep.col
        block = ctx.enter_context(nc.Block())

        @block.sync
        def _(sp):
            sp.dma_start(keep.consts[:, :], io.consts).then_inc(keep.ld_consts, 16)
            sp.dma_start(w_a[:, :, :], io.w_a).then_inc(ld_w, 16)
            sp.dma_start(rows_sb[:, :], io.rows[:, 0:D]).then_inc(ld_rows, 16)
            sp.dma_start(wqkvT[:, :, :], io.w_qkvT).then_inc(ld_qkv, 16)

            def load_T(b):
                sp.wait_ge(s_sc, reuse(b.s))
                sp.dma_start(ctxT[:, b.u, :, :], io.ctxT[b.s]).then_inc(ld_ct[b.u], 16)

            def load_N(b):
                sp.wait_ge(s_av, reuse(b.s))
                sp.dma_start(ctxN[:, b.u, 0:2, :],
                             io.ctx[b.s, 0:2 * P, :].rearrange("(c p) d -> p c d", p=P)).then_inc(ld_cn[b.u], 16)
                sp.dma_start(ctxN[0:CK[2], b.u, 2, :], io.ctx[b.s, 2 * P:CTX, :]).then_inc(ld_cn[b.u], 16)

            def store_v(b):
                sp.wait_ge(a_qkv, done(b.s))
                sp.dma_start(keep.values[b.s], V[0:B, b.u, :]).then_inc(st_v[b.u], 16)

            for x in st_v:
                sp.sem_inc(x, 16)
            sp.wait_ge(g_const, 3)
            for slots, rows in ((keep.slots0, ROWS0), (keep.slots1, ROWS1)):
                sp.dma_start(slots.rearrange("(a p) f -> p a f", p=rows),
                             keep.zeros[0:rows, :].unsqueeze(1).to_broadcast(
                                 [rows, slots.shape[0] // rows, D])).then_inc(keep.zeroed, 16)

            pipeline(sp, [(load_T, 2), (store_v, -1), (load_N, 1)])
            for x in st_v:
                sp.wait_ge(x, 16 * (S // 2) + 16)

        @block.scalar
        def _(act):
            act.dma_start(X[0:B, :, :], io.x.rearrange("s b d -> b s d")).then_inc(ld_x, 16)
            for x in act_sems:
                act.sem_inc(x, CREDIT)
            act.wait_ge(keep.ld_consts, 16)
            act.wait_ge(g_const, 3)
            for k, name in enumerate(("bq", "bv")):
                for c in range(DC):
                    last = act.activation(bcast[:, k, c, :], keep.zeros[:, 0:P], ACT.Identity, bias=col(name, c))
            last.then_inc(fold_in, 1)
            act.wait_ge(folded, 1)
            act.copy(A[:, 0, :], ps_t[:, 0:D]).then_inc(fold_out, 1)
            act.copy(A[:, 1, :], ps_q[:, 0:D]).then_inc(fold_out, 1)
            act.copy(Wov[:, 0, :], ps_s[0][:, 0:D]).then_inc(fold_out, 1)
            act.copy(Wov[:, 1, :], ps_s[1][:, 0:D]).then_inc(fold_out, 1)
            act.copy(orow[:, :], ps_o[:, 0:D]).then_inc(fold_out, 1)
            act.copy(wqbk[:, :], ps_p[:, 0:DC]).then_inc(fold_out, 1)
            act.copy(bqWk[:, :], ps_p[:, DC:2 * DC]).then_inc(fold_out, 1)
            act.copy(qbk0[:, :], ps_p[:, 4:5]).then_inc(fold_out, 1)
            act.wait_ge(fold_out, 8)

            def query(b):
                act.wait_ge(s_yT, done(b.s))
                act.copy(yT[:, b.u, :, :], ps_t[:, 0:DC * B]).then_inc(a_yT, 1)
                act.wait_ge(s_q, done(b.s))
                for c in range(DC):
                    act.activation(qT[:, b.u, c, :], ps_q[:, c * B:(c + 1) * B], ACT.Identity,
                                          bias=bqWk[:, c:c + 1])
                act.wait_ge(a_sc, reuse(b.s))
                act.activation(qb[0:B, b.u:b.u + 1], ps_q[0:B, 2 * B:2 * B + 1], ACT.Identity,
                               bias=qbk0[0:B, :]).then_inc(a_q, 1)
                act.wait_ge(s_sc, done(b.s))
                act.wait_ge(a_q, done(b.s))
                act.wait_ge(d_pr, reuse(b.s))
                act.activation(sc[0:B, b.u, :], ps_s[b.u][0:B, 0:CTX], ACT.Identity,
                               bias=qb[0:B, b.u:b.u + 1]).then_inc(a_sc, 1)

            def exponent(b):
                act.wait_ge(d_max, done(b.s))
                act.activation(ex[0:B, b.u, :], sc[0:B, b.u, :], ACT.Exp, bias=nmax[0:B, b.u:b.u + 1],
                               scale=1.0 / D ** 0.5).then_inc(a_ex, 1)

            def attend(b):
                act.wait_ge(s_prT, done(b.s))
                act.copy(prT[:, b.u, 0:2, :], ps_p[:, 0:2 * B])
                act.copy(prT[0:CK[2], b.u, 2, :], ps_p[0:CK[2], 2 * B:3 * B]).then_inc(a_prT, 1)
                act.wait_ge(s_av, done(b.s))
                act.copy(avT[:, b.u, :, :], ps_av[:, 0:DC * B]).then_inc(a_av, 1)

            def project(b):
                act.wait_ge(s_zT, done(b.s))
                for c in range(DC):
                    last = act.activation(zT[:, b.u, c, :], ps_t[:, 200 + c * B:200 + (c + 1) * B], ACT.Identity,
                                          bias=col("ln1b", c), scale=col("ln1w", c))
                last.then_inc(a_zT, 1)
                act.wait_ge(s_qkv, done(b.s))
                act.wait_ge(st_v[b.u], b.loaded)
                act.copy(K[:, :, b.s], ps_qkv[:, 2 * B:3 * B])
                act.copy(Q[:, :, :, b.s].rearrange("p b j -> p j b"),
                         ps_qkv[:, 0:2 * B].rearrange("p (j b) -> p j b", j=QJ))
                act.copy(V[0:B, b.u, :], ps_qkv[0:B, 3 * B:3 * B + P]).then_inc(a_qkv, 1)

            pipeline(act, [(attend, -1), (exponent, 0), (query, 1), (project, -1)])

        @block.gpsimd
        def _(pool):
            pool.memset(ones[:, :], 1.0).then_inc(g_const, 1)
            pool.memset(half[:, 0:1], -0.5).then_inc(g_const, 1)
            pool.memset(keep.zeros[:, :], 0.0).then_inc(g_const, 1)
            for x in pool_sems:
                pool.sem_inc(x, CREDIT)
            for b in range(0, B, B // 4):
                pool.memset(keep.VX[:, b:b + B // 4, :], 0.0).then_inc(keep.vx_zero, 1)
            pool.wait_ge(g_const, 3)
            pool.wait_ge(keep.ld_consts, 16)
            pool.wait_ge(fold_out, 8)

            def rsqrt(k, b, var, ready, plus_eps, power):
                pool.wait_ge(ready, done(b.s))
                pool.tensor_tensor(ve[0:B, b.u, k:k + 1], var, keep.view("eps")[0:B, :], ALU.add).then_inc(plus_eps, 1)
                pool.wait_ge(plus_eps, done(b.s))
                pool.tensor_tensor(rs[0:B, b.u, k:k + 1], ve[0:B, b.u, k:k + 1], half[0:B, 0:1],
                                   ALU.pow).then_inc(power, 1)

            def norm_x(b):
                rsqrt(0, b, mv[0:B, b.u, 0, 1:2], d_mv, g_ve, g_rs)

            def add_row(b):
                pool.wait_ge(d_y, done(b.s))
                pool.tensor_tensor(X[0:B, b.s, :], X[0:B, b.s, :], orow[0:B, :], ALU.add).then_inc(g_row, 1)

            def norm_x1(b):
                rsqrt(1, b, mv[0:B, b.u, 1, 1:2], d_mv1, g_ve1, g_rs1)

            def norm_y1(b):
                rsqrt(2, b, v2[0:B, b.u:b.u + 1], d_v2, g_ve2, g_rs2)

            pipeline(pool, [(norm_x, 1), (norm_x1, -1), (norm_y1, -1), (add_row, 1)])

        @block.vector
        def _(dve):
            for x in dve_sems:
                dve.sem_inc(x, CREDIT)
            dve.wait_ge(ld_x, 16)
            dve.wait_ge(fold_out, 8)

            def stats_x(b):
                dve.bn_stats(st[0:B, b.u, 0, :], X[0:B, b.s, :]).then_inc(d_st, 1)
                dve.wait_ge(d_st, done(b.s))
                carry(dve, passed)
                dve.bn_aggr(mv[0:B, b.u, 0, :], st[0:B, b.u, 0, :]).then_inc(d_mv, 1)

            def norm_x(b):
                dve.wait_ge(g_rs, done(b.s))
                dve.tensor_scalar(y[0:B, b.u, :], X[0:B, b.s, :], mv[0:B, b.u, 0, 0:1], rs[0:B, b.u, 0:1],
                                  ALU.subtract, ALU.mult).then_inc(d_y, 1)

            def find(b, r):
                src = sc[0:B, b.u, :] if r == 0 else left[0:B, :]
                t = top[0:B, r % 2, :]
                if r == 0:
                    dve.wait_ge(a_sc, done(b.s))
                    t = best[0:B, b.u, :]
                carry(dve, passed)
                dve.max(t, src).then_inc(d_top, 1)
                dve.wait_ge(d_top, 4 * b.s + r + 1 + CREDIT)
                if r == 0:
                    dve.tensor_scalar(nmax[0:B, b.u:b.u + 1], best[0:B, b.u, 0:1], -1.0 / D ** 0.5, None,
                                      ALU.mult).then_inc(d_max, 1)
                carry(dve, passed)
                dve.match_replace(left[0:B, :], t, src, GONE).then_inc(d_left, 1)
                dve.wait_ge(d_left, 4 * b.s + r + 1 + CREDIT)

            def find_first(b):
                find(b, 0)
                find(b, 1)

            def find_rest(b):
                find(b, 2)
                find(b, 3)

            def select(b):
                dve.wait_ge(a_ex, done(b.s))
                dve.scalar_tensor_tensor(out=pr[0:B, b.u, :], in0=left[0:B, :], scalar=0.9 * GONE,
                                         in1=ex[0:B, b.u, :], op0=ALU.is_le, op1=ALU.mult,
                                         accum_out=psums[0:B, b.u:b.u + 1]).then_inc(d_pr, 1)
                dve.wait_ge(d_pr, done(b.s))
                dve.reciprocal(pinv[0:B, b.u:b.u + 1], psums[0:B, b.u:b.u + 1]).then_inc(d_inv, 1)

            def residual(b):
                dve.wait_ge(s_out, done(b.s))
                dve.wait_ge(g_row, done(b.s))
                dve.wait_ge(d_inv, done(b.s))
                dve.scalar_tensor_tensor(out=X[0:B, b.s, :], in0=ps_o[0:B, 0:D], scalar=pinv[0:B, b.u:b.u + 1],
                                         in1=X[0:B, b.s, :], op0=ALU.mult, op1=ALU.add).then_inc(d_x1, 1)
                dve.wait_ge(d_x1, done(b.s))
                carry(dve, passed)
                dve.bn_stats(st[0:B, b.u, 1, :], X[0:B, b.s, :]).then_inc(d_st1, 1)
                dve.wait_ge(d_st1, done(b.s))
                carry(dve, passed)
                dve.bn_aggr(mv[0:B, b.u, 1, :], st[0:B, b.u, 1, :]).then_inc(d_mv1, 1)

            def norm_x1(b):
                dve.wait_ge(g_rs1, done(b.s))
                dve.tensor_scalar(Y1[0:B, b.s, :], X[0:B, b.s, :], mv[0:B, b.u, 1, 0:1], rs[0:B, b.u, 1:2],
                                  ALU.subtract, ALU.mult).then_inc(d_y1, 1)
                dve.tensor_scalar(v2[0:B, b.u:b.u + 1], mv[0:B, b.u, 1, 1:2], rs[0:B, b.u, 1:2],
                                  rs[0:B, b.u, 1:2], ALU.mult, ALU.mult).then_inc(d_v2, 1)

            def norm_y1(b):
                dve.wait_ge(g_rs2, done(b.s))
                dve.wait_ge(d_y1, done(b.s))
                dve.tensor_scalar(z[0:B, b.u, :], Y1[0:B, b.s, :], rs[0:B, b.u, 2:3], None,
                                  ALU.mult).then_inc(d_z, 1)

            pipeline(dve, [(stats_x, 1), (find_first, 0), (norm_x, 1), (residual, -1), (find_rest, 0),
                           (norm_x1, -1), (select, 0), (norm_y1, -1)])

        @block.tensor
        def _(pe):
            for x in pe_sems:
                pe.sem_inc(x, CREDIT)
            pe.wait_ge(keep.ld_consts, 16)
            pe.wait_ge(ld_w, 16)
            pe.wait_ge(ld_rows, 16)
            pe.wait_ge(fold_in, 1)
            pe.wait_ge(g_const, 3)

            def fold(out, pairs):
                for k, (l, r) in enumerate(pairs):
                    mm = pe.matmul(out, l, r, start=(k == 0), stop=(k == len(pairs) - 1))
                return mm

            for c in range(DC):
                m = slice(c * P, (c + 1) * P)
                fold((ps_t, ps_q)[c][:, 0:D], [(wq[:, o, m], wk[:, o, :]) for o in range(DC)])
                fold(ps_s[c][:, 0:D], [(wv[:, o, m], woT[:, o, :]) for o in range(DC)])
                fold(ps_p[:, c:c + 1], [(wq[:, o, m], col("bk", o)) for o in range(DC)])
                fold(ps_p[:, DC + c:DC + c + 1], [(wk[:, o, m], col("bq", o)) for o in range(DC)])
            fold(ps_p[:, 4:5], [(bcast[:, 0, o, :], col("bk", o)) for o in range(DC)])
            fold(ps_o[:, 0:D], [(bcast[:, 1, o, :], woT[:, o, :]) for o in range(DC)]
                 + [(ones[0:1, :], rows_sb[0:1, :])]).then_inc(folded, 1)
            pe.wait_ge(fold_out, 8)
            pe.wait_ge(ld_qkv, 16)

            def query(b):
                pe.wait_ge(d_y, done(b.s))
                for c in range(DC):
                    mm = pe.transpose(ps_t[:, c * B:(c + 1) * B], y[0:B, b.u, c * P:(c + 1) * P],
                                      ident[0:B, 0:B])
                mm.then_inc(s_yT, 1)
                pe.wait_ge(a_yT, done(b.s))
                pe.wait_ge(a_q, done(b.s - 1))
                for c in range(DC):
                    for k in range(DC):
                        pe.matmul(ps_q[:, c * B:(c + 1) * B], A[:, k, c * P:(c + 1) * P], yT[:, b.u, k, :],
                                  start=(k == 0), stop=(k == DC - 1))
                for k in range(DC):
                    mm = pe.matmul(ps_q[0:B, 2 * B:2 * B + 1], yT[:, b.u, k, :], wqbk[:, k:k + 1],
                                   start=(k == 0), stop=(k == DC - 1))
                mm.then_inc(s_q, 1)
                pe.wait_ge(a_q, done(b.s))
                pe.wait_ge(ld_ct[b.u], b.loaded)
                for k in range(DC):
                    mm = pe.matmul(ps_s[b.u][0:B, 0:CTX], qT[:, b.u, k, :], ctxT[:, b.u, k, :],
                                   start=(k == 0), stop=(k == DC - 1))
                mm.then_inc(s_sc, 1)

            def attend(b):
                pe.wait_ge(d_pr, done(b.s))
                for k in range(3):
                    mm = pe.transpose(ps_p[0:CK[k], k * B:(k + 1) * B], pr[0:B, b.u, k * P:k * P + CK[k]],
                                      ident[0:B, 0:B])
                mm.then_inc(s_prT, 1)
                pe.wait_ge(a_prT, done(b.s))
                pe.wait_ge(ld_cn[b.u], 2 * b.loaded)
                for c in range(DC):
                    for k in range(3):
                        mm = pe.matmul(ps_av[:, c * B:(c + 1) * B], ctxN[0:CK[k], b.u, k, c * P:(c + 1) * P],
                                       prT[0:CK[k], b.u, k, :], start=(k == 0), stop=(k == 2))
                mm.then_inc(s_av, 1)
                pe.wait_ge(a_av, done(b.s))
                pe.wait_ge(d_x1, done(b.s - 1))
                for k in range(DC):
                    mm = pe.matmul(ps_o[0:B, 0:D], avT[:, b.u, k, :], Wov[:, k, :],
                                   start=(k == 0), stop=(k == DC - 1))
                mm.then_inc(s_out, 1)

            def project(b):
                pe.wait_ge(d_z, done(b.s))
                for c in range(DC):
                    mm = pe.transpose(ps_t[:, 200 + c * B:200 + (c + 1) * B], z[0:B, b.u, c * P:(c + 1) * P],
                                      ident[0:B, 0:B])
                mm.then_inc(s_zT, 1)
                pe.wait_ge(a_zT, done(b.s))
                pe.wait_ge(a_qkv, done(b.s - 1))
                for m in range(3):
                    for k in range(DC):
                        pe.matmul(ps_qkv[:, m * B:(m + 1) * B], wqkvT[:, k, m * P:(m + 1) * P], zT[:, b.u, k, :],
                                  start=(k == 0), stop=(k == DC - 1))
                for k in range(DC):
                    mm = pe.matmul(ps_qkv[0:B, 3 * B:3 * B + P], zT[:, b.u, k, :], wqkvT[:, k, 3 * P:4 * P],
                                   start=(k == 0), stop=(k == DC - 1))
                mm.then_inc(s_qkv, 1)

            pipeline(pe, [(attend, -1), (query, 1), (project, -1)])


GROUPS = B // 4


def self_attention(nc, io, keep):
    with ExitStack() as ctx:
        sb = lambda name, shape, dt=F32: ctx.enter_context(nc.sbuf_tensor(name, shape, dt))
        own = ctx.enter_context(semaphores(nc))
        sem = lambda name: own(name)
        both = lambda name: [ctx.enter_context(nc.psum_tensor(f"{name}{k}", [P, 512], F32)) for k in range(2)]

        Qs = sb("Qs", [P, 2, P])
        Ks = sb("Ks", [P, 2, 4, G, T])
        Vs = sb("Vs", [P, 2, 4, P])
        sm = sb("sm", [P, 2, P])
        top = sb("top_b", [P, 2, G])
        ex = sb("ex_b", [P, 2, P])
        den = sb("den", [P, 2, G])
        rden = sb("rden", [P, 2, G])
        exT = sb("exT", [P, 2, P])
        o = sb("o", [P, 2, P])
        ps_s, ps_t, ps_o, ps_u = both("psb_s"), both("psb_t"), both("psb_o"), both("psb_u")

        vx = sem("vx_loaded")
        g_k = sem("b_keys")
        s_sc, s_exT, s_o, s_oT = pe_sems = [sem(n) for n in ("b_sc", "b_exT_ps", "b_o", "b_oT_ps")]
        a_q, a_ex, a_exT, a_oT = act_sems = [sem(n) for n in ("b_q", "b_ex", "b_exT", "b_oT")]
        d_m, d_top, d_sub, d_sum, d_den, d_v, d_o = dve_sems = [
            sem(n) for n in ("b_m", "b_top", "b_sub", "b_sum", "b_den", "b_v", "b_o_sb")]
        Q, K, VX, AT = keep.Q, keep.K, keep.VX, keep.AT
        block = ctx.enter_context(nc.Block())

        @block.sync
        def _(sp):
            sp.wait_ge(keep.vx_zero, 4)
            for g in range(G):
                with nc.allow_non_contiguous_dma(reason="a head's 16 values"):
                    sp.dma_start(VX[g * T:(g + 1) * T, :, g * HD:(g + 1) * HD],
                                 keep.values[:, :, g * HD:(g + 1) * HD]).then_inc(vx, 16)
            sp.wait_ge(keep.zeroed, 32)

        @block.scalar
        def _(act):
            for x in act_sems:
                act.sem_inc(x, CREDIT)

            def queries(b):
                act.wait_ge(s_sc, reuse(b.s))
                act.copy(Qs[:, b.u, :], Q[:, bass.ds(4 * b.s, 4), :, :]).then_inc(a_q, 1)

            def exponent(b):
                act.wait_ge(d_sub, done(b.s))
                act.wait_ge(s_exT, reuse(b.s))
                act.wait_ge(d_sum, reuse(b.s))
                act.activation(ex[:, b.u, :], sm[:, b.u, :], ACT.Exp).then_inc(a_ex, 1)

            def turn(b):
                act.wait_ge(s_exT, done(b.s))
                act.wait_ge(s_o, reuse(b.s))
                act.copy(exT[:, b.u, :], ps_t[b.u][:, 0:P]).then_inc(a_exT, 1)

            def out(b):
                act.wait_ge(s_oT, done(b.s))
                act.copy(AT[:, :, :, bass.ds(4 * b.s, 4)].rearrange("p j s b -> p b j s"),
                         ps_u[b.u][:, 0:P].rearrange("p (b j s) -> p b j s", b=4, j=QJ)).then_inc(a_oT, 1)

            pipeline(act, [(queries, 2), (exponent, 1), (turn, 0), (out, -2)], GROUPS)

        @block.gpsimd
        def _(pool):
            pool.sem_inc(g_k, CREDIT)

            def keys(b):
                pool.wait_ge(s_sc, reuse(b.s))
                pool.tensor_tensor(Ks[:, b.u, :, :, :],
                                   K[:, bass.ds(4 * b.s, 4), :].unsqueeze(2).to_broadcast([P, 4, G, T]),
                                   keep.kmask.unsqueeze(1).unsqueeze(3).to_broadcast([P, 4, G, T]),
                                   ALU.mult).then_inc(g_k, 1)

            pipeline(pool, [(keys, 2)], GROUPS)

        @block.vector
        def _(dve):
            for x in dve_sems:
                dve.sem_inc(x, CREDIT)

            by_group = lambda ap: ap.rearrange("p (g t) -> p g t", g=G)

            def softmax(b):
                dve.wait_ge(s_sc, done(b.s))
                dve.wait_ge(a_ex, reuse(b.s))
                dve.scalar_tensor_tensor(out=sm[:, b.u, :], in0=ps_s[b.u][:, 0:P], scalar=1.0 / HD ** 0.5,
                                         in1=keep.view("causal"), op0=ALU.mult, op1=ALU.add).then_inc(d_m, 1)
                dve.wait_ge(d_m, done(b.s))
                dve.tensor_reduce(top[:, b.u, :], by_group(sm[:, b.u, :]), AX.X, ALU.max).then_inc(d_top, 1)
                dve.wait_ge(d_top, done(b.s))
                dve.tensor_tensor(by_group(sm[:, b.u, :]), by_group(sm[:, b.u, :]),
                                  top[:, b.u, :].unsqueeze(2).to_broadcast([P, G, T]),
                                  ALU.subtract).then_inc(d_sub, 1)

            waited = []

            def values(b):
                if not waited:
                    waited.append(dve.wait_ge(vx, 16 * G))
                dve.wait_ge(s_o, reuse(b.s))
                dve.tensor_copy(Vs[:, b.u, :, :], VX[:, bass.ds(4 * b.s, 4), :]).then_inc(d_v, 1)

            def sums(b):
                dve.wait_ge(a_ex, done(b.s))
                dve.tensor_reduce(den[:, b.u, :], by_group(ex[:, b.u, :]), AX.X, ALU.add).then_inc(d_sum, 1)
                dve.wait_ge(d_sum, done(b.s))
                dve.reciprocal(rden[:, b.u, :], den[:, b.u, :]).then_inc(d_den, 1)

            def divide(b):
                dve.wait_ge(s_o, done(b.s))
                dve.wait_ge(d_den, done(b.s))
                dve.wait_ge(s_oT, reuse(b.s))
                dve.tensor_tensor(by_group(o[:, b.u, :]), by_group(ps_o[b.u][:, 0:P]),
                                  rden[:, b.u, :].unsqueeze(2).to_broadcast([P, G, HD]),
                                  ALU.mult).then_inc(d_o, 1)

            pipeline(dve, [(softmax, 1), (values, 0), (sums, 0), (divide, -1)], GROUPS)

        @block.tensor
        def _(pe):
            for x in pe_sems:
                pe.sem_inc(x, CREDIT)

            def scores(b):
                pe.wait_ge(a_q, done(b.s))
                pe.wait_ge(g_k, done(b.s))
                pe.wait_ge(d_m, reuse(b.s))
                for r in range(4):
                    mm = pe.matmul(ps_s[b.u][32 * r:32 * r + 32, 0:P], Qs[:, b.u, 32 * r:32 * r + 32],
                                   Ks[:, b.u, r, :, :], start=True, stop=True)
                mm.then_inc(s_sc, 1)

            def turn(b):
                pe.wait_ge(a_ex, done(b.s))
                pe.wait_ge(a_exT, reuse(b.s))
                pe.transpose(ps_t[b.u][:, 0:P], ex[:, b.u, :], keep.ident).then_inc(s_exT, 1)

            def attend(b):
                pe.wait_ge(a_exT, done(b.s))
                pe.wait_ge(d_v, done(b.s))
                pe.wait_ge(d_o, reuse(b.s))
                for r in range(4):
                    mm = pe.matmul(ps_o[b.u][32 * r:32 * r + 32, 0:P], exT[:, b.u, 32 * r:32 * r + 32],
                                   Vs[:, b.u, r, :], start=True, stop=True)
                mm.then_inc(s_o, 1)

            def turn_out(b):
                pe.wait_ge(d_o, done(b.s))
                pe.wait_ge(a_oT, reuse(b.s))
                pe.transpose(ps_u[b.u][:, 0:P], o[:, b.u, :], keep.ident).then_inc(s_oT, 1)

            pipeline(pe, [(scores, 1), (turn, 0), (attend, -1), (turn_out, -2)], GROUPS)


def project_and_score(nc, io, keep):
    with ExitStack() as ctx:
        sb = lambda name, shape, dt=F32: ctx.enter_context(nc.sbuf_tensor(name, shape, dt))
        own = ctx.enter_context(semaphores(nc))
        sem = lambda name: own(name)
        both = lambda name: [ctx.enter_context(nc.psum_tensor(f"{name}{k}", [P, 512], F32)) for k in range(2)]
        X, Y1, Z, AT, half = keep.X, keep.Y1, keep.Z, keep.AT, keep.half
        projT = sb("projT", [P, QJ, D])
        at = sb("at", [P, 2, QJ, B])
        h = sb("h", [P, 2, D])
        st = sb("st_c", [P, 2, 6])
        mv = sb("mv_c", [P, 2, 2])
        ve = sb("ve_c", [P, 2])
        rs = sb("rs_c", [P, 2])
        z = sb("z_c", [P, 2, D])
        zT = sb("zT_c", [P, 2, DC, B])
        ps_h, ps_t, ps_l = both("psc_h"), both("psc_t"), both("psc_l")
        ld = sem("ld_proj")
        s_h, s_zT, s_l = pe_sems = [sem(n) for n in ("c_h", "c_zT", "c_l")]
        a_at, a_zT = act_sems = [sem(n) for n in ("c_at", "c_zTs")]
        d_h, d_st, d_mv, d_z, d_l = dve_sems = [
            sem(n) for n in ("c_hs", "c_st", "c_mv", "c_z", "c_logits")]
        g_x, g_ve, g_rs, g_z = pool_sems = [sem(n) for n in ("c_x", "c_ve", "c_rs", "c_zcopy")]
        passed = sem("passed_c")
        router = keep.view("router").rearrange("p (c e) -> p c e", c=DC)
        block = ctx.enter_context(nc.Block())

        @block.sync
        def _(sp):
            sp.dma_start(projT[:, :, :], io.w_projT).then_inc(ld, 16)

        @block.scalar
        def _(act):
            for x in act_sems:
                act.sem_inc(x, CREDIT)

            def take(b):
                act.wait_ge(s_h, reuse(b.s))
                act.copy(at[:, b.u, :, :], AT[:, :, b.s, :]).then_inc(a_at, 1)

            def turned(b):
                act.wait_ge(s_zT, done(b.s))
                act.wait_ge(s_l, reuse(b.s))
                for c in range(DC):
                    last = act.activation(zT[:, b.u, c, :], ps_t[b.u][:, c * B:(c + 1) * B], ACT.Identity,
                                          bias=keep.col("ln2b", c), scale=keep.col("ln2w", c))
                last.then_inc(a_zT, 1)

            pipeline(act, [(take, 2), (turned, 0)])

        @block.gpsimd
        def _(pool):
            for x in pool_sems:
                pool.sem_inc(x, CREDIT)

            def norm(b):
                pool.wait_ge(d_mv, done(b.s))
                pool.wait_ge(d_z, reuse(b.s))
                pool.tensor_tensor(ve[0:B, b.u:b.u + 1], mv[0:B, b.u, 1:2], keep.view("eps")[0:B, :],
                                   ALU.add).then_inc(g_ve, 1)
                pool.wait_ge(g_ve, done(b.s))
                pool.tensor_tensor(rs[0:B, b.u:b.u + 1], ve[0:B, b.u:b.u + 1], half[0:B, 0:1],
                                   ALU.pow).then_inc(g_rs, 1)

            def add(b):
                pool.wait_ge(d_h, done(b.s))
                pool.tensor_tensor(X[0:B, b.s, :], X[0:B, b.s, :], h[0:B, b.u, :], ALU.add).then_inc(g_x, 1)

            def store(b):
                pool.wait_ge(d_z, done(b.s))
                pool.tensor_copy(Z[0:B, b.s, :], z[0:B, b.u, :]).then_inc(g_z, 1)

            pipeline(pool, [(norm, 1), (add, 1), (store, 0)])

        @block.vector
        def _(dve):
            for x in dve_sems:
                dve.sem_inc(x, CREDIT)

            def hidden(b):
                dve.wait_ge(s_h, done(b.s))
                dve.wait_ge(g_x, reuse(b.s))
                dve.tensor_tensor(h[0:B, b.u, :], ps_h[b.u][0:B, 0:D], Y1[0:B, b.s, :], ALU.add).then_inc(d_h, 1)
                dve.wait_ge(d_h, done(b.s))
                carry(dve, passed)
                dve.bn_stats(st[0:B, b.u, :], h[0:B, b.u, :]).then_inc(d_st, 1)
                dve.wait_ge(d_st, done(b.s))
                dve.wait_ge(g_ve, reuse(b.s))
                carry(dve, passed)
                dve.bn_aggr(mv[0:B, b.u, :], st[0:B, b.u, :]).then_inc(d_mv, 1)

            def norm(b):
                dve.wait_ge(g_rs, done(b.s))
                dve.wait_ge(g_z, reuse(b.s))
                dve.wait_ge(s_zT, reuse(b.s))
                dve.tensor_scalar(z[0:B, b.u, :], h[0:B, b.u, :], mv[0:B, b.u, 0:1], rs[0:B, b.u:b.u + 1],
                                  ALU.subtract, ALU.mult).then_inc(d_z, 1)

            def take_logits(b):
                dve.wait_ge(s_l, done(b.s))
                dve.tensor_copy(keep.LG[0:B, b.s, :], ps_l[b.u][0:B, 0:E0]).then_inc(d_l, 1)

            pipeline(dve, [(hidden, 1), (norm, 0), (take_logits, -1)])

        @block.tensor
        def _(pe):
            for x in pe_sems:
                pe.sem_inc(x, CREDIT)
            pe.wait_ge(ld, 16)

            def project(b):
                pe.wait_ge(a_at, done(b.s))
                pe.wait_ge(d_h, reuse(b.s))
                for j in range(QJ):
                    mm = pe.matmul(ps_h[b.u][0:B, 0:D], at[:, b.u, j, :], projT[:, j, :],
                                   start=(j == 0), stop=(j == QJ - 1))
                mm.then_inc(s_h, 1)

            def turn(b):
                pe.wait_ge(d_z, done(b.s))
                pe.wait_ge(a_zT, reuse(b.s))
                for c in range(DC):
                    mm = pe.transpose(ps_t[b.u][:, c * B:(c + 1) * B], z[0:B, b.u, c * P:(c + 1) * P],
                                      keep.ident[0:B, 0:B])
                mm.then_inc(s_zT, 1)

            def logits(b):
                pe.wait_ge(a_zT, done(b.s))
                pe.wait_ge(d_l, reuse(b.s))
                for c in range(DC):
                    mm = pe.matmul(ps_l[b.u][0:B, 0:E0], zT[:, b.u, c, :], router[:, c, :],
                                   start=(c == 0), stop=(c == DC - 1))
                mm.then_inc(s_l, 1)

            pipeline(pe, [(project, 1), (turn, 0), (logits, -1)])


def route(nc, io, keep, second):
    name = "r1" if second else "r0"
    with ExitStack() as ctx:
        sb = lambda n, shape, dt=F32: ctx.enter_context(nc.sbuf_tensor(f"{name}_{n}", shape, dt))
        own = ctx.enter_context(semaphores(nc))
        sem = lambda n: own(f"{name}_{n}")
        E = G
        diff, ex, den, rden = sb("diff", [P, S, E]), sb("ex", [P, S, E]), sb("den", [P, S]), sb("rden", [P, S])
        idx = sb("idx", [P, 2, S])
        hot = sb("hot", [P, 2, S, E])
        taken = sb("taken", [P, S, E])
        run = [sb("run0", [P, S, E]), sb("run1", [P, S, E])]
        tot = sb("tot", [P, S, E])
        rank = sb("rank", [P, S, E])
        mine = sb("mine", [P, 2, S, E])
        slot = sb("slot", [P, 2, S])
        kept = sb("kept", [P, 2, S])
        gone = sb("gone", [P, 2, S])
        full = sb("full", [P, E, 5])
        tiles = sb("tiles", [P, E])
        upto = [sb("upto0", [P, E]), sb("upto1", [P, E])]
        base = sb("base", [P, E])
        below = sb("below", [P, TILES1, E])
        te = sb("te", [P, TILES1])
        ones = sb("ones", [P, P])
        ps = ctx.enter_context(nc.psum_tensor(f"{name}_ps", [P, 512], F32))
        d_step, a_ex, s_counts, g_ones = sem("step"), sem("ex"), sem("counts"), sem("ones")
        LG, V8, I8, W2, scat, gath = keep.LG, keep.V8, keep.I8, keep.W2, keep.scat, keep.gath
        by8 = lambda ap, n: ap.unsqueeze(len(ap.shape)).to_broadcast(n)
        block = ctx.enter_context(nc.Block())
        steps = {}

        @block.gpsimd
        def _(pool):
            pool.memset(ones[:, :], 1.0).then_inc(g_ones, 1)

        @block.vector
        def _(dve):
            count = [0]

            def link(ins, label=None):
                count[0] += 1
                ins.then_inc(d_step, 1)
                dve.wait_ge(d_step, count[0])
                if label:
                    steps[label] = count[0]

            A = slice(0, B)
            for s in range(S):
                top = dve.max(keep.V8[A, s, :], keep.LG[A, s, :])
            link(top)
            for s in range(S):
                whose = dve.max_index(keep.I8[A, s, :], keep.V8[A, s, :], keep.LG[A, s, :])
            link(whose)
            link(dve.tensor_tensor(diff[A], V8[A, :, :], by8(V8[A, :, 0], [B, S, E]), ALU.subtract), "diff")
            link(dve.tensor_copy(idx[A], I8[A, :, 0:2].rearrange("p s j -> p j s")))
            for j in range(2):
                link(dve.tensor_tensor(hot[A, j], by8(idx[A, j, :], [B, S, E]),
                                       keep.view("iota8")[A].unsqueeze(1).to_broadcast([B, S, E]), ALU.is_equal))
            link(dve.tensor_tensor(taken[A], hot[A, 0], hot[A, 1], ALU.add), "taken")
            dve.wait_ge(a_ex, 1)
            link(dve.tensor_reduce(den[A], ex[A] if second else ex[A, :, 0:2], AX.X, ALU.add))
            link(dve.reciprocal(rden[A], den[A]))
            link(dve.tensor_tensor(W2[A], ex[A, :, 0:2].rearrange("p s j -> p j s"),
                                   rden[A].unsqueeze(1).to_broadcast([B, 2, S]), ALU.mult))
            dve.wait_ge(s_counts, 1)
            link(dve.tensor_copy(tot[A], ps[A, P:2 * P]))
            link(dve.tensor_copy(run[0][A], tot[A]))
            at, step = 0, 1
            while step < S:
                link(dve.tensor_copy(run[1 - at][A, 0:step, :], run[at][A, 0:step, :]))
                link(dve.tensor_tensor(run[1 - at][A, step:S, :], run[at][A, step:S, :],
                                       run[at][A, 0:S - step, :], ALU.add))
                at, step = 1 - at, 2 * step
            link(dve.tensor_tensor(rank[A], run[at][A], tot[A], ALU.subtract))
            link(dve.tensor_tensor(rank[A], rank[A], ps[A, 0:P].rearrange("p (s e) -> p s e", e=E), ALU.add))
            if second:
                link(dve.tensor_tensor(full[A], by8(run[at][A, S - 1, :], [B, E, 5]),
                                       keep.view("thresholds")[A].unsqueeze(1).to_broadcast([B, E, 5]), ALU.is_gt))
                link(dve.tensor_reduce(tiles[A], full[A], AX.X, ALU.add))
                link(dve.tensor_copy(upto[0][A], tiles[A]))
                au, step = 0, 1
                while step < E:
                    link(dve.tensor_copy(upto[1 - au][A, 0:step], upto[au][A, 0:step]))
                    link(dve.tensor_tensor(upto[1 - au][A, step:E], upto[au][A, step:E],
                                           upto[au][A, 0:E - step], ALU.add))
                    au, step = 1 - au, 2 * step
                link(dve.tensor_tensor(base[A], upto[au][A], tiles[A], ALU.subtract))
                link(dve.tensor_scalar(base[A], base[A], float(TILE1), None, ALU.mult))
                link(dve.tensor_tensor(rank[A], rank[A], base[A].unsqueeze(1).to_broadcast([B, S, E]), ALU.add))
                link(dve.tensor_tensor(below[A], upto[au][A].unsqueeze(1).to_broadcast([B, TILES1, E]),
                                       by8(keep.view("fills")[A, 0:TILES1], [B, TILES1, E]), ALU.is_le))
                link(dve.tensor_reduce(te[A], below[A], AX.X, ALU.add))
                link(dve.tensor_scalar(keep.tile_expert[A], te[A], float(E1 - 1), None, ALU.min))
            for j in range(2):
                link(dve.tensor_tensor(mine[A, j], hot[A, j], rank[A], ALU.mult))
                link(dve.tensor_reduce(slot[A, j], mine[A, j], AX.X, ALU.add))
            if second:
                link(dve.tensor_copy(scat[A], slot[A]))
                link(dve.tensor_copy(gath[A], slot[A]))
            else:
                link(dve.tensor_scalar(kept[A], slot[A], float(CAP), None, ALU.is_lt))
                link(dve.tensor_scalar(gone[A], kept[A], -1.0e5, 1.0e5, ALU.mult, ALU.add))
                link(dve.scalar_tensor_tensor(out=slot[A], in0=idx[A], scalar=float(CAP), in1=slot[A],
                                              op0=ALU.mult, op1=ALU.add))
                link(dve.tensor_tensor(scat[A], slot[A], gone[A], ALU.add))
                link(dve.tensor_tensor(gath[A], slot[A], kept[A], ALU.mult))
                link(dve.tensor_tensor(W2[A], W2[A], kept[A], ALU.mult))

        @block.scalar
        def _(act):
            act.wait_ge(d_step, steps["diff"])
            act.activation(ex[0:B], diff[0:B], ACT.Exp).then_inc(a_ex, 1)

        @block.tensor
        def _(pe):
            pe.wait_ge(g_ones, 1)
            pe.wait_ge(d_step, steps["taken"])
            flat = taken[0:B].rearrange("p s e -> p (s e)")
            pe.matmul(ps[0:B, 0:P], keep.view("before")[0:B, 0:B], flat, start=True, stop=True)
            pe.matmul(ps[0:B, P:2 * P], ones[0:B, 0:B], flat, start=True, stop=True).then_inc(s_counts, 1)


def expert_tiles(nc, io, keep, second):
    name = "f1" if second else "f0"
    with ExitStack() as ctx:
        sb = lambda n, shape, dt=F32: ctx.enter_context(nc.sbuf_tensor(f"{name}_{n}", shape, dt))
        own = ctx.enter_context(semaphores(nc))
        sem = lambda n: own(f"{name}_{n}")
        psum = lambda n, w=512: ctx.enter_context(nc.psum_tensor(f"{name}_{n}", [P, w], F32))
        R, SUB, TILES = (ROWS1, SUB1, TILES1) if second else (ROWS0, SUB0, E0)
        N = R * SUB
        slots, outs = (keep.slots1, keep.outs1) if second else (keep.slots0, keep.outs0)
        weights = io.w_f1 if second else io.w_f0
        W1 = DC * FFN
        WALL = W1 + FC * D
        PIECE = WALL // FC
        RING = 4

        raw = sb("raw", [P, 2, WALL])
        w_hi, w_lo = sb("w_hi", [P, 2, WALL], F32R), sb("w_lo", [P, 2, WALL], F32R)
        xs = sb("xs", [P, 2, SUB, D])
        xT = sb("xT", [P, DC, N])
        x_hi, x_lo = sb("x_hi", [P, 2, DC, N], F32R), sb("x_lo", [P, 2, DC, N], F32R)
        g = sb("g", [P, 2, N])
        h_hi, h_lo = sb("h_hi", [P, RING, N], F32R), sb("h_lo", [P, RING, N], F32R)
        ys = sb("ys", [P, 2, SUB, D])
        b1, b2 = sb("b1", [P, 2, FC]), sb("b2", [P, 2, D])
        ps_x = psum("ps_x", 1024)
        ps_h = [psum("ps_h0"), psum("ps_h1")]
        ps_y = [psum("ps_y0", 1024), psum("ps_y1", 1024)]

        scattered, passed = sem("scattered"), sem("passed")
        ld_w, ld_x, st_y = ([sem(f"{n}{k}") for k in range(2)] for n in ("ld_w", "ld_x", "st_y"))
        s_xT, s_h, s_y = pe_sems = [sem(n) for n in ("xT_ps", "h_ps", "y_ps")]
        a_xT, a_g, a_w = act_sems = [sem(n) for n in ("xT", "gelu", "w_hi_r")]
        d_xh, d_x, d_hh, d_h, d_y = dve_sems = [sem(n) for n in ("x_hi_r", "x_r", "h_hi_r", "h_r", "ys_r")]
        g_w = sem("w_lo_r")
        block = ctx.enter_context(nc.Block())

        def upto(b, f):
            return FC * b.s + f + 1 + 2 * FC

        TWO_BEFORE = -FC - 1
        per_load = 3 if second else 1

        @block.sync
        def _(sp):
            for x in st_y:
                sp.sem_inc(x, 16)

            def load_w(b):
                sp.wait_ge(g_w, upto(b, TWO_BEFORE))
                e = b.s
                if second:
                    sp.wait_ge(a_g, upto(b, TWO_BEFORE))
                    carry(sp, passed)
                    sp.wait_ge(d_y, reuse(b.s))
                    at = bass.ds(b.s, 1) if b.looped else slice(b.s, b.s + 1)
                    carry(sp, passed)
                    e = sp.value_load(keep.tile_expert[0:1, at], min_val=0, max_val=E1 - 1)
                    sp.dma_start(b1[:, b.u, :], io.be1[e]).then_inc(ld_w[b.u], 16)
                    sp.dma_start(b2[:, b.u, :], io.be2[e].to_broadcast([P, D])).then_inc(ld_w[b.u], 16)
                sp.dma_start(raw[:, b.u, :], weights[e]).then_inc(ld_w[b.u], 16)

            def load_x(b):
                sp.wait_ge(scattered, 16 * 2 * S)
                sp.wait_ge(s_xT, reuse(b.s))
                sp.dma_start(xs[0:R, b.u, :, :],
                             slots.rearrange("(t m r) d -> t r m d", m=SUB, r=R)[b.s]).then_inc(ld_x[b.u], 16)

            def store(b):
                sp.wait_ge(d_y, done(b.s))
                sp.dma_start(outs.rearrange("(t m r) d -> t r m d", m=SUB, r=R)[b.s],
                             ys[0:R, b.u, :, :]).then_inc(st_y[b.u], 16)

            pipeline(sp, [(load_w, 2), (load_x, 2), (store, 0)], TILES)
            for x in st_y:
                sp.wait_ge(x, 16 * (TILES // 2) + 16)

        @block.gpsimd
        def _(pool):
            pool.sem_inc(g_w, 2 * FC)
            for j in range(2):
                for s in range(S):
                    pool.indirect_dma_start(
                        slots, bass.IndirectOffsetOnAxis(ap=keep.scat[0:B, j, s:s + 1], axis=0),
                        keep.Z[0:B, s, :], None, bounds_check=slots.shape[0] - 1,
                        oob_is_err=False).then_inc(scattered, 16)

            def low(b):
                pool.wait_ge(ld_w[b.u], per_load * b.loaded)
                pool.wait_ge(s_y, upto(b, TWO_BEFORE))
                for k in range(FC):
                    c = slice(k * PIECE, (k + 1) * PIECE)
                    pool.wait_ge(a_w, upto(b, k))
                    pool.tensor_tensor(w_lo[:, b.u, c], raw[:, b.u, c], w_hi[:, b.u, c].bitcast(F32),
                                       ALU.subtract).then_inc(g_w, 1)

            pipeline(pool, [(low, 0)], TILES)

        @block.scalar
        def _(act):
            act.sem_inc(a_xT, CREDIT)
            act.sem_inc(a_g, 2 * FC)
            act.sem_inc(a_w, 2 * FC)

            def high(k):
                def stage(b):
                    if k == 0:
                        act.wait_ge(ld_w[b.u], per_load * b.loaded)
                        act.wait_ge(s_y, upto(b, TWO_BEFORE))
                        act.wait_ge(g_w, upto(b, TWO_BEFORE))
                    c = slice(k * PIECE, (k + 1) * PIECE)
                    act.copy(w_hi[:, b.u, c], raw[:, b.u, c]).then_inc(a_w, 1)
                return stage

            def turned(b):
                act.wait_ge(s_xT, done(b.s))
                act.wait_ge(d_x, done(b.s - 1))
                for c in range(DC):
                    src = ps_x[:, 512 * c:512 * c + N]
                    if second:
                        last = act.copy(xT[:, c, :], src)
                    else:
                        last = act.activation(xT[:, c, :], src, ACT.Identity, bias=keep.col("ln2b", c),
                                              scale=keep.col("ln2w", c))
                last.then_inc(a_xT, 1)

            def gelu(f):
                def stage(b):
                    act.wait_ge(s_h, upto(b, f))
                    act.wait_ge(d_h, upto(b, f - 2))
                    act.activation(g[:, f % 2, :], ps_h[f % 2][:, 0:N], ACT.Gelu,
                                   bias=b1[:, b.u, f:f + 1] if second else 0.0).then_inc(a_g, 1)
                return stage

            stages = []
            for f, ks in enumerate([[], [], [0], [1], [2, 3], [4], [5], [6, 7]]):
                stages += [(gelu(f), 0)] + [(high(k), 1) for k in ks] + ([(turned, 1)] if f == 5 else [])
            pipeline(act, stages, TILES)

        @block.vector
        def _(dve):
            for x in (d_xh, d_x, d_y):
                dve.sem_inc(x, CREDIT)
            dve.sem_inc(d_hh, 2 * FC)
            dve.sem_inc(d_h, 2 * FC)

            def split_x(b):
                dve.wait_ge(a_xT, done(b.s))
                dve.wait_ge(s_h, upto(b, TWO_BEFORE))
                dve.tensor_copy(x_hi[:, b.u, :, :], xT[:, :, :]).then_inc(d_xh, 1)
                dve.wait_ge(d_xh, done(b.s))
                dve.tensor_tensor(x_lo[:, b.u, :, :], xT[:, :, :], x_hi[:, b.u, :, :].bitcast(F32),
                                  ALU.subtract).then_inc(d_x, 1)

            def split_h(f):
                def stage(b):
                    dve.wait_ge(a_g, upto(b, f))
                    dve.wait_ge(s_y, upto(b, f - RING))
                    dve.tensor_copy(h_hi[:, f % RING, :], g[:, f % 2, :]).then_inc(d_hh, 1)
                    dve.wait_ge(d_hh, upto(b, f))
                    dve.tensor_tensor(h_lo[:, f % RING, :], g[:, f % 2, :], h_hi[:, f % RING, :].bitcast(F32),
                                      ALU.subtract).then_inc(d_h, 1)
                return stage

            def out(b):
                dve.wait_ge(s_y, upto(b, FC - 1))
                dve.wait_ge(st_y[b.u], b.loaded)
                src = ps_y[b.u][0:R, 0:SUB * D].rearrange("p (m d) -> p m d", d=D)
                if second:
                    dve.wait_ge(ld_w[b.u], per_load * b.loaded)
                    dve.tensor_tensor(ys[0:R, b.u, :, :], src, b2[0:R, b.u, :].unsqueeze(1).to_broadcast([R, SUB, D]),
                                      ALU.add).then_inc(d_y, 1)
                else:
                    dve.tensor_copy(ys[0:R, b.u, :, :], src).then_inc(d_y, 1)

            stages = []
            for f in range(FC):
                stages += [(split_h(f), 0)] + ([(out, -1)] if f == 2 else []) + ([(split_x, 1)] if f == 5 else [])
            pipeline(dve, stages, TILES)

        @block.tensor
        def _(pe):
            pe.sem_inc(s_xT, CREDIT)
            pe.sem_inc(s_h, 2 * FC)
            pe.sem_inc(s_y, 2 * FC)

            def turn(b):
                pe.wait_ge(ld_x[b.u], b.loaded)
                pe.wait_ge(a_xT, done(b.s - 1))
                for m in range(SUB):
                    for c in range(DC):
                        at = 512 * c + m * R
                        mm = pe.transpose(ps_x[:, at:at + R], xs[0:R, b.u, m, c * P:(c + 1) * P],
                                          keep.ident[0:R, 0:R])
                mm.then_inc(s_xT, 1)

            def passes(hi_lo_left, hi_lo_right):
                (lh, ll), (rh, rl) = hi_lo_left, hi_lo_right
                return [(lh, rh), (lh, rl), (ll, rh)]

            def hidden(f):
                def stage(b):
                    if f == 0:
                        pe.wait_ge(d_x, done(b.s))
                        pe.wait_ge(g_w, upto(b, FC - 1))
                    pe.wait_ge(a_g, upto(b, f - 2))
                    todo = []
                    for c in range(DC):
                        w = slice(c * FFN + f * P, c * FFN + (f + 1) * P)
                        todo += passes((w_hi[:, b.u, w], w_lo[:, b.u, w]), (x_hi[:, b.u, c, :], x_lo[:, b.u, c, :]))
                    for k, (l, r) in enumerate(todo):
                        mm = pe.matmul(ps_h[f % 2][:, 0:N], l, r, start=(k == 0), stop=(k == len(todo) - 1))
                    mm.then_inc(s_h, 1)
                return stage

            def output(f):
                def stage(b):
                    if f == 0:
                        pe.wait_ge(d_y, reuse(b.s))
                    pe.wait_ge(d_h, upto(b, f))
                    w = slice(W1 + f * D, W1 + (f + 1) * D)
                    for m in range(SUB):
                        t = slice(m * R, (m + 1) * R)
                        todo = passes((h_hi[:, f % RING, t], h_lo[:, f % RING, t]),
                                      (w_hi[:, b.u, w], w_lo[:, b.u, w]))
                        for k, (l, r) in enumerate(todo):
                            mm = pe.matmul(ps_y[b.u][0:R, m * D:(m + 1) * D], l, r,
                                           start=(f == 0 and k == 0 and m % 2 == 0),
                                           stop=(f == FC - 1 and k == 2), skip_group_check=True)
                    mm.then_inc(s_y, 1)
                return stage

            LAG = 2
            stages = []
            for f in range(FC):
                back = f - LAG
                stages += [(hidden(f), 0), (output(back % FC), 0 if back >= 0 else -1)]
                if f == 4:
                    stages += [(turn, 1)]
            pipeline(pe, stages, TILES)


def gather(pool, keep, outs, at_sb, copied, passed, g, b, landed):
    at = bass.ds(b.s, 1) if b.looped else slice(b.s, b.s + 1)
    pool.tensor_copy(at_sb[0:B, b.u, :].unsqueeze(2), keep.gath[0:B, :, at]).then_inc(copied, 1)
    pool.wait_ge(copied, done(b.s))
    carry(pool, passed)
    for j in range(2):
        pool.indirect_dma_start(
            g[0:B, b.u, j, :], None, outs, bass.IndirectOffsetOnAxis(ap=at_sb[0:B, b.u, j:j + 1], axis=0),
            bounds_check=outs.shape[0] - 1, oob_is_err=True).then_inc(landed[b.u], 16)


def weight(keep, b, j):
    at = bass.ds(b.s, 1) if b.looped else slice(b.s, b.s + 1)
    return keep.W2[0:B, j, at]


def second_cross_attention(nc, io, keep):
    with ExitStack() as ctx:
        sb = lambda name, shape, dt=F32: ctx.enter_context(nc.sbuf_tensor("e_" + name, shape, dt))
        own = ctx.enter_context(semaphores(nc))
        sem = lambda name: own("e_" + name)
        psum = lambda name: ctx.enter_context(nc.psum_tensor("e_" + name, [P, 512], F32))
        X, Z, Y3T, half = keep.X, keep.Z, keep.Y3T, keep.half
        FILL = -99999.0

        w_e = sb("w_e", [P, DC, 3 * D])
        wq, wk, wvT = (w_e[:, :, k * D:(k + 1) * D] for k in range(3))
        A = sb("A", [P, DC, D])
        ones = sb("ones", [1, P])
        got = sb("got", [P, 2, 2, D])
        at = sb("at", [P, 2, 2], I32)
        ctxT = sb("ctxT", [P, 2, DC, CTX])
        ctxN = sb("ctxN", [P, 2, 3, D])
        mask = sb("mask", [P, 2, CTX], I32)
        open_ = sb("open", [P, 2, CTX])
        fill = sb("fill", [1, 2, CTX])
        part = sb("part", [P, D])
        st = sb("st", [P, 2, 2, 6])
        mv = sb("mv", [P, 2, 2, 2])
        ve = sb("ve", [P, 2, 2])
        rs = sb("rs", [P, 2, 2])
        y = sb("y", [P, 2, D])
        z = sb("z", [P, 2, D])
        yT = sb("yT", [P, 2, DC, B])
        qT = sb("qT", [P, 2, DC, B])
        top = sb("top", [P, 2])
        nmax = sb("nmax", [P, 2])
        ex = sb("ex", [P, 2, CTX])
        sums = sb("sums", [P, 2])
        inv = sb("inv", [P, 2])
        exT = sb("exT", [P, 2, 3, B])
        avT = sb("avT", [P, 2, DC, B])
        ps_t, ps_q, ps_p, ps_av, ps_o, ps_z = (psum(n) for n in ("ps_t", "ps_q", "ps_p", "ps_av", "ps_o", "ps_z"))
        ps_s = [psum("ps_s0"), psum("ps_s1")]

        ld_w = sem("ld_w")
        ld_ct, ld_cn, ld_m, ld_got = ([sem(f"{n}{k}") for k in range(2)] for n in ("ld_ct", "ld_cn", "ld_m", "ld_got"))
        passed, pool_passed = sem("passed"), sem("pool_passed")
        folded, fold_out, g_ones = sem("folded"), sem("fold_out"), sem("g_ones")
        s_yT, s_q, s_sc, s_exT, s_av, s_out, s_zT = pe_sems = [
            sem(n) for n in ("yT_ps", "q_ps", "sc_ps", "exT_ps", "av_ps", "out_ps", "zT_ps")]
        a_yT, a_q, a_ex, a_exT, a_av, a_zT = act_sems = [
            sem(n) for n in ("yT_sb", "q_sb", "ex_sb", "exT_sb", "av_sb", "zT_sb")]
        d_part, d_x2, d_st, d_mv, d_open, d_fill, d_y, d_top, d_max, d_inv, d_x3, d_st3, d_mv3, d_z = dve_sems = [
            sem(n) for n in ("part_r", "x2_r", "st_r", "mv_r", "open_r", "fill_r", "y_r", "top_r", "max_r", "inv_r",
                             "x3_r", "st3_r", "mv3_r", "z_r")]
        g_at, g_ve, g_rs, g_ct, g_ve3, g_rs3, g_z = pool_sems = [
            sem(n) for n in ("at_r", "ve_r", "rs_r", "ct_r", "ve3_r", "rs3_r", "zcopy")]
        block = ctx.enter_context(nc.Block())

        @block.sync
        def _(sp):
            sp.dma_start(w_e[:, :, :], io.w_e[:, :, 0:3 * D]).then_inc(ld_w, 16)

            def load_T(b):
                sp.wait_ge(s_sc, reuse(b.s))
                sp.dma_start(ctxT[:, b.u, :, :], io.ctxT[b.s]).then_inc(ld_ct[b.u], 16)
                sp.wait_ge(d_fill, reuse(b.s))
                sp.dma_start(mask[:, b.u, :], io.mask[b.s].to_broadcast([P, CTX])).then_inc(ld_m[b.u], 16)

            def load_N(b):
                sp.wait_ge(s_av, reuse(b.s))
                sp.dma_start(ctxN[:, b.u, 0:2, :],
                             io.ctx[b.s, 0:2 * P, :].rearrange("(c p) d -> p c d", p=P)).then_inc(ld_cn[b.u], 16)
                sp.dma_start(ctxN[0:CK[2], b.u, 2, :], io.ctx[b.s, 2 * P:CTX, :]).then_inc(ld_cn[b.u], 16)

            pipeline(sp, [(load_T, 2), (load_N, 1)])

        @block.gpsimd
        def _(pool):
            pool.memset(ones[:, :], 1.0).then_inc(g_ones, 1)
            for x in pool_sems:
                pool.sem_inc(x, CREDIT)

            def gather_rows(b):
                pool.wait_ge(d_x2, reuse(b.s))
                gather(pool, keep, keep.outs0, at, g_at, pool_passed, got, b, ld_got)

            def rsqrt(k, b, ready, last_reader, plus_eps, power):
                pool.wait_ge(ready, done(b.s))
                pool.wait_ge(last_reader, reuse(b.s))
                pool.tensor_tensor(ve[0:B, b.u, k:k + 1], mv[0:B, b.u, k, 1:2], keep.view("eps")[0:B, :],
                                   ALU.add).then_inc(plus_eps, 1)
                pool.wait_ge(plus_eps, done(b.s))
                pool.tensor_tensor(rs[0:B, b.u, k:k + 1], ve[0:B, b.u, k:k + 1], half[0:B, 0:1],
                                   ALU.pow).then_inc(power, 1)

            def norm_x2(b):
                rsqrt(0, b, d_mv, d_y, g_ve, g_rs)

            def norm_x3(b):
                rsqrt(1, b, d_mv3, d_z, g_ve3, g_rs3)

            def hide(b):
                pool.wait_ge(ld_ct[b.u], b.loaded)
                pool.wait_ge(d_open, done(b.s))
                pool.tensor_tensor(ctxT[:, b.u, :, :], ctxT[:, b.u, :, :],
                                   open_[:, b.u, :].unsqueeze(1).to_broadcast([P, DC, CTX]),
                                   ALU.mult).then_inc(g_ct, 1)

            def store_z(b):
                pool.wait_ge(d_z, done(b.s))
                pool.tensor_copy(Z[0:B, b.s, :], z[0:B, b.u, :]).then_inc(g_z, 1)

            pipeline(pool, [(gather_rows, 3), (norm_x2, 2), (hide, 2), (norm_x3, 0), (store_z, 0)])

        @block.scalar
        def _(act):
            for x in act_sems:
                act.sem_inc(x, CREDIT)
            act.wait_ge(folded, 1)
            act.copy(A[:, 0, :], ps_t[:, 0:D]).then_inc(fold_out, 1)
            act.copy(A[:, 1, :], ps_q[:, 0:D]).then_inc(fold_out, 1)

            def query(b):
                act.wait_ge(s_yT, done(b.s))
                act.copy(yT[:, b.u, :, :], ps_t[:, 0:DC * B]).then_inc(a_yT, 1)
                act.wait_ge(s_q, done(b.s))
                act.copy(qT[:, b.u, :, :], ps_q[:, 0:DC * B]).then_inc(a_q, 1)

            def exponent(b):
                act.wait_ge(d_max, done(b.s))
                act.wait_ge(s_exT, reuse(b.s))
                act.wait_ge(d_inv, reuse(b.s))
                act.activation(ex[0:B, b.u, :], ps_s[b.u][0:B, 0:CTX], ACT.Exp, bias=nmax[0:B, b.u:b.u + 1],
                               accum_out=sums[0:B, b.u:b.u + 1]).then_inc(a_ex, 1)

            def attend(b):
                act.wait_ge(s_exT, done(b.s))
                act.copy(exT[:, b.u, 0:2, :], ps_p[:, 0:2 * B])
                act.copy(exT[0:CK[2], b.u, 2, :], ps_p[0:CK[2], 2 * B:3 * B]).then_inc(a_exT, 1)
                act.wait_ge(s_av, done(b.s))
                act.copy(avT[:, b.u, :, :], ps_av[:, 0:DC * B]).then_inc(a_av, 1)

            def turned(b):
                act.wait_ge(s_zT, done(b.s))
                at = bass.ds(b.s * B, B) if b.looped else slice(b.s * B, (b.s + 1) * B)
                act.copy(Y3T[:, :, at], ps_z[:, 0:DC * B].rearrange("p (c b) -> p c b", c=DC)).then_inc(a_zT, 1)

            pipeline(act, [(query, 1), (attend, 0), (exponent, 1), (turned, -1)])

        @block.vector
        def _(dve):
            for x in dve_sems:
                dve.sem_inc(x, CREDIT)

            def combine(b):
                dve.wait_ge(ld_got[b.u], 2 * b.loaded)
                dve.scalar_tensor_tensor(out=part[0:B, :], in0=got[0:B, b.u, 0, :], scalar=weight(keep, b, 0),
                                         in1=X[0:B, b.s, :], op0=ALU.mult, op1=ALU.add).then_inc(d_part, 1)
                dve.wait_ge(d_part, done(b.s))
                dve.scalar_tensor_tensor(out=X[0:B, b.s, :], in0=got[0:B, b.u, 1, :], scalar=weight(keep, b, 1),
                                         in1=part[0:B, :], op0=ALU.mult, op1=ALU.add).then_inc(d_x2, 1)
                dve.wait_ge(ld_m[b.u], b.loaded)
                dve.wait_ge(g_ct, reuse(b.s))
                dve.tensor_scalar(open_[:, b.u, :], mask[:, b.u, :], 0.0, None, ALU.not_equal).then_inc(d_open, 1)
                dve.wait_ge(d_x2, done(b.s))
                carry(dve, passed)
                dve.bn_stats(st[0:B, b.u, 0, :], X[0:B, b.s, :]).then_inc(d_st, 1)
                dve.wait_ge(s_sc, reuse(b.s))
                dve.tensor_scalar(fill[0:1, b.u, :], mask[0:1, b.u, :], 0.0, FILL, ALU.is_equal,
                                  ALU.mult).then_inc(d_fill, 1)
                dve.wait_ge(d_st, done(b.s))
                dve.wait_ge(g_ve, reuse(b.s))
                carry(dve, passed)
                dve.bn_aggr(mv[0:B, b.u, 0, :], st[0:B, b.u, 0, :]).then_inc(d_mv, 1)

            def norm_x2(b):
                dve.wait_ge(g_rs, done(b.s))
                dve.wait_ge(s_yT, reuse(b.s))
                dve.tensor_scalar(y[0:B, b.u, :], X[0:B, b.s, :], mv[0:B, b.u, 0, 0:1], rs[0:B, b.u, 0:1],
                                  ALU.subtract, ALU.mult).then_inc(d_y, 1)

            def maximum(b):
                dve.wait_ge(s_sc, done(b.s))
                dve.tensor_reduce(top[0:B, b.u:b.u + 1], ps_s[b.u][0:B, 0:CTX], AX.X, ALU.max).then_inc(d_top, 1)
                dve.wait_ge(d_top, done(b.s))
                dve.wait_ge(a_ex, reuse(b.s))
                dve.tensor_scalar(nmax[0:B, b.u:b.u + 1], top[0:B, b.u:b.u + 1], -1.0, None,
                                  ALU.mult).then_inc(d_max, 1)

            def residual(b):
                dve.wait_ge(a_ex, done(b.s))
                dve.reciprocal(inv[0:B, b.u:b.u + 1], sums[0:B, b.u:b.u + 1]).then_inc(d_inv, 1)
                dve.wait_ge(s_out, done(b.s))
                dve.wait_ge(d_inv, done(b.s))
                dve.scalar_tensor_tensor(out=X[0:B, b.s, :], in0=ps_o[0:B, 0:D], scalar=inv[0:B, b.u:b.u + 1],
                                         in1=X[0:B, b.s, :], op0=ALU.mult, op1=ALU.add).then_inc(d_x3, 1)
                dve.wait_ge(d_x3, done(b.s))
                carry(dve, passed)
                dve.bn_stats(st[0:B, b.u, 1, :], X[0:B, b.s, :]).then_inc(d_st3, 1)
                dve.wait_ge(d_st3, done(b.s))
                dve.wait_ge(g_ve3, reuse(b.s))
                carry(dve, passed)
                dve.bn_aggr(mv[0:B, b.u, 1, :], st[0:B, b.u, 1, :]).then_inc(d_mv3, 1)

            def norm_x3(b):
                dve.wait_ge(g_rs3, done(b.s))
                dve.wait_ge(s_zT, reuse(b.s))
                dve.wait_ge(g_z, reuse(b.s))
                dve.tensor_scalar(z[0:B, b.u, :], X[0:B, b.s, :], mv[0:B, b.u, 1, 0:1], rs[0:B, b.u, 1:2],
                                  ALU.subtract, ALU.mult).then_inc(d_z, 1)

            pipeline(dve, [(combine, 2), (maximum, 1), (norm_x2, 2), (residual, 0), (norm_x3, 0)])

        @block.tensor
        def _(pe):
            for x in pe_sems:
                pe.sem_inc(x, CREDIT)
            pe.wait_ge(ld_w, 16)
            pe.wait_ge(g_ones, 1)
            for c in range(DC):
                m = slice(c * P, (c + 1) * P)
                for o in range(DC):
                    mm = pe.matmul((ps_t, ps_q)[c][:, 0:D], wq[:, o, m], wk[:, o, :],
                                   start=(o == 0), stop=(o == DC - 1))
            mm.then_inc(folded, 1)
            pe.wait_ge(fold_out, 2)

            def query(b):
                pe.wait_ge(d_y, done(b.s))
                for c in range(DC):
                    mm = pe.transpose(ps_t[:, c * B:(c + 1) * B], y[0:B, b.u, c * P:(c + 1) * P],
                                      keep.ident[0:B, 0:B])
                mm.then_inc(s_yT, 1)
                pe.wait_ge(a_yT, done(b.s))
                for c in range(DC):
                    for k in range(DC):
                        mm = pe.matmul(ps_q[:, c * B:(c + 1) * B], A[:, k, c * P:(c + 1) * P], yT[:, b.u, k, :],
                                       start=(k == 0), stop=(k == DC - 1))
                mm.then_inc(s_q, 1)
                pe.wait_ge(a_q, done(b.s))
                pe.wait_ge(g_ct, done(b.s))
                pe.wait_ge(d_fill, done(b.s))
                for k in range(DC):
                    pe.matmul(ps_s[b.u][0:B, 0:CTX], qT[:, b.u, k, :], ctxT[:, b.u, k, :],
                              start=(k == 0), stop=False)
                pe.matmul(ps_s[b.u][0:B, 0:CTX], ones[0:1, 0:B], fill[0:1, b.u, :], start=False,
                          stop=True).then_inc(s_sc, 1)

            def attend(b):
                pe.wait_ge(a_ex, done(b.s))
                for k in range(3):
                    mm = pe.transpose(ps_p[0:CK[k], k * B:(k + 1) * B], ex[0:B, b.u, k * P:k * P + CK[k]],
                                      keep.ident[0:B, 0:B])
                mm.then_inc(s_exT, 1)
                pe.wait_ge(a_exT, done(b.s))
                pe.wait_ge(ld_cn[b.u], 2 * b.loaded)
                for c in range(DC):
                    for k in range(3):
                        mm = pe.matmul(ps_av[:, c * B:(c + 1) * B], ctxN[0:CK[k], b.u, k, c * P:(c + 1) * P],
                                       exT[0:CK[k], b.u, k, :], start=(k == 0), stop=(k == 2))
                mm.then_inc(s_av, 1)
                pe.wait_ge(a_av, done(b.s))
                pe.wait_ge(d_x3, done(b.s - 1))
                for k in range(DC):
                    mm = pe.matmul(ps_o[0:B, 0:D], avT[:, b.u, k, :], wvT[:, k, :],
                                   start=(k == 0), stop=(k == DC - 1))
                mm.then_inc(s_out, 1)

            def turn(b):
                pe.wait_ge(d_z, done(b.s))
                pe.wait_ge(a_zT, done(b.s - 1))
                for c in range(DC):
                    mm = pe.transpose(ps_z[:, c * B:(c + 1) * B], z[0:B, b.u, c * P:(c + 1) * P],
                                      keep.ident[0:B, 0:B])
                mm.then_inc(s_zT, 1)

            pipeline(pe, [(query, 1), (attend, 0), (turn, -1)])


TOK = 4 * B


def second_router(nc, io, keep):
    with ExitStack() as ctx:
        sb = lambda name, shape, dt=F32: ctx.enter_context(nc.sbuf_tensor("f_" + name, shape, dt))
        own = ctx.enter_context(semaphores(nc))
        sem = lambda name: own("f_" + name)
        Y3T = keep.Y3T
        RC = RH // P
        rW1 = sb("rW1", [P, DC, RH])
        rW2 = keep.view("rW2").rearrange("p (c e) -> p c e", c=RC)
        rb2 = sb("rb2", [1, E1])
        ones = sb("ones", [1, P])
        rh = sb("rh", [P, 2, RC, TOK])
        ps_h = [ctx.enter_context(nc.psum_tensor(f"f_ps_h{k}", [P, 512], F32)) for k in range(RC)]
        ps_l = [ctx.enter_context(nc.psum_tensor(f"f_ps_l{k}", [P, 512], F32)) for k in range(2)]
        ld_w, g_ones, g_pad = sem("ld_w"), sem("g_ones"), sem("g_pad")
        s_h, s_l, a_h, d_l = sem("h_ps"), sem("l_ps"), sem("h"), sem("l")
        block = ctx.enter_context(nc.Block())
        upto = lambda b, f: RC * b.s + f + 1 + 2 * RC

        @block.sync
        def _(sp):
            sp.dma_start(rW1[:, :, :], io.w_e[:, :, 3 * D:3 * D + RH]).then_inc(ld_w, 16)
            sp.dma_start(rb2[:, :], io.rows[:, D:D + E1]).then_inc(ld_w, 16)

        @block.gpsimd
        def _(pool):
            pool.memset(ones[:, :], 1.0).then_inc(g_ones, 1)
            pool.memset(keep.LG[:, :, :], NEG).then_inc(g_pad, 1)

        @block.scalar
        def _(act):
            act.sem_inc(a_h, 2 * RC)

            def gelus(b):
                act.wait_ge(s_l, reuse(b.s))
                for f in range(RC):
                    act.wait_ge(s_h, upto(b, f))
                    act.activation(rh[:, b.u, f, :], ps_h[f][:, 0:TOK], ACT.Gelu,
                                   bias=keep.col("rb1", f)).then_inc(a_h, 1)

            pipeline(act, [(gelus, 0)], S * B // TOK)

        @block.vector
        def _(dve):
            dve.sem_inc(d_l, CREDIT)
            dve.wait_ge(g_pad, 1)

            def logits(b):
                dve.wait_ge(s_l, done(b.s))
                at = bass.ds(4 * b.s, 4) if b.looped else slice(4 * b.s, 4 * b.s + 4)
                dve.tensor_copy(keep.LG[0:B, at, 0:E1],
                                ps_l[b.u][0:B, 0:4 * E1].rearrange("p (k e) -> p k e", e=E1)).then_inc(d_l, 1)

            pipeline(dve, [(logits, 0)], S * B // TOK)

        @block.tensor
        def _(pe):
            pe.sem_inc(s_h, 2 * RC)
            pe.sem_inc(s_l, CREDIT)
            pe.wait_ge(ld_w, 32)
            pe.wait_ge(g_ones, 1)

            def hidden(b):
                at = bass.ds(TOK * b.s, TOK) if b.looped else slice(TOK * b.s, TOK * (b.s + 1))
                for f in range(RC):
                    pe.wait_ge(a_h, upto(b, f - RC))
                    for c in range(DC):
                        mm = pe.matmul(ps_h[f][:, 0:TOK], rW1[:, c, f * P:(f + 1) * P], Y3T[:, c, at],
                                       start=(c == 0), stop=(c == DC - 1))
                    mm.then_inc(s_h, 1)

            def logits(b):
                pe.wait_ge(a_h, upto(b, RC - 1))
                pe.wait_ge(d_l, reuse(b.s))
                for k in range(4):
                    out = ps_l[b.u][0:B, k * E1:(k + 1) * E1]
                    for f in range(RC):
                        pe.matmul(out, rh[:, b.u, f, k * B:(k + 1) * B], rW2[:, f, :], start=(f == 0), stop=False)
                    mm = pe.matmul(out, ones[0:1, 0:B], rb2[0:1, :], start=False, stop=True)
                mm.then_inc(s_l, 1)

            pipeline(pe, [(hidden, 0), (logits, -1)], S * B // TOK)


def finish(nc, io, keep):
    with ExitStack() as ctx:
        own = ctx.enter_context(semaphores(nc))
        sem = lambda name: own("g_" + name)
        got = ctx.enter_context(nc.sbuf_tensor("g_got", [P, 2, 2, D], F32))
        at = ctx.enter_context(nc.sbuf_tensor("g_at", [P, 2, 2], I32))
        part = ctx.enter_context(nc.sbuf_tensor("g_part", [P, D], F32))
        landed, out = [sem("landed0"), sem("landed1")], sem("stored")
        d_part, d_out, copied, passed = sem("part"), sem("out"), sem("copied"), sem("passed")
        block = ctx.enter_context(nc.Block())

        @block.gpsimd
        def _(pool):
            pool.sem_inc(copied, CREDIT)

            def rows(b):
                pool.wait_ge(d_out, reuse(b.s))
                gather(pool, keep, keep.outs1, at, copied, passed, got, b, landed)

            pipeline(pool, [(rows, 0)])

        @block.vector
        def _(dve):
            dve.sem_inc(d_part, CREDIT)
            dve.sem_inc(d_out, CREDIT)

            def add(b):
                dve.wait_ge(d_out, done(b.s - 1))
                dve.wait_ge(landed[b.u], 2 * b.loaded)
                dve.scalar_tensor_tensor(out=part[0:B, :], in0=got[0:B, b.u, 0, :], scalar=weight(keep, b, 0),
                                         in1=keep.X[0:B, b.s, :], op0=ALU.mult, op1=ALU.add).then_inc(d_part, 1)
                dve.wait_ge(d_part, done(b.s))
                dve.scalar_tensor_tensor(out=keep.X[0:B, b.s, :], in0=got[0:B, b.u, 1, :], scalar=weight(keep, b, 1),
                                         in1=part[0:B, :], op0=ALU.mult, op1=ALU.add).then_inc(d_out, 1)

            pipeline(dve, [(add, 0)])

        @block.sync
        def _(sp):
            def store(b):
                sp.wait_ge(d_out, done(b.s))
                sp.dma_start(io.out[b.s], keep.X[0:B, b.s, :]).then_inc(out, 16)

            pipeline(sp, [(store, 0)])
            sp.wait_ge(out, 16 * S)


COLS = {}
WIDTH = 0
for _name, _w in (("ident", P), ("before", P), ("causal", P), ("kmask", G), ("iota8", G),
                  ("bq", DC), ("bk", DC), ("bv", DC), ("ln1w", DC), ("ln1b", DC), ("ln2w", DC),
                  ("ln2b", DC), ("rb1", RH // P), ("fills", 16), ("thresholds", 5), ("eps", 1),
                  ("router", DC * E0), ("rW2", (RH // P) * E1)):
    COLS[_name] = (WIDTH, _w)
    WIDTH += _w


def laid_out(w):
    f = lambda a: np.ascontiguousarray(a, dtype=a.dtype)
    chunks = lambda a: a.reshape(a.shape[0] // P, P, a.shape[1]).transpose(1, 0, 2)
    L0 = {k[9:]: v for k, v in w.items() if k.startswith("L0_xattn_")}
    F0 = {k[7:]: v for k, v in w.items() if k.startswith("L0_ffn_")}
    L1 = {k[9:]: v for k, v in w.items() if k.startswith("L1_xattn_")}
    F1 = {k[7:]: v for k, v in w.items() if k.startswith("L1_ffn_")}
    p = np.arange(P)
    c = np.zeros((P, WIDTH), np.float32)

    def put(name, a):
        at, n = COLS[name]
        c[:a.shape[0], at:at + n] = a

    put("ident", np.eye(P))
    put("before", p[:, None] < p[None, :])
    put("causal", np.where(p[None, :] % T <= p[:, None] % T, 0.0, NEG))
    put("kmask", p[:, None] // HD == np.arange(G)[None, :])
    put("iota8", np.broadcast_to(np.arange(G), (P, G)))
    put("eps", np.full((P, 1), EPS))
    put("fills", np.broadcast_to(np.arange(16), (P, 16)))
    put("thresholds", np.broadcast_to(TILE1 * np.arange(5), (P, 5)))
    for name, v in (("bq", L0["bq"]), ("bk", L0["bk"]), ("bv", L0["bv"]), ("ln1w", F0["ln1_weight"]),
                    ("ln1b", F0["ln1_bias"]), ("ln2w", F0["ln2_weight"]), ("ln2b", F0["ln2_bias"]),
                    ("rb1", F1["rb1"])):
        put(name, v.reshape(-1, P).T)
    put("router", chunks(F0["router_weight"]).reshape(P, -1))
    put("rW2", chunks(F1["rW2"]).reshape(P, -1))
    qkv = F0["qkv_weight"].reshape(G, QJ + 2, HD, D).transpose(1, 0, 2, 3).reshape(4 * P, D)
    proj = F0["proj_weight"].reshape(D, G, QJ, HD).transpose(2, 1, 3, 0).reshape(D, D)
    return {
        "x": f(w["x"]), "ctx": f(w["ctx_1024"]),
        "ctxT": f(w["ctx_1024"].transpose(0, 2, 1).reshape(S, DC, P, CTX).transpose(0, 2, 1, 3)),
        "mask": f(w["mask_BxS2_ik1"][:, None, :]),
        "consts": c,
        "rows": f(np.concatenate([L0["bo"], F1["rb2"]])[None, :]),
        "w_a": f(np.concatenate([chunks(L0["Wq"]), chunks(L0["Wk"]), chunks(L0["Wv"]),
                                 chunks(L0["Wo"].T)], axis=2)),
        "w_qkvT": f(chunks(qkv.T)),
        "w_projT": f(chunks(proj)),
        "w_e": f(np.concatenate([chunks(L1["Wq"]), chunks(L1["Wk"]), chunks(L1["Wv"].T),
                                 chunks(F1["rW1"])], axis=2)),
        "w_f0": f(np.concatenate([np.stack([chunks(a).reshape(P, -1) for a in F0["moe_w1"]]),
                                  np.stack([chunks(a).reshape(P, -1) for a in F0["moe_w2"]])], axis=2)),
        "w_f1": f(np.concatenate([np.stack([chunks(a).reshape(P, -1) for a in F1["We1"]]),
                                  np.stack([chunks(a).reshape(P, -1) for a in F1["We2"]])], axis=2)),
        "be1": f(F1["be1"].reshape(E1, FC, P).transpose(0, 2, 1)),
        "be2": f(F1["be2"][:, None, :]),
    }




class Kept:
    pass


def two_layers(nc, io):
    keep = Kept()
    with ExitStack() as ctx:
        sb = lambda name, shape, dt=F32: ctx.enter_context(nc.sbuf_tensor(name, shape, dt))
        keep.consts = sb("consts", [P, WIDTH])
        keep.ld_consts = ctx.enter_context(nc.semaphore("ld_consts"))
        view = lambda name: keep.consts[:, COLS[name][0]:sum(COLS[name])]
        keep.view = view
        keep.col = lambda name, c: view(name)[:, c:c + 1]
        keep.ident, keep.kmask = view("ident"), view("kmask")
        keep.half = sb("half", [P, 1])
        keep.zeros = sb("zeros", [P, D])
        dram = lambda name, shape: nc.dram_tensor(name, shape, F32, kind="Internal").ap()
        keep.values = dram("values", (T, B, P))
        keep.slots0, keep.outs0 = dram("slots0", (E0 * CAP, D)), dram("outs0", (E0 * CAP, D))
        keep.slots1, keep.outs1 = dram("slots1", (TILES1 * TILE1, D)), dram("outs1", (TILES1 * TILE1, D))
        keep.zeroed = ctx.enter_context(nc.semaphore("zeroed"))
        keep.vx_zero = ctx.enter_context(nc.semaphore("vx_zero"))
        keep.X = sb("X", [P, S, D])
        keep.Z = sb("Z", [P, S, D])
        keep.LG = sb("LG", [P, S, G])
        keep.V8 = sb("V8", [P, S, G])
        keep.I8 = sb("I8", [P, S, G], U32)
        keep.W2 = sb("W2", [P, 2, S])
        keep.scat = sb("scat", [P, 2, S], I32)
        keep.gath = sb("gath", [P, 2, S], I32)
        keep.tile_expert = sb("tile_expert", [P, TILES1], I32)
        with ExitStack() as first:
            sb0 = lambda name, shape, dt=F32: first.enter_context(nc.sbuf_tensor(name, shape, dt))
            keep.Y1 = sb0("Y1", [P, S, D])
            keep.Q = sb0("Q", [P, B, QJ, T])
            keep.K = sb0("K", [P, B, T])
            keep.VX = sb0("VX", [P, B, P])
            first_cross_attention(nc, io, keep)
            keep.AT = sb0("AT", [P, QJ, S, B])
            self_attention(nc, io, keep)
            project_and_score(nc, io, keep)
        route(nc, io, keep, False)
        expert_tiles(nc, io, keep, False)
        keep.Y3T = sb("Y3T", [P, DC, S * B])
        second_cross_attention(nc, io, keep)
        second_router(nc, io, keep)
        route(nc, io, keep, True)
        expert_tiles(nc, io, keep, True)
        finish(nc, io, keep)


def kernel(**inputs):
    import concourse.bacc as bacc
    from concourse.bass_utils import run_bass_kernel_spmd

    arrays = laid_out({k: np.asarray(v) for k, v in inputs.items()})
    nc = bacc.Bacc("TRN2", target_bir_lowering=False, num_devices=1)
    io = Kept()
    for name, a in arrays.items():
        io.__dict__[name] = nc.dram_tensor(f"in_{name}", a.shape, mybir.dt.from_np(a.dtype),
                                           kind="ExternalInput").ap()
    io.out = nc.dram_tensor("out_0", (S, B, D), F32, kind="ExternalOutput").ap()
    two_layers(nc, io)
    r = run_bass_kernel_spmd(nc, [{f"in_{k}": a for k, a in arrays.items()}], core_ids=[0])
    return r.results[0]["out_0"]
```

```python
from contextlib import ExitStack, contextmanager

import numpy as np

import concourse.bass as bass
import concourse.mybir as mybir

F32 = mybir.dt.float32
F32R = mybir.dt.float32r
I32 = mybir.dt.int32
U32 = mybir.dt.uint32
ALU = mybir.AluOpType
ACT = mybir.ActivationFunctionType
AX = mybir.AxisListType

S, B, D = 16, 100, 256
CTX = 361
P = 128
DC = D // P
CK = [128, 128, CTX - 256]
G, HD, T = 8, 16, 16
QJ = 2
FFN = 1024
FC = FFN // P
E0, CAP = 8, 500
ROWS0, SUB0 = 125, 4
E1 = 4
ROWS1, SUB1 = 128, 3
TILE1 = ROWS1 * SUB1
TILES1 = (2 * S * B + E1 * (TILE1 - 1)) // TILE1
RH = 2 * D
TOPK = 32
EPS = 1e-5
GONE = -3.0e38
NEG = -1.0e30
CREDIT = 2


def done(s):
    return s + 1 + CREDIT


def reuse(s):
    return s - 1 + CREDIT


@contextmanager
def semaphores(nc):
    own = []

    def allocate(name):
        own.append(nc.alloc_semaphore(name))
        return own[-1]

    yield allocate
    nc.clear_and_free_semaphores(own)
    nc.all_engine_barrier()


def carry(eng, passed):
    eng.sem_inc(passed, 1)


class Batch:

    def __init__(self, first, loop=0):
        self.first, self.loop = first, loop
        self.s, self.u, self.h = first + 2 * loop, first % 2, first // 2 + loop
        self.looped = not isinstance(loop, int)
        self.loaded = 16 * self.h + 16

    def plus(self, d):
        return Batch(self.first + d, self.loop)


def pipeline(eng, stages, count=S):
    least, most = min(o for _, o in stages), max(o for _, o in stages)
    start = max(-least, 0)
    pairs = (count - most - start) // 2

    def step(n, loop=0, full=False):
        for stage, offset in stages:
            if full or 0 <= n + offset < count:
                stage(Batch(n + offset, loop))

    for n in range(-most, start):
        step(n)
    with eng.Fori(0, pairs) as i:
        step(start, i, True)
        step(start + 1, i, True)
    for n in range(start + 2 * pairs, count - least):
        step(n)


def first_cross_attention(nc, io, keep):
    with ExitStack() as ctx:
        sb = lambda name, shape, dt=F32: ctx.enter_context(nc.sbuf_tensor(name, shape, dt))
        own = ctx.enter_context(semaphores(nc))
        sem = lambda name: own(name)
        psum = lambda name: ctx.enter_context(nc.psum_tensor(name, [P, 512], F32))

        w_a = sb("w_a", [P, DC, 4 * D])
        wq, wk, wv, woT = (w_a[:, :, k * D:(k + 1) * D] for k in range(4))
        wqkvT = sb("wqkvT", [P, DC, 4 * P])
        rows_sb = sb("rows_a", [1, D])
        ones = sb("ones_a", [1, P])
        A = sb("A", [P, DC, D])
        wqbk = sb("wqbk", [P, DC])
        Wov = sb("Wov", [P, DC, D])
        bqWk = sb("bqWk", [P, DC])
        bcast = sb("bcast", [P, 2, DC, P])
        qbk0 = sb("qbk0", [P, 1])
        orow = sb("orow", [P, D])

        ctxT = sb("ctxT", [P, 2, DC, CTX])
        ctxN = sb("ctxN", [P, 2, 3, D])
        st = sb("st", [P, 2, 2, 6])
        mv = sb("mv", [P, 2, 2, 2])
        ve = sb("ve", [P, 2, 3])
        rs = sb("rs", [P, 2, 3])
        v2 = sb("v2", [P, 2])
        y = sb("y", [P, 2, D])
        yT = sb("yT", [P, 2, DC, B])
        qT = sb("qT", [P, 2, DC, B])
        qb = sb("qb", [P, 2])
        sc = sb("sc", [P, 2, CTX])
        left = sb("left", [P, CTX])
        top = sb("top", [P, 2, 8])
        best = sb("best", [P, 2, 8])
        nmax = sb("nmax", [P, 2])
        ex = sb("ex", [P, 2, CTX])
        pr = sb("pr", [P, 2, CTX])
        psums = sb("psums", [P, 2])
        pinv = sb("pinv", [P, 2])
        prT = sb("prT", [P, 2, 3, B])
        avT = sb("avT", [P, 2, DC, B])
        z = sb("z", [P, 2, D])
        zT = sb("zT", [P, 2, DC, B])
        V = sb("V", [P, 2, P])

        ps_q, ps_p, ps_z, ps_o, ps_qkv = (psum(n) for n in ("ps_q", "ps_p", "ps_z", "ps_o", "ps_qkv"))
        ps_s = [psum("ps_s0"), psum("ps_s1")]
        ps_yT, ps_av = ps_q[:, 256:256 + DC * B], ps_p[:, 3 * B:(3 + DC) * B]

        ld_w, ld_w2, ld_x, ld_x2 = sem("ld_w"), sem("ld_w2"), sem("ld_x"), sem("ld_x2")
        ld_rows, ld_qkv = sem("ld_rows"), sem("ld_qkv")
        ld_ct = [sem("ld_ct0"), sem("ld_ct1")]
        ld_cn = [sem("ld_cn0"), sem("ld_cn1")]
        st_v = [sem("st_v0"), sem("st_v1")]
        fold_in, folded, fold_out = sem("fold_in"), sem("folded"), sem("fold_out")
        s_yT, s_q, s_sc, s_prT, s_av, s_out, s_zT, s_qkv = pe_sems = [
            sem(n) for n in ("yT_ps", "q_ps", "sc_ps", "prT_ps", "av_ps", "out_ps", "zT_ps", "qkv_ps")]
        a_yT, a_q, a_sc, a_ex, a_prT, a_av, a_zT, a_qkv = act_sems = [
            sem(n) for n in ("yT_sb", "q_sb", "sc_sb", "exp_sb", "prT_sb", "av_sb", "zT_sb", "qkv_sb")]
        d_st, d_mv, d_y, d_top, d_max, d_left, d_pr, d_inv, d_x1, d_st1, d_mv1, d_y1, d_v2, d_z = dve_sems = [
            sem(n) for n in ("st", "mv_r", "y_r", "top_r", "max_r", "left_r", "pr_r", "inv_r", "x1_r",
                             "st1_r", "mv1_r", "y1_r", "v2_r", "z_r")]
        g_ve, g_rs, g_row, g_ve1, g_rs1, g_ve2, g_rs2 = pool_sems = [
            sem(n) for n in ("ve_r", "rs_r", "row_r", "ve1_r", "rs1_r", "ve2_r", "rs2_r")]
        g_const = sem("g_const_a")
        passed = sem("passed")

        X, Y1, Q, K = keep.X, keep.Y1, keep.Q, keep.K
        ident, half = keep.ident, keep.half
        col = keep.col
        block = ctx.enter_context(nc.Block())

        @block.sync
        def _(sp):
            sp.dma_start(keep.consts[:, :], io.consts).then_inc(keep.ld_consts, 16)
            sp.dma_start(w_a[:, :, 0:2 * D], io.w_a[:, :, 0:2 * D]).then_inc(ld_w, 16)
            sp.dma_start(w_a[:, :, 2 * D:4 * D], io.w_a[:, :, 2 * D:4 * D]).then_inc(ld_w2, 16)
            sp.dma_start(rows_sb[:, :], io.rows[:, 0:D]).then_inc(ld_rows, 16)
            sp.dma_start(wqkvT[:, :, :], io.w_qkvT).then_inc(ld_qkv, 16)

            def load_T(b):
                sp.wait_ge(s_sc, reuse(b.s))
                sp.dma_start(ctxT[:, b.u, :, :], io.ctxT[b.s]).then_inc(ld_ct[b.u], 16)

            def load_N(b):
                sp.wait_ge(s_av, reuse(b.s))
                sp.dma_start(ctxN[:, b.u, 0:2, :],
                             io.ctx[b.s, 0:2 * P, :].rearrange("(c p) d -> p c d", p=P)).then_inc(ld_cn[b.u], 16)
                sp.dma_start(ctxN[0:CK[2], b.u, 2, :], io.ctx[b.s, 2 * P:CTX, :]).then_inc(ld_cn[b.u], 16)

            def store_v(b):
                sp.wait_ge(a_qkv, done(b.s))
                sp.dma_start(keep.values[b.s], V[0:B, b.u, :]).then_inc(st_v[b.u], 16)

            for x in st_v:
                sp.sem_inc(x, 16)
            def clear(b):
                if not b.looped and b.s < 2:
                    slots, rows = ((keep.slots0, ROWS0), (keep.slots1, ROWS1))[b.s]
                    sp.wait_ge(g_const, 3)
                    sp.dma_start(slots.rearrange("(a p) f -> p a f", p=rows),
                                 keep.zeros[0:rows, :].unsqueeze(1).to_broadcast(
                                     [rows, slots.shape[0] // rows, D])).then_inc(keep.zeroed, 16)

            pipeline(sp, [(load_T, 2), (load_N, 1), (store_v, -3), (clear, 0)])
            for x in st_v:
                sp.wait_ge(x, 16 * (S // 2) + 16)

        @block.scalar
        def _(act):
            x = io.x.rearrange("s b d -> b s d")
            act.dma_start(X[0:B, 0:2, :], x[:, 0:2, :]).then_inc(ld_x, 16)
            act.dma_start(X[0:B, 2:S, :], x[:, 2:S, :]).then_inc(ld_x2, 16)
            for x in act_sems:
                act.sem_inc(x, CREDIT)
            act.wait_ge(keep.ld_consts, 16)
            act.wait_ge(g_const, 3)
            for k, name in enumerate(("bq", "bv")):
                for c in range(DC):
                    last = act.activation(bcast[:, k, c, :], keep.zeros[:, 0:P], ACT.Identity, bias=col(name, c))
            last.then_inc(fold_in, 1)
            act.wait_ge(folded, 1)
            act.copy(A[:, 0, :], ps_z[:, 0:D]).then_inc(fold_out, 1)
            act.copy(A[:, 1, :], ps_q[:, 0:D]).then_inc(fold_out, 1)
            act.copy(wqbk[:, :], ps_p[:, 0:DC]).then_inc(fold_out, 1)
            act.copy(bqWk[:, :], ps_p[:, DC:2 * DC]).then_inc(fold_out, 1)
            act.copy(qbk0[:, :], ps_p[:, 4:5]).then_inc(fold_out, 1)
            act.wait_ge(folded, 2)
            act.copy(Wov[:, 0, :], ps_s[0][:, 0:D]).then_inc(fold_out, 1)
            act.copy(Wov[:, 1, :], ps_s[1][:, 0:D]).then_inc(fold_out, 1)
            act.copy(orow[:, :], ps_o[:, 0:D]).then_inc(fold_out, 1)
            act.wait_ge(fold_out, 8)

            def turned_y(b):
                act.wait_ge(s_yT, done(b.s))
                act.copy(yT[:, b.u, :, :], ps_yT).then_inc(a_yT, 1)

            def query(b):
                act.wait_ge(s_q, done(b.s))
                for c in range(DC):
                    act.activation(qT[:, b.u, c, :], ps_q[:, c * B:(c + 1) * B], ACT.Identity,
                                   bias=bqWk[:, c:c + 1])
                act.wait_ge(a_sc, reuse(b.s))
                act.activation(qb[0:B, b.u:b.u + 1], ps_q[0:B, 2 * B:2 * B + 1], ACT.Identity,
                               bias=qbk0[0:B, :]).then_inc(a_q, 1)

            def scores(b):
                act.wait_ge(s_sc, done(b.s))
                act.wait_ge(a_q, done(b.s))
                act.wait_ge(d_pr, reuse(b.s))
                act.activation(sc[0:B, b.u, :], ps_s[b.u][0:B, 0:CTX], ACT.Identity,
                               bias=qb[0:B, b.u:b.u + 1]).then_inc(a_sc, 1)

            def exponent(b):
                act.wait_ge(d_max, done(b.s))
                act.activation(ex[0:B, b.u, :], sc[0:B, b.u, :], ACT.Exp, bias=nmax[0:B, b.u:b.u + 1],
                               scale=1.0 / D ** 0.5).then_inc(a_ex, 1)

            def turned_p(b):
                act.wait_ge(s_prT, done(b.s))
                act.copy(prT[:, b.u, 0:2, :], ps_p[:, 0:2 * B])
                act.copy(prT[0:CK[2], b.u, 2, :], ps_p[0:CK[2], 2 * B:3 * B]).then_inc(a_prT, 1)

            def attended(b):
                act.wait_ge(s_av, done(b.s))
                act.copy(avT[:, b.u, :, :], ps_av).then_inc(a_av, 1)

            def turned_z(b):
                act.wait_ge(s_zT, done(b.s))
                for c in range(DC):
                    last = act.activation(zT[:, b.u, c, :], ps_z[:, c * B:(c + 1) * B], ACT.Identity,
                                          bias=col("ln1b", c), scale=col("ln1w", c))
                last.then_inc(a_zT, 1)

            def projected(b):
                act.wait_ge(s_qkv, done(b.s))
                act.wait_ge(st_v[b.u], b.loaded)
                act.copy(K[:, :, b.s], ps_qkv[:, 2 * B:3 * B])
                act.copy(Q[:, :, :, b.s].rearrange("p b j -> p j b"),
                         ps_qkv[:, 0:2 * B].rearrange("p (j b) -> p j b", j=QJ))
                act.copy(V[0:B, b.u, :], ps_qkv[0:B, 3 * B:3 * B + P]).then_inc(a_qkv, 1)

            pipeline(act, [(turned_y, 1), (turned_p, -1), (exponent, 0), (turned_z, -3), (query, 1), (attended, -1),
                           (projected, -3), (scores, 1)])

        @block.gpsimd
        def _(pool):
            pool.memset(ones[:, :], 1.0).then_inc(g_const, 1)
            pool.memset(half[:, 0:1], -0.5).then_inc(g_const, 1)
            pool.memset(keep.zeros[:, :], 0.0).then_inc(g_const, 1)
            for x in pool_sems:
                pool.sem_inc(x, CREDIT)
            for b in range(0, B, B // 4):
                pool.memset(keep.VX[:, b:b + B // 4, :], 0.0).then_inc(keep.vx_zero, 1)
            pool.wait_ge(g_const, 3)
            pool.wait_ge(keep.ld_consts, 16)

            def rsqrt(k, b, var, ready, plus_eps, power):
                pool.wait_ge(ready, done(b.s))
                pool.tensor_tensor(ve[0:B, b.u, k:k + 1], var, keep.view("eps")[0:B, :], ALU.add).then_inc(plus_eps, 1)
                pool.wait_ge(plus_eps, done(b.s))
                pool.tensor_tensor(rs[0:B, b.u, k:k + 1], ve[0:B, b.u, k:k + 1], half[0:B, 0:1],
                                   ALU.pow).then_inc(power, 1)

            def norm_x(b):
                rsqrt(0, b, mv[0:B, b.u, 0, 1:2], d_mv, g_ve, g_rs)

            def add_row(b):
                if not b.looped and b.s == 0:
                    pool.wait_ge(fold_out, 8)
                pool.wait_ge(d_y, done(b.s))
                pool.tensor_tensor(X[0:B, b.s, :], X[0:B, b.s, :], orow[0:B, :], ALU.add).then_inc(g_row, 1)

            def norm_x1(b):
                rsqrt(1, b, mv[0:B, b.u, 1, 1:2], d_mv1, g_ve1, g_rs1)

            def norm_y1(b):
                rsqrt(2, b, v2[0:B, b.u:b.u + 1], d_v2, g_ve2, g_rs2)

            pipeline(pool, [(norm_x1, -2), (add_row, 2), (norm_y1, -2), (norm_x, 3)])

        @block.vector
        def _(dve):
            for x in dve_sems:
                dve.sem_inc(x, CREDIT)
            dve.wait_ge(ld_x, 16)

            def stats_x(b):
                if not b.looped and b.s == 2:
                    dve.wait_ge(ld_x2, 16)
                dve.bn_stats(st[0:B, b.u, 0, :], X[0:B, b.s, :]).then_inc(d_st, 1)

            def aggregate_x(b):
                dve.wait_ge(d_st, done(b.s))
                carry(dve, passed)
                dve.bn_aggr(mv[0:B, b.u, 0, :], st[0:B, b.u, 0, :]).then_inc(d_mv, 1)

            def norm_x(b):
                dve.wait_ge(g_rs, done(b.s))
                dve.tensor_scalar(y[0:B, b.u, :], X[0:B, b.s, :], mv[0:B, b.u, 0, 0:1], rs[0:B, b.u, 0:1],
                                  ALU.subtract, ALU.mult).then_inc(d_y, 1)

            def source(b, r):
                return sc[0:B, b.u, :] if r == 0 else left[0:B, :]

            def found(b, r):
                return best[0:B, b.u, :] if r == 0 else top[0:B, r % 2, :]

            def find(r):
                def stage(b):
                    if r == 0:
                        dve.wait_ge(a_sc, done(b.s))
                    else:
                        dve.wait_ge(d_left, 4 * b.s + r + CREDIT)
                    carry(dve, passed)
                    dve.max(found(b, r), source(b, r)).then_inc(d_top, 1)
                return stage

            def negate(b):
                dve.wait_ge(d_top, 4 * b.s + 1 + CREDIT)
                dve.tensor_scalar(nmax[0:B, b.u:b.u + 1], best[0:B, b.u, 0:1], -1.0 / D ** 0.5, None,
                                  ALU.mult).then_inc(d_max, 1)

            def remove(r):
                def stage(b):
                    dve.wait_ge(d_top, 4 * b.s + r + 1 + CREDIT)
                    carry(dve, passed)
                    dve.match_replace(left[0:B, :], found(b, r), source(b, r), GONE).then_inc(d_left, 1)
                return stage

            def select(b):
                dve.wait_ge(d_left, 4 * b.s + 4 + CREDIT)
                dve.wait_ge(a_ex, done(b.s))
                dve.scalar_tensor_tensor(out=pr[0:B, b.u, :], in0=left[0:B, :], scalar=0.9 * GONE,
                                         in1=ex[0:B, b.u, :], op0=ALU.is_le, op1=ALU.mult,
                                         accum_out=psums[0:B, b.u:b.u + 1]).then_inc(d_pr, 1)

            def invert(b):
                dve.wait_ge(d_pr, done(b.s))
                dve.reciprocal(pinv[0:B, b.u:b.u + 1], psums[0:B, b.u:b.u + 1]).then_inc(d_inv, 1)

            def residual(b):
                dve.wait_ge(s_out, done(b.s))
                dve.wait_ge(g_row, done(b.s))
                dve.wait_ge(d_inv, done(b.s))
                dve.scalar_tensor_tensor(out=X[0:B, b.s, :], in0=ps_o[0:B, 0:D], scalar=pinv[0:B, b.u:b.u + 1],
                                         in1=X[0:B, b.s, :], op0=ALU.mult, op1=ALU.add).then_inc(d_x1, 1)

            def stats_x1(b):
                dve.wait_ge(d_x1, done(b.s))
                carry(dve, passed)
                dve.bn_stats(st[0:B, b.u, 1, :], X[0:B, b.s, :]).then_inc(d_st1, 1)

            def aggregate_x1(b):
                dve.wait_ge(d_st1, done(b.s))
                carry(dve, passed)
                dve.bn_aggr(mv[0:B, b.u, 1, :], st[0:B, b.u, 1, :]).then_inc(d_mv1, 1)

            def norm_x1(b):
                dve.wait_ge(g_rs1, done(b.s))
                dve.tensor_scalar(Y1[0:B, b.s, :], X[0:B, b.s, :], mv[0:B, b.u, 1, 0:1], rs[0:B, b.u, 1:2],
                                  ALU.subtract, ALU.mult).then_inc(d_y1, 1)
                dve.tensor_scalar(v2[0:B, b.u:b.u + 1], mv[0:B, b.u, 1, 1:2], rs[0:B, b.u, 1:2],
                                  rs[0:B, b.u, 1:2], ALU.mult, ALU.mult).then_inc(d_v2, 1)

            def norm_y1(b):
                dve.wait_ge(g_rs2, done(b.s))
                dve.wait_ge(d_y1, done(b.s))
                dve.tensor_scalar(z[0:B, b.u, :], Y1[0:B, b.s, :], rs[0:B, b.u, 2:3], None,
                                  ALU.mult).then_inc(d_z, 1)

            pipeline(dve, [(find(0), 0), (residual, -2), (negate, 0), (remove(0), 0), (stats_x1, -2), (find(1), 0),
                           (aggregate_x1, -2), (remove(1), 0), (norm_x, 2), (find(2), 0), (norm_x1, -2),
                           (remove(2), 0), (stats_x, 3), (find(3), 0), (norm_y1, -2), (remove(3), 0),
                           (aggregate_x, 3), (select, 0), (invert, 0)])

        @block.tensor
        def _(pe):
            for x in pe_sems:
                pe.sem_inc(x, CREDIT)
            pe.wait_ge(keep.ld_consts, 16)
            pe.wait_ge(ld_w, 16)
            pe.wait_ge(fold_in, 1)
            pe.wait_ge(g_const, 3)

            def fold(out, pairs):
                for k, (l, r) in enumerate(pairs):
                    mm = pe.matmul(out, l, r, start=(k == 0), stop=(k == len(pairs) - 1))
                return mm

            for c in range(DC):
                m = slice(c * P, (c + 1) * P)
                fold((ps_z, ps_q)[c][:, 0:D], [(wq[:, o, m], wk[:, o, :]) for o in range(DC)])
                fold(ps_p[:, c:c + 1], [(wq[:, o, m], col("bk", o)) for o in range(DC)])
                fold(ps_p[:, DC + c:DC + c + 1], [(wk[:, o, m], col("bq", o)) for o in range(DC)])
            fold(ps_p[:, 4:5], [(bcast[:, 0, o, :], col("bk", o)) for o in range(DC)]).then_inc(folded, 1)
            pe.wait_ge(ld_w2, 16)
            pe.wait_ge(ld_rows, 16)
            for c in range(DC):
                fold(ps_s[c][:, 0:D], [(wv[:, o, c * P:(c + 1) * P], woT[:, o, :]) for o in range(DC)])
            fold(ps_o[:, 0:D], [(bcast[:, 1, o, :], woT[:, o, :]) for o in range(DC)]
                 + [(ones[0:1, :], rows_sb[0:1, :])]).then_inc(folded, 1)
            pe.wait_ge(fold_out, 8)
            pe.wait_ge(ld_qkv, 16)

            def turn_y(b):
                pe.wait_ge(d_y, done(b.s))
                for c in range(DC):
                    mm = pe.transpose(ps_yT[:, c * B:(c + 1) * B], y[0:B, b.u, c * P:(c + 1) * P], ident[0:B, 0:B])
                mm.then_inc(s_yT, 1)

            def query(b):
                pe.wait_ge(a_yT, done(b.s))
                for c in range(DC):
                    for k in range(DC):
                        pe.matmul(ps_q[:, c * B:(c + 1) * B], A[:, k, c * P:(c + 1) * P], yT[:, b.u, k, :],
                                  start=(k == 0), stop=(k == DC - 1))
                for k in range(DC):
                    mm = pe.matmul(ps_q[0:B, 2 * B:2 * B + 1], yT[:, b.u, k, :], wqbk[:, k:k + 1],
                                   start=(k == 0), stop=(k == DC - 1))
                mm.then_inc(s_q, 1)

            def scores(b):
                pe.wait_ge(a_q, done(b.s))
                pe.wait_ge(ld_ct[b.u], b.loaded)
                for k in range(DC):
                    mm = pe.matmul(ps_s[b.u][0:B, 0:CTX], qT[:, b.u, k, :], ctxT[:, b.u, k, :],
                                   start=(k == 0), stop=(k == DC - 1))
                mm.then_inc(s_sc, 1)

            def turn_p(b):
                pe.wait_ge(d_pr, done(b.s))
                for k in range(3):
                    mm = pe.transpose(ps_p[0:CK[k], k * B:(k + 1) * B], pr[0:B, b.u, k * P:k * P + CK[k]],
                                      ident[0:B, 0:B])
                mm.then_inc(s_prT, 1)

            def attend(b):
                pe.wait_ge(a_prT, done(b.s))
                pe.wait_ge(ld_cn[b.u], 2 * b.loaded)
                for c in range(DC):
                    for k in range(3):
                        mm = pe.matmul(ps_av[:, c * B:(c + 1) * B], ctxN[0:CK[k], b.u, k, c * P:(c + 1) * P],
                                       prT[0:CK[k], b.u, k, :], start=(k == 0), stop=(k == 2))
                mm.then_inc(s_av, 1)

            def output(b):
                pe.wait_ge(a_av, done(b.s))
                pe.wait_ge(d_x1, done(b.s - 1))
                for k in range(DC):
                    mm = pe.matmul(ps_o[0:B, 0:D], avT[:, b.u, k, :], Wov[:, k, :],
                                   start=(k == 0), stop=(k == DC - 1))
                mm.then_inc(s_out, 1)

            def turn_z(b):
                pe.wait_ge(d_z, done(b.s))
                for c in range(DC):
                    mm = pe.transpose(ps_z[:, c * B:(c + 1) * B], z[0:B, b.u, c * P:(c + 1) * P], ident[0:B, 0:B])
                mm.then_inc(s_zT, 1)

            def project(b):
                pe.wait_ge(a_zT, done(b.s))
                pe.wait_ge(a_qkv, done(b.s - 1))
                for m in range(3):
                    for k in range(DC):
                        pe.matmul(ps_qkv[:, m * B:(m + 1) * B], wqkvT[:, k, m * P:(m + 1) * P], zT[:, b.u, k, :],
                                  start=(k == 0), stop=(k == DC - 1))
                for k in range(DC):
                    mm = pe.matmul(ps_qkv[0:B, 3 * B:3 * B + P], zT[:, b.u, k, :], wqkvT[:, k, 3 * P:4 * P],
                                   start=(k == 0), stop=(k == DC - 1))
                mm.then_inc(s_qkv, 1)

            pipeline(pe, [(turn_y, 1), (turn_p, -1), (turn_z, -3), (query, 1), (attend, -1), (project, -3),
                          (scores, 1), (output, -1)])


GROUPS = B // 4


def self_attention(nc, io, keep):
    with ExitStack() as ctx:
        sb = lambda name, shape, dt=F32: ctx.enter_context(nc.sbuf_tensor(name, shape, dt))
        own = ctx.enter_context(semaphores(nc))
        sem = lambda name: own(name)
        both = lambda name: [ctx.enter_context(nc.psum_tensor(f"{name}{k}", [P, 512], F32)) for k in range(2)]

        Qs = sb("Qs", [P, 2, P])
        Ks = sb("Ks", [P, 2, 4, G, T])
        Vs = sb("Vs", [P, 2, 4, P])
        sm = sb("sm", [P, 2, P])
        top = sb("top_b", [P, 2, G])
        ex = sb("ex_b", [P, 2, P])
        den = sb("den", [P, 2, G])
        rden = sb("rden", [P, 2, G])
        exT = sb("exT", [P, 2, P])
        o = sb("o", [P, 2, P])
        ps_s, ps_t, ps_o, ps_u = both("psb_s"), both("psb_t"), both("psb_o"), both("psb_u")

        vx = sem("vx_loaded")
        g_k = sem("b_keys")
        s_sc, s_exT, s_o, s_oT = pe_sems = [sem(n) for n in ("b_sc", "b_exT_ps", "b_o", "b_oT_ps")]
        a_q, a_ex, a_exT, a_oT = act_sems = [sem(n) for n in ("b_q", "b_ex", "b_exT", "b_oT")]
        d_m, d_top, d_sub, d_sum, d_den, d_v, d_o = dve_sems = [
            sem(n) for n in ("b_m", "b_top", "b_sub", "b_sum", "b_den", "b_v", "b_o_sb")]
        Q, K, VX, AT = keep.Q, keep.K, keep.VX, keep.AT
        block = ctx.enter_context(nc.Block())

        @block.sync
        def _(sp):
            sp.dma_start(keep.projT[:, :, :], io.w_projT).then_inc(keep.ld_proj, 16)
            sp.wait_ge(keep.vx_zero, 4)
            for g in range(G):
                with nc.allow_non_contiguous_dma(reason="a head's 16 values"):
                    sp.dma_start(VX[g * T:(g + 1) * T, :, g * HD:(g + 1) * HD],
                                 keep.values[:, :, g * HD:(g + 1) * HD]).then_inc(vx, 16)
            sp.wait_ge(keep.zeroed, 32)

        @block.scalar
        def _(act):
            for x in act_sems:
                act.sem_inc(x, CREDIT)

            def queries(b):
                act.wait_ge(s_sc, reuse(b.s))
                act.copy(Qs[:, b.u, :], Q[:, bass.ds(4 * b.s, 4), :, :]).then_inc(a_q, 1)

            def exponent(b):
                act.wait_ge(d_sub, done(b.s))
                act.wait_ge(s_exT, reuse(b.s))
                act.wait_ge(d_sum, reuse(b.s))
                act.activation(ex[:, b.u, :], sm[:, b.u, :], ACT.Exp).then_inc(a_ex, 1)

            def turn(b):
                act.wait_ge(s_exT, done(b.s))
                act.wait_ge(s_o, reuse(b.s))
                act.copy(exT[:, b.u, :], ps_t[b.u][:, 0:P]).then_inc(a_exT, 1)

            def out(b):
                act.wait_ge(s_oT, done(b.s))
                act.copy(AT[:, :, :, bass.ds(4 * b.s, 4)].rearrange("p j s b -> p b j s"),
                         ps_u[b.u][:, 0:P].rearrange("p (b j s) -> p b j s", b=4, j=QJ)).then_inc(a_oT, 1)

            pipeline(act, [(queries, 2), (exponent, 1), (turn, 0), (out, -2)], GROUPS)

        @block.gpsimd
        def _(pool):
            pool.sem_inc(g_k, CREDIT)

            def keys(b):
                pool.wait_ge(s_sc, reuse(b.s))
                pool.tensor_tensor(Ks[:, b.u, :, :, :],
                                   K[:, bass.ds(4 * b.s, 4), :].unsqueeze(2).to_broadcast([P, 4, G, T]),
                                   keep.kmask.unsqueeze(1).unsqueeze(3).to_broadcast([P, 4, G, T]),
                                   ALU.mult).then_inc(g_k, 1)

            pipeline(pool, [(keys, 2)], GROUPS)

        @block.vector
        def _(dve):
            for x in dve_sems:
                dve.sem_inc(x, CREDIT)

            by_group = lambda ap: ap.rearrange("p (g t) -> p g t", g=G)

            def mask(b):
                dve.wait_ge(s_sc, done(b.s))
                dve.wait_ge(a_ex, reuse(b.s))
                dve.scalar_tensor_tensor(out=sm[:, b.u, :], in0=ps_s[b.u][:, 0:P], scalar=1.0 / HD ** 0.5,
                                         in1=keep.view("causal"), op0=ALU.mult, op1=ALU.add).then_inc(d_m, 1)

            def maxima(b):
                dve.wait_ge(d_m, done(b.s))
                dve.tensor_reduce(top[:, b.u, :], by_group(sm[:, b.u, :]), AX.X, ALU.max).then_inc(d_top, 1)

            def subtract(b):
                dve.wait_ge(d_top, done(b.s))
                dve.tensor_tensor(by_group(sm[:, b.u, :]), by_group(sm[:, b.u, :]),
                                  top[:, b.u, :].unsqueeze(2).to_broadcast([P, G, T]),
                                  ALU.subtract).then_inc(d_sub, 1)

            def values(b):
                if not b.looped and b.s == 0:
                    dve.wait_ge(vx, 16 * G)
                dve.wait_ge(s_o, reuse(b.s))
                dve.tensor_copy(Vs[:, b.u, :, :], VX[:, bass.ds(4 * b.s, 4), :]).then_inc(d_v, 1)

            def sums(b):
                dve.wait_ge(a_ex, done(b.s))
                dve.tensor_reduce(den[:, b.u, :], by_group(ex[:, b.u, :]), AX.X, ALU.add).then_inc(d_sum, 1)

            def invert(b):
                dve.wait_ge(d_sum, done(b.s))
                dve.reciprocal(rden[:, b.u, :], den[:, b.u, :]).then_inc(d_den, 1)

            def divide(b):
                dve.wait_ge(s_o, done(b.s))
                dve.wait_ge(d_den, done(b.s))
                dve.wait_ge(s_oT, reuse(b.s))
                dve.tensor_tensor(by_group(o[:, b.u, :]), by_group(ps_o[b.u][:, 0:P]),
                                  rden[:, b.u, :].unsqueeze(2).to_broadcast([P, G, HD]),
                                  ALU.mult).then_inc(d_o, 1)

            pipeline(dve, [(mask, 1), (sums, 0), (maxima, 1), (invert, 0), (subtract, 1), (divide, -1),
                           (values, 0)], GROUPS)

        @block.tensor
        def _(pe):
            for x in pe_sems:
                pe.sem_inc(x, CREDIT)

            def scores(b):
                pe.wait_ge(a_q, done(b.s))
                pe.wait_ge(g_k, done(b.s))
                pe.wait_ge(d_m, reuse(b.s))
                for r in range(4):
                    mm = pe.matmul(ps_s[b.u][32 * r:32 * r + 32, 0:P], Qs[:, b.u, 32 * r:32 * r + 32],
                                   Ks[:, b.u, r, :, :], start=True, stop=True)
                mm.then_inc(s_sc, 1)

            def turn(b):
                pe.wait_ge(a_ex, done(b.s))
                pe.wait_ge(a_exT, reuse(b.s))
                pe.transpose(ps_t[b.u][:, 0:P], ex[:, b.u, :], keep.ident).then_inc(s_exT, 1)

            def attend(b):
                pe.wait_ge(a_exT, done(b.s))
                pe.wait_ge(d_v, done(b.s))
                pe.wait_ge(d_o, reuse(b.s))
                for r in range(4):
                    mm = pe.matmul(ps_o[b.u][32 * r:32 * r + 32, 0:P], exT[:, b.u, 32 * r:32 * r + 32],
                                   Vs[:, b.u, r, :], start=True, stop=True)
                mm.then_inc(s_o, 1)

            def turn_out(b):
                pe.wait_ge(d_o, done(b.s))
                pe.wait_ge(a_oT, reuse(b.s))
                pe.transpose(ps_u[b.u][:, 0:P], o[:, b.u, :], keep.ident).then_inc(s_oT, 1)

            pipeline(pe, [(scores, 1), (turn, 0), (attend, -1), (turn_out, -2)], GROUPS)


def project_and_score(nc, io, keep):
    with ExitStack() as ctx:
        sb = lambda name, shape, dt=F32: ctx.enter_context(nc.sbuf_tensor(name, shape, dt))
        own = ctx.enter_context(semaphores(nc))
        sem = lambda name: own(name)
        both = lambda name: [ctx.enter_context(nc.psum_tensor(f"{name}{k}", [P, 512], F32)) for k in range(2)]
        X, Y1, Z, AT, half = keep.X, keep.Y1, keep.Z, keep.AT, keep.half
        projT = keep.projT
        at = sb("at", [P, 2, QJ, B])
        h = sb("h", [P, 2, D])
        st = sb("st_c", [P, 2, 6])
        mv = sb("mv_c", [P, 2, 2])
        ve = sb("ve_c", [P, 2])
        rs = sb("rs_c", [P, 2])
        z = sb("z_c", [P, 2, D])
        zT = sb("zT_c", [P, 2, DC, B])
        ps_h, ps_t, ps_l = both("psc_h"), both("psc_t"), both("psc_l")
        s_h, s_zT, s_l = pe_sems = [sem(n) for n in ("c_h", "c_zT", "c_l")]
        a_at, a_zT, a_z = act_sems = [sem(n) for n in ("c_at", "c_zTs", "c_zcopy")]
        d_h, d_st, d_mv, d_z, d_l = dve_sems = [
            sem(n) for n in ("c_hs", "c_st", "c_mv", "c_z", "c_logits")]
        g_x, g_ve, g_rs = pool_sems = [sem(n) for n in ("c_x", "c_ve", "c_rs")]
        passed = sem("passed_c")
        router = keep.view("router").rearrange("p (c e) -> p c e", c=DC)
        block = ctx.enter_context(nc.Block())

        @block.scalar
        def _(act):
            for x in act_sems:
                act.sem_inc(x, CREDIT)

            def take(b):
                act.wait_ge(s_h, reuse(b.s))
                act.copy(at[:, b.u, :, :], AT[:, :, b.s, :]).then_inc(a_at, 1)

            def turned(b):
                act.wait_ge(s_zT, done(b.s))
                act.wait_ge(s_l, reuse(b.s))
                for c in range(DC):
                    last = act.activation(zT[:, b.u, c, :], ps_t[b.u][:, c * B:(c + 1) * B], ACT.Identity,
                                          bias=keep.col("ln2b", c), scale=keep.col("ln2w", c))
                last.then_inc(a_zT, 1)

            def store(b):
                act.wait_ge(d_z, done(b.s))
                act.copy(Z[0:B, b.s, :], z[0:B, b.u, :]).then_inc(a_z, 1)

            pipeline(act, [(take, 4), (turned, 0), (store, 0)])

        @block.gpsimd
        def _(pool):
            for x in pool_sems:
                pool.sem_inc(x, CREDIT)

            def norm(b):
                pool.wait_ge(d_mv, done(b.s))
                pool.wait_ge(d_z, reuse(b.s))
                pool.tensor_tensor(ve[0:B, b.u:b.u + 1], mv[0:B, b.u, 1:2], keep.view("eps")[0:B, :],
                                   ALU.add).then_inc(g_ve, 1)
                pool.wait_ge(g_ve, done(b.s))
                pool.tensor_tensor(rs[0:B, b.u:b.u + 1], ve[0:B, b.u:b.u + 1], half[0:B, 0:1],
                                   ALU.pow).then_inc(g_rs, 1)

            def add(b):
                pool.wait_ge(d_h, done(b.s))
                pool.tensor_tensor(X[0:B, b.s, :], X[0:B, b.s, :], h[0:B, b.u, :], ALU.add).then_inc(g_x, 1)

            pipeline(pool, [(norm, 2), (add, 2)])

        @block.vector
        def _(dve):
            for x in dve_sems:
                dve.sem_inc(x, CREDIT)

            def hidden(b):
                dve.wait_ge(s_h, done(b.s))
                dve.wait_ge(g_x, reuse(b.s))
                dve.tensor_tensor(h[0:B, b.u, :], ps_h[b.u][0:B, 0:D], Y1[0:B, b.s, :], ALU.add).then_inc(d_h, 1)

            def stats(b):
                dve.wait_ge(d_h, done(b.s))
                carry(dve, passed)
                dve.bn_stats(st[0:B, b.u, :], h[0:B, b.u, :]).then_inc(d_st, 1)

            def aggregate(b):
                dve.wait_ge(d_st, done(b.s))
                dve.wait_ge(g_ve, reuse(b.s))
                carry(dve, passed)
                dve.bn_aggr(mv[0:B, b.u, :], st[0:B, b.u, :]).then_inc(d_mv, 1)

            def norm(b):
                dve.wait_ge(g_rs, done(b.s))
                dve.wait_ge(a_z, reuse(b.s))
                dve.wait_ge(s_zT, reuse(b.s))
                dve.tensor_scalar(z[0:B, b.u, :], h[0:B, b.u, :], mv[0:B, b.u, 0:1], rs[0:B, b.u:b.u + 1],
                                  ALU.subtract, ALU.mult).then_inc(d_z, 1)

            def take_logits(b):
                dve.wait_ge(s_l, done(b.s))
                dve.tensor_copy(keep.LG[0:B, b.s, :], ps_l[b.u][0:B, 0:E0]).then_inc(d_l, 1)

            pipeline(dve, [(hidden, 2), (norm, 1), (stats, 2), (take_logits, -2), (aggregate, 2)])

        @block.tensor
        def _(pe):
            for x in pe_sems:
                pe.sem_inc(x, CREDIT)
            pe.wait_ge(keep.ld_proj, 16)

            def project(b):
                pe.wait_ge(a_at, done(b.s))
                pe.wait_ge(d_h, reuse(b.s))
                for j in range(QJ):
                    mm = pe.matmul(ps_h[b.u][0:B, 0:D], at[:, b.u, j, :], projT[:, j, :],
                                   start=(j == 0), stop=(j == QJ - 1))
                mm.then_inc(s_h, 1)

            def turn(b):
                pe.wait_ge(d_z, done(b.s))
                pe.wait_ge(a_zT, reuse(b.s))
                for c in range(DC):
                    mm = pe.transpose(ps_t[b.u][:, c * B:(c + 1) * B], z[0:B, b.u, c * P:(c + 1) * P],
                                      keep.ident[0:B, 0:B])
                mm.then_inc(s_zT, 1)

            def logits(b):
                pe.wait_ge(a_zT, done(b.s))
                pe.wait_ge(d_l, reuse(b.s))
                for c in range(DC):
                    mm = pe.matmul(ps_l[b.u][0:B, 0:E0], zT[:, b.u, c, :], router[:, c, :],
                                   start=(c == 0), stop=(c == DC - 1))
                mm.then_inc(s_l, 1)

            pipeline(pe, [(project, 3), (turn, 0), (logits, -1)])


def route(nc, io, keep, second):
    name = "r1" if second else "r0"
    with ExitStack() as ctx:
        sb = lambda n, shape, dt=F32: ctx.enter_context(nc.sbuf_tensor(f"{name}_{n}", shape, dt))
        own = ctx.enter_context(semaphores(nc))
        sem = lambda n: own(f"{name}_{n}")
        E = G
        diff, ex, den, rden = sb("diff", [P, S, E]), sb("ex", [P, S, E]), sb("den", [P, S]), sb("rden", [P, S])
        idx = sb("idx", [P, 2, S])
        hot = sb("hot", [P, 2, S, E])
        taken = sb("taken", [P, S, E])
        PAD, PADE = S // 2, E // 2
        run = [sb("run0", [P, PAD + S, E]), sb("run1", [P, PAD + S, E])]
        rank = sb("rank", [P, S, E])
        mine = sb("mine", [P, 2, S, E])
        slot = sb("slot", [P, 2, S])
        kept = sb("kept", [P, 2, S])
        gone = sb("gone", [P, 2, S])
        full = sb("full", [P, E, 5])
        upto = [sb("upto0", [P, PADE + E]), sb("upto1", [P, PADE + E])]
        base = sb("base", [P, E])
        below = sb("below", [P, TILES1, E])
        te = sb("te", [P, TILES1])
        ones = sb("ones", [P, P])
        ps = ctx.enter_context(nc.psum_tensor(f"{name}_ps", [P, 512], F32))
        d_step, a_ex, s_counts, g_ones = sem("step"), sem("ex"), sem("counts"), sem("ones")
        if not second:
            wqk = sb("wqk", [P, DC, 2 * D])
            ps_A = [ctx.enter_context(nc.psum_tensor(f"ps_A{c}", [P, 512], F32)) for c in range(DC)]
            ld_w, folded, a_fold = sem("ld_w"), sem("folded"), sem("fold")
        LG, V8, I8, W2, scat, gath = keep.LG, keep.V8, keep.I8, keep.W2, keep.scat, keep.gath
        by8 = lambda ap, n: ap.unsqueeze(len(ap.shape)).to_broadcast(n)
        block = ctx.enter_context(nc.Block())
        steps = {}

        @block.gpsimd
        def _(pool):
            pool.memset(ones[:, :], 1.0).then_inc(g_ones, 1)
            for k in range(2):
                pool.memset(run[k][:, 0:PAD, :], 0.0).then_inc(g_ones, 1)
                pool.memset(upto[k][:, 0:PADE], 0.0).then_inc(g_ones, 1)

        @block.vector
        def _(dve):
            count = [0]

            def link(ins, label=None):
                count[0] += 1
                ins.then_inc(d_step, 1)
                dve.wait_ge(d_step, count[0])
                if label:
                    steps[label] = count[0]

            A = slice(0, B)
            for s in range(S):
                top = dve.max(keep.V8[A, s, :], keep.LG[A, s, :])
            link(top)
            for s in range(S):
                whose = dve.max_index(keep.I8[A, s, :], keep.V8[A, s, :], keep.LG[A, s, :])
            link(whose)
            link(dve.tensor_tensor(diff[A], V8[A, :, :], by8(V8[A, :, 0], [B, S, E]), ALU.subtract), "diff")
            link(dve.tensor_copy(idx[A], I8[A, :, 0:2].rearrange("p s j -> p j s")))
            for j in range(2):
                link(dve.tensor_tensor(hot[A, j], by8(idx[A, j, :], [B, S, E]),
                                       keep.view("iota8")[A].unsqueeze(1).to_broadcast([B, S, E]), ALU.is_equal))
            link(dve.tensor_tensor(taken[A], hot[A, 0], hot[A, 1], ALU.add), "taken")
            dve.wait_ge(a_ex, 1)
            link(dve.tensor_reduce(den[A], ex[A] if second else ex[A, :, 0:2], AX.X, ALU.add))
            link(dve.reciprocal(rden[A], den[A]))
            link(dve.tensor_tensor(W2[A], ex[A, :, 0:2].rearrange("p s j -> p j s"),
                                   rden[A].unsqueeze(1).to_broadcast([B, 2, S]), ALU.mult))
            dve.wait_ge(s_counts, 1)
            dve.wait_ge(g_ones, 5)
            link(dve.tensor_copy(run[0][A, PAD:PAD + S, :], ps[A, P:2 * P].rearrange("p (s e) -> p s e", e=E)))
            at, step = 0, 1
            while step < S:
                link(dve.tensor_tensor(run[1 - at][A, PAD:PAD + S, :], run[at][A, PAD:PAD + S, :],
                                       run[at][A, PAD - step:PAD + S - step, :], ALU.add))
                at, step = 1 - at, 2 * step
            link(dve.tensor_tensor(rank[A], run[at][A, PAD - 1:PAD + S - 1, :],
                                   ps[A, 0:P].rearrange("p (s e) -> p s e", e=E), ALU.add))
            if second:
                link(dve.tensor_tensor(full[A], by8(run[at][A, PAD + S - 1, :], [B, E, 5]),
                                       keep.view("thresholds")[A].unsqueeze(1).to_broadcast([B, E, 5]), ALU.is_gt))
                link(dve.tensor_reduce(upto[0][A, PADE:PADE + E], full[A], AX.X, ALU.add))
                au, step = 0, 1
                while step < E:
                    link(dve.tensor_tensor(upto[1 - au][A, PADE:PADE + E], upto[au][A, PADE:PADE + E],
                                           upto[au][A, PADE - step:PADE + E - step], ALU.add))
                    au, step = 1 - au, 2 * step
                link(dve.tensor_scalar(base[A], upto[au][A, PADE - 1:PADE + E - 1], float(TILE1), None, ALU.mult))
                link(dve.tensor_tensor(rank[A], rank[A], base[A].unsqueeze(1).to_broadcast([B, S, E]), ALU.add))
                link(dve.tensor_tensor(below[A], upto[au][A, PADE:PADE + E].unsqueeze(1).to_broadcast([B, TILES1, E]),
                                       by8(keep.view("fills")[A, 0:TILES1], [B, TILES1, E]), ALU.is_le))
                link(dve.tensor_reduce(te[A], below[A], AX.X, ALU.add))
                link(dve.tensor_scalar(keep.tile_expert[A], te[A], float(E1 - 1), None, ALU.min))
            for j in range(2):
                link(dve.tensor_tensor(mine[A, j], hot[A, j], rank[A], ALU.mult))
                link(dve.tensor_reduce(slot[A, j], mine[A, j], AX.X, ALU.add))
            if second:
                link(dve.tensor_copy(scat[A], slot[A]))
                link(dve.tensor_copy(gath[A], slot[A]))
            else:
                link(dve.tensor_scalar(kept[A], slot[A], float(CAP), None, ALU.is_lt))
                link(dve.tensor_scalar(gone[A], kept[A], -1.0e5, 1.0e5, ALU.mult, ALU.add))
                link(dve.scalar_tensor_tensor(out=slot[A], in0=idx[A], scalar=float(CAP), in1=slot[A],
                                              op0=ALU.mult, op1=ALU.add))
                link(dve.tensor_tensor(scat[A], slot[A], gone[A], ALU.add))
                link(dve.tensor_tensor(gath[A], slot[A], kept[A], ALU.mult))
                link(dve.tensor_tensor(W2[A], W2[A], kept[A], ALU.mult))

        @block.sync
        def _(sp):
            if not second:
                sp.dma_start(wqk[:, :, :], io.w_e[:, :, 0:2 * D]).then_inc(ld_w, 16)
                sp.dma_start(keep.wvT[:, :, :], io.w_e[:, :, 2 * D:3 * D]).then_inc(ld_w, 16)

        @block.scalar
        def _(act):
            act.wait_ge(d_step, steps["diff"])
            act.activation(ex[0:B], diff[0:B], ACT.Exp).then_inc(a_ex, 1)
            if not second:
                act.wait_ge(folded, 1)
                for c in range(DC):
                    act.copy(keep.A[:, c, :], ps_A[c][:, 0:D]).then_inc(a_fold, 1)

        @block.tensor
        def _(pe):
            pe.wait_ge(g_ones, 1)
            pe.wait_ge(d_step, steps["taken"])
            flat = taken[0:B].rearrange("p s e -> p (s e)")
            pe.matmul(ps[0:B, 0:P], keep.view("before")[0:B, 0:B], flat, start=True, stop=True)
            pe.matmul(ps[0:B, P:2 * P], ones[0:B, 0:B], flat, start=True, stop=True).then_inc(s_counts, 1)
            if not second:
                pe.wait_ge(ld_w, 32)
                for c in range(DC):
                    for o in range(DC):
                        mm = pe.matmul(ps_A[c][:, 0:D], wqk[:, o, c * P:(c + 1) * P], wqk[:, o, D:2 * D],
                                       start=(o == 0), stop=(o == DC - 1))
                mm.then_inc(folded, 1)


def expert_tiles(nc, io, keep, second):
    name = "f1" if second else "f0"
    with ExitStack() as ctx:
        sb = lambda n, shape, dt=F32: ctx.enter_context(nc.sbuf_tensor(f"{name}_{n}", shape, dt))
        own = ctx.enter_context(semaphores(nc))
        sem = lambda n: own(f"{name}_{n}")
        psum = lambda n, w=512: ctx.enter_context(nc.psum_tensor(f"{name}_{n}", [P, w], F32))
        R, SUB, TILES = (ROWS1, SUB1, TILES1) if second else (ROWS0, SUB0, E0)
        N = R * SUB
        slots, outs = (keep.slots1, keep.outs1) if second else (keep.slots0, keep.outs0)
        weights = io.w_f1 if second else io.w_f0
        W1 = DC * FFN
        WALL = W1 + FC * D
        PIECE = WALL // FC
        RING = 4

        raw = sb("raw", [P, 2, WALL])
        w_hi, w_lo = sb("w_hi", [P, 2, WALL], F32R), sb("w_lo", [P, 2, WALL], F32R)
        xs = sb("xs", [P, 2, SUB, D])
        xT = sb("xT", [P, DC, N])
        x_hi, x_lo = sb("x_hi", [P, 2, DC, N], F32R), sb("x_lo", [P, 2, DC, N], F32R)
        g = sb("g", [P, 2, N])
        h_hi, h_lo = sb("h_hi", [P, RING, N], F32R), sb("h_lo", [P, RING, N], F32R)
        ys = sb("ys", [P, 2, SUB, D])
        b1, b2 = sb("b1", [P, 2, FC]), sb("b2", [P, 2, D])
        ps_x = psum("ps_x", 1024)
        ps_h = [psum("ps_h0"), psum("ps_h1")]
        ps_y = [psum("ps_y0", 1024), psum("ps_y1", 1024)]

        scattered, passed = sem("scattered"), sem("passed")
        ld_w, ld_x, ld_b, st_y = ([sem(f"{n}{k}") for k in range(2)] for n in ("ld_w", "ld_x", "ld_b", "st_y"))
        s_xT, s_h, s_y = pe_sems = [sem(n) for n in ("xT_ps", "h_ps", "y_ps")]
        a_xT, a_g, a_w = act_sems = [sem(n) for n in ("xT", "gelu", "w_hi_r")]
        d_xh, d_x, d_hh, d_h, d_y = dve_sems = [sem(n) for n in ("x_hi_r", "x_r", "h_hi_r", "h_r", "ys_r")]
        g_w, d_w = sem("w_lo_r"), sem("w_lo_first")
        block = ctx.enter_context(nc.Block())

        def upto(b, f):
            return FC * b.s + f + 1 + 2 * FC

        def piece(k):
            at = [0, 2, 1, 3, 4, 5, 6, 7][k]
            return slice(at * PIECE, (at + 1) * PIECE)

        TWO_BEFORE = -FC - 1

        @block.sync
        def _(sp):
            for x in st_y:
                sp.sem_inc(x, 16)

            def expert(b):
                if not second:
                    return b.s
                carry(sp, passed)
                at = bass.ds(b.s, 1) if b.looped else slice(b.s, b.s + 1)
                return sp.value_load(keep.tile_expert[0:1, at], min_val=0, max_val=E1 - 1)

            def load_w(b):
                sp.wait_ge(g_w, upto(b, TWO_BEFORE))
                sp.dma_start(raw[:, b.u, :], weights[expert(b)]).then_inc(ld_w[b.u], 16)

            def biases(b):
                sp.wait_ge(a_g, upto(b, TWO_BEFORE))
                sp.wait_ge(d_y, reuse(b.s))
                e = expert(b)
                sp.dma_start(b1[:, b.u, :], io.be1[e]).then_inc(ld_b[b.u], 16)
                sp.dma_start(b2[:, b.u, :], io.be2[e].to_broadcast([P, D])).then_inc(ld_b[b.u], 16)

            def load_x(b):
                sp.wait_ge(scattered, 16 * 2 * S)
                sp.wait_ge(s_xT, reuse(b.s))
                sp.dma_start(xs[0:R, b.u, :, :],
                             slots.rearrange("(t m r) d -> t r m d", m=SUB, r=R)[b.s]).then_inc(ld_x[b.u], 16)

            def store(b):
                sp.wait_ge(d_y, done(b.s))
                sp.dma_start(outs.rearrange("(t m r) d -> t r m d", m=SUB, r=R)[b.s],
                             ys[0:R, b.u, :, :]).then_inc(st_y[b.u], 16)

            def load_b(b):
                if b.looped or b.s > 0:
                    biases(b)

            if second:
                biases(Batch(0))
            pipeline(sp, [(load_w, 2), (load_x, 2), (store, -1)] + ([(load_b, 1)] if second else []), TILES)
            for x in st_y:
                sp.wait_ge(x, 16 * (TILES // 2) + 16)

        @block.gpsimd
        def _(pool):
            pool.sem_inc(g_w, 2 * FC)
            for j in range(2):
                for s in range(S):
                    pool.indirect_dma_start(
                        slots, bass.IndirectOffsetOnAxis(ap=keep.scat[0:B, j, s:s + 1], axis=0),
                        keep.Z[0:B, s, :], None, bounds_check=slots.shape[0] - 1,
                        oob_is_err=False).then_inc(scattered, 16)

            def low(b):
                if not b.looped and b.s == 0:
                    for k in range(FC):
                        pool.wait_ge(d_w, k + 1)
                        pool.sem_inc(g_w, 1)
                    return
                pool.wait_ge(ld_w[b.u], b.loaded)
                pool.wait_ge(s_y, upto(b, TWO_BEFORE))
                for k in range(FC):
                    c = piece(k)
                    pool.wait_ge(a_w, upto(b, k))
                    pool.tensor_tensor(w_lo[:, b.u, c], raw[:, b.u, c], w_hi[:, b.u, c].bitcast(F32),
                                       ALU.subtract).then_inc(g_w, 1)

            pipeline(pool, [(low, 1)], TILES)

        @block.scalar
        def _(act):
            act.sem_inc(a_xT, CREDIT)
            act.sem_inc(a_g, 2 * FC)
            act.sem_inc(a_w, 2 * FC)

            act.wait_ge(ld_w[0], 16)
            for k in range(FC):
                act.copy(w_hi[:, 0, piece(k)], raw[:, 0, piece(k)]).then_inc(a_w, 1)

            def high(k):
                def stage(b):
                    if not b.looped and b.s == 0:
                        return
                    if k == 0:
                        act.wait_ge(ld_w[b.u], b.loaded)
                        act.wait_ge(s_y, upto(b, TWO_BEFORE))
                        act.wait_ge(g_w, upto(b, TWO_BEFORE))
                    c = piece(k)
                    act.copy(w_hi[:, b.u, c], raw[:, b.u, c]).then_inc(a_w, 1)
                return stage

            def turned(b):
                act.wait_ge(s_xT, done(b.s))
                act.wait_ge(d_x, done(b.s - 1))
                for c in range(DC):
                    src = ps_x[:, 512 * c:512 * c + N]
                    if second:
                        last = act.copy(xT[:, c, :], src)
                    else:
                        last = act.activation(xT[:, c, :], src, ACT.Identity, bias=keep.col("ln2b", c),
                                              scale=keep.col("ln2w", c))
                last.then_inc(a_xT, 1)

            def gelu(f):
                def stage(b):
                    if second and f == 0:
                        act.wait_ge(ld_b[b.u], 2 * b.loaded)
                    act.wait_ge(s_h, upto(b, f))
                    act.wait_ge(d_h, upto(b, f - 2))
                    act.activation(g[:, f % 2, :], ps_h[f % 2][:, 0:N], ACT.Gelu,
                                   bias=b1[:, b.u, f:f + 1] if second else 0.0).then_inc(a_g, 1)
                return stage

            stages = []
            for f, ks in enumerate([[], [], [0], [1], [2, 3], [4], [5], [6, 7]]):
                stages += [(gelu(f), 0)] + [(high(k), 1) for k in ks] + ([(turned, 1)] if f == 5 else [])
            pipeline(act, stages, TILES)

        @block.vector
        def _(dve):
            for x in (d_xh, d_x, d_y):
                dve.sem_inc(x, CREDIT)
            dve.sem_inc(d_hh, 2 * FC)
            dve.sem_inc(d_h, 2 * FC)

            for k in range(FC):
                dve.wait_ge(a_w, upto(Batch(0), k))
                dve.tensor_tensor(w_lo[:, 0, piece(k)], raw[:, 0, piece(k)], w_hi[:, 0, piece(k)].bitcast(F32),
                                  ALU.subtract).then_inc(d_w, 1)

            def split_x(b):
                dve.wait_ge(a_xT, done(b.s))
                dve.wait_ge(s_h, upto(b, TWO_BEFORE))
                dve.tensor_copy(x_hi[:, b.u, :, :], xT[:, :, :]).then_inc(d_xh, 1)
                dve.wait_ge(d_xh, done(b.s))
                dve.tensor_tensor(x_lo[:, b.u, :, :], xT[:, :, :], x_hi[:, b.u, :, :].bitcast(F32),
                                  ALU.subtract).then_inc(d_x, 1)

            def split_h(f):
                def stage(b):
                    dve.wait_ge(a_g, upto(b, f))
                    dve.wait_ge(s_y, upto(b, f - RING))
                    dve.tensor_copy(h_hi[:, f % RING, :], g[:, f % 2, :]).then_inc(d_hh, 1)
                    dve.wait_ge(d_hh, upto(b, f))
                    dve.tensor_tensor(h_lo[:, f % RING, :], g[:, f % 2, :], h_hi[:, f % RING, :].bitcast(F32),
                                      ALU.subtract).then_inc(d_h, 1)
                return stage

            def out(b):
                dve.wait_ge(s_y, upto(b, FC - 1))
                dve.wait_ge(st_y[b.u], b.loaded)
                src = ps_y[b.u][0:R, 0:SUB * D].rearrange("p (m d) -> p m d", d=D)
                if second:
                    dve.wait_ge(ld_b[b.u], 2 * b.loaded)
                    dve.tensor_tensor(ys[0:R, b.u, :, :], src, b2[0:R, b.u, :].unsqueeze(1).to_broadcast([R, SUB, D]),
                                      ALU.add).then_inc(d_y, 1)
                else:
                    dve.tensor_copy(ys[0:R, b.u, :, :], src).then_inc(d_y, 1)

            stages = []
            for f in range(FC):
                stages += [(split_h(f), 0)] + ([(out, -1)] if f == 2 else []) + ([(split_x, 1)] if f == 5 else [])
            pipeline(dve, stages, TILES)

        @block.tensor
        def _(pe):
            pe.sem_inc(s_xT, CREDIT)
            pe.sem_inc(s_h, 2 * FC)
            pe.sem_inc(s_y, 2 * FC)

            def turn(b):
                pe.wait_ge(ld_x[b.u], b.loaded)
                pe.wait_ge(a_xT, done(b.s - 1))
                for m in range(SUB):
                    for c in range(DC):
                        at = 512 * c + m * R
                        mm = pe.transpose(ps_x[:, at:at + R], xs[0:R, b.u, m, c * P:(c + 1) * P],
                                          keep.ident[0:R, 0:R])
                mm.then_inc(s_xT, 1)

            def passes(hi_lo_left, hi_lo_right):
                (lh, ll), (rh, rl) = hi_lo_left, hi_lo_right
                return [(lh, rh), (lh, rl), (ll, rh)]

            def hidden(f):
                def stage(b):
                    if f == 0:
                        pe.wait_ge(d_x, done(b.s))
                    if f in (0, FC // 2):
                        pe.wait_ge(g_w, upto(b, 1 if f == 0 else 3))
                    pe.wait_ge(a_g, upto(b, f - 2))
                    todo = []
                    for c in range(DC):
                        w = slice(c * FFN + f * P, c * FFN + (f + 1) * P)
                        todo += passes((w_hi[:, b.u, w], w_lo[:, b.u, w]), (x_hi[:, b.u, c, :], x_lo[:, b.u, c, :]))
                    for k, (l, r) in enumerate(todo):
                        mm = pe.matmul(ps_h[f % 2][:, 0:N], l, r, start=(k == 0), stop=(k == len(todo) - 1))
                    mm.then_inc(s_h, 1)
                return stage

            def output(f):
                def stage(b):
                    if f == 0:
                        pe.wait_ge(d_y, reuse(b.s))
                    if f % 2 == 0:
                        pe.wait_ge(g_w, upto(b, 4 + f // 2))
                    pe.wait_ge(d_h, upto(b, f))
                    w = slice(W1 + f * D, W1 + (f + 1) * D)
                    for m in range(SUB):
                        t = slice(m * R, (m + 1) * R)
                        todo = passes((h_hi[:, f % RING, t], h_lo[:, f % RING, t]),
                                      (w_hi[:, b.u, w], w_lo[:, b.u, w]))
                        for k, (l, r) in enumerate(todo):
                            mm = pe.matmul(ps_y[b.u][0:R, m * D:(m + 1) * D], l, r,
                                           start=(f == 0 and k == 0 and m % 2 == 0),
                                           stop=(f == FC - 1 and k == 2), skip_group_check=True)
                    mm.then_inc(s_y, 1)
                return stage

            LAG = 2
            stages = []
            for f in range(FC):
                back = f - LAG
                stages += [(hidden(f), 0), (output(back % FC), 0 if back >= 0 else -1)]
                if f == 4:
                    stages += [(turn, 1)]
            pipeline(pe, stages, TILES)


def gather(pool, keep, outs, at_sb, copied, passed, g, b, landed):
    at = bass.ds(b.s, 1) if b.looped else slice(b.s, b.s + 1)
    pool.tensor_copy(at_sb[0:B, b.u, :].unsqueeze(2), keep.gath[0:B, :, at]).then_inc(copied, 1)
    pool.wait_ge(copied, done(b.s))
    carry(pool, passed)
    for j in range(2):
        pool.indirect_dma_start(
            g[0:B, b.u, j, :], None, outs, bass.IndirectOffsetOnAxis(ap=at_sb[0:B, b.u, j:j + 1], axis=0),
            bounds_check=outs.shape[0] - 1, oob_is_err=True).then_inc(landed[b.u], 16)


def weight(keep, b, j):
    at = bass.ds(b.s, 1) if b.looped else slice(b.s, b.s + 1)
    return keep.W2[0:B, j, at]


def second_cross_attention(nc, io, keep):
    with ExitStack() as ctx:
        sb = lambda name, shape, dt=F32: ctx.enter_context(nc.sbuf_tensor("e_" + name, shape, dt))
        own = ctx.enter_context(semaphores(nc))
        sem = lambda name: own("e_" + name)
        psum = lambda name: ctx.enter_context(nc.psum_tensor("e_" + name, [P, 512], F32))
        X, Z, Y3T, half = keep.X, keep.Z, keep.Y3T, keep.half
        FILL = -99999.0

        A, wvT = keep.A, keep.wvT
        got = sb("got", [P, 2, 2, D])
        at = sb("at", [P, 2, 2], I32)
        ctxT = sb("ctxT", [P, 2, DC, CTX])
        ctxN = sb("ctxN", [P, 2, 3, D])
        mask = sb("mask", [P, 2, CTX], I32)
        sm = sb("sm", [P, 2, CTX])
        part = sb("part", [P, D])
        st = sb("st", [P, 2, 2, 6])
        mv = sb("mv", [P, 2, 2, 2])
        ve = sb("ve", [P, 2, 2])
        rs = sb("rs", [P, 2, 2])
        y = sb("y", [P, 2, D])
        z = sb("z", [P, 2, D])
        yT = sb("yT", [P, 2, DC, B])
        qT = sb("qT", [P, 2, DC, B])
        top = sb("top", [P, 2])
        nmax = sb("nmax", [P, 2])
        ex = sb("ex", [P, 2, CTX])
        sums = sb("sums", [P, 2])
        inv = sb("inv", [P, 2])
        exT = sb("exT", [P, 2, 3, B])
        avT = sb("avT", [P, 2, DC, B])
        ps_q, ps_p, ps_o, ps_z = (psum(n) for n in ("ps_q", "ps_p", "ps_o", "ps_z"))
        ps_yT, ps_av = ps_q[:, 256:256 + DC * B], ps_p[:, 3 * B:(3 + DC) * B]
        ps_s = [psum("ps_s0"), psum("ps_s1")]

        ld_ct, ld_cn, ld_m, ld_got = ([sem(f"{n}{k}") for k in range(2)] for n in ("ld_ct", "ld_cn", "ld_m", "ld_got"))
        passed, pool_passed = sem("passed"), sem("pool_passed")
        s_yT, s_q, s_sc, s_exT, s_av, s_out, s_zT = pe_sems = [
            sem(n) for n in ("yT_ps", "q_ps", "sc_ps", "exT_ps", "av_ps", "out_ps", "zT_ps")]
        a_yT, a_q, a_ex, a_exT, a_av, a_zT, a_z = act_sems = [
            sem(n) for n in ("yT_sb", "q_sb", "ex_sb", "exT_sb", "av_sb", "zT_sb", "zcopy")]
        d_part, d_x2, d_st, d_mv, d_sm, d_y, d_top, d_max, d_inv, d_x3, d_st3, d_mv3, d_z = dve_sems = [
            sem(n) for n in ("part_r", "x2_r", "st_r", "mv_r", "sm_r", "y_r", "top_r", "max_r", "inv_r",
                             "x3_r", "st3_r", "mv3_r", "z_r")]
        g_at, g_ve, g_rs, g_fill, g_ve3, g_rs3 = pool_sems = [
            sem(n) for n in ("at_r", "ve_r", "rs_r", "fill_r", "ve3_r", "rs3_r")]
        block = ctx.enter_context(nc.Block())

        @block.sync
        def _(sp):
            sp.dma_start(keep.rW1[:, :, :], io.w_e[:, :, 3 * D:3 * D + RH]).then_inc(keep.ld_rW1, 16)

            def load_T(b):
                sp.wait_ge(s_sc, reuse(b.s))
                sp.dma_start(ctxT[:, b.u, :, :], io.ctxT[b.s]).then_inc(ld_ct[b.u], 16)

            def load_mask(b):
                sp.wait_ge(d_sm, reuse(b.s))
                sp.dma_start(mask[:, b.u, :], io.mask[b.s].to_broadcast([P, CTX])).then_inc(ld_m[b.u], 16)

            def load_N(b):
                sp.wait_ge(s_av, reuse(b.s))
                sp.dma_start(ctxN[:, b.u, 0:2, :],
                             io.ctx[b.s, 0:2 * P, :].rearrange("(c p) d -> p c d", p=P)).then_inc(ld_cn[b.u], 16)
                sp.dma_start(ctxN[0:CK[2], b.u, 2, :], io.ctx[b.s, 2 * P:CTX, :]).then_inc(ld_cn[b.u], 16)

            pipeline(sp, [(load_N, 2), (load_T, 4), (load_mask, 3)])

        @block.gpsimd
        def _(pool):
            for x in pool_sems:
                pool.sem_inc(x, CREDIT)

            def gather_rows(b):
                pool.wait_ge(d_x2, reuse(b.s))
                gather(pool, keep, keep.outs0, at, g_at, pool_passed, got, b, ld_got)

            def rsqrt(k, b, ready, last_reader, plus_eps, power):
                pool.wait_ge(ready, done(b.s))
                pool.wait_ge(last_reader, reuse(b.s))
                pool.tensor_tensor(ve[0:B, b.u, k:k + 1], mv[0:B, b.u, k, 1:2], keep.view("eps")[0:B, :],
                                   ALU.add).then_inc(plus_eps, 1)
                pool.wait_ge(plus_eps, done(b.s))
                pool.tensor_tensor(rs[0:B, b.u, k:k + 1], ve[0:B, b.u, k:k + 1], half[0:B, 0:1],
                                   ALU.pow).then_inc(power, 1)

            def norm_x2(b):
                rsqrt(0, b, d_mv, d_y, g_ve, g_rs)

            def norm_x3(b):
                rsqrt(1, b, d_mv3, d_z, g_ve3, g_rs3)

            def fill(b):
                pool.wait_ge(a_ex, reuse(b.s))
                carry(pool, pool_passed)
                pool.memset(sm[:, b.u, :], FILL).then_inc(g_fill, 1)

            pipeline(pool, [(gather_rows, 5), (norm_x3, -1), (fill, 2), (norm_x2, 4)])

        @block.scalar
        def _(act):
            for x in act_sems:
                act.sem_inc(x, CREDIT)

            def turned_y(b):
                act.wait_ge(s_yT, done(b.s))
                act.copy(yT[:, b.u, :, :], ps_yT).then_inc(a_yT, 1)

            def query(b):
                act.wait_ge(s_q, done(b.s))
                act.copy(qT[:, b.u, :, :], ps_q[:, 0:DC * B]).then_inc(a_q, 1)

            def exponent(b):
                act.wait_ge(d_max, done(b.s))
                act.wait_ge(s_exT, reuse(b.s))
                act.wait_ge(d_inv, reuse(b.s))
                act.activation(ex[0:B, b.u, :], sm[0:B, b.u, :], ACT.Exp, bias=nmax[0:B, b.u:b.u + 1],
                               accum_out=sums[0:B, b.u:b.u + 1]).then_inc(a_ex, 1)

            def turned_ex(b):
                act.wait_ge(s_exT, done(b.s))
                act.copy(exT[:, b.u, 0:2, :], ps_p[:, 0:2 * B])
                act.copy(exT[0:CK[2], b.u, 2, :], ps_p[0:CK[2], 2 * B:3 * B]).then_inc(a_exT, 1)

            def attended(b):
                act.wait_ge(s_av, done(b.s))
                act.copy(avT[:, b.u, :, :], ps_av).then_inc(a_av, 1)

            def turned_z(b):
                act.wait_ge(s_zT, done(b.s))
                at = bass.ds(b.s * B, B) if b.looped else slice(b.s * B, (b.s + 1) * B)
                act.copy(Y3T[:, :, at], ps_z[:, 0:DC * B].rearrange("p (c b) -> p c b", c=DC)).then_inc(a_zT, 1)
                act.copy(Z[0:B, b.s, :], z[0:B, b.u, :]).then_inc(a_z, 1)

            pipeline(act, [(turned_y, 2), (turned_ex, 0), (turned_z, -2), (query, 2), (attended, 0), (exponent, 1)])

        @block.vector
        def _(dve):
            for x in dve_sems:
                dve.sem_inc(x, CREDIT)

            def combine_first(b):
                dve.wait_ge(ld_got[b.u], 2 * b.loaded)
                dve.scalar_tensor_tensor(out=part[0:B, :], in0=got[0:B, b.u, 0, :], scalar=weight(keep, b, 0),
                                         in1=X[0:B, b.s, :], op0=ALU.mult, op1=ALU.add).then_inc(d_part, 1)

            def combine_second(b):
                dve.wait_ge(d_part, done(b.s))
                dve.scalar_tensor_tensor(out=X[0:B, b.s, :], in0=got[0:B, b.u, 1, :], scalar=weight(keep, b, 1),
                                         in1=part[0:B, :], op0=ALU.mult, op1=ALU.add).then_inc(d_x2, 1)

            def stats_x2(b):
                dve.wait_ge(d_x2, done(b.s))
                carry(dve, passed)
                dve.bn_stats(st[0:B, b.u, 0, :], X[0:B, b.s, :]).then_inc(d_st, 1)

            def aggregate_x2(b):
                dve.wait_ge(d_st, done(b.s))
                dve.wait_ge(g_ve, reuse(b.s))
                carry(dve, passed)
                dve.bn_aggr(mv[0:B, b.u, 0, :], st[0:B, b.u, 0, :]).then_inc(d_mv, 1)

            def norm_x2(b):
                dve.wait_ge(g_rs, done(b.s))
                dve.wait_ge(s_yT, reuse(b.s))
                dve.tensor_scalar(y[0:B, b.u, :], X[0:B, b.s, :], mv[0:B, b.u, 0, 0:1], rs[0:B, b.u, 0:1],
                                  ALU.subtract, ALU.mult).then_inc(d_y, 1)

            def masked(b):
                dve.wait_ge(s_sc, done(b.s))
                dve.wait_ge(ld_m[b.u], b.loaded)
                dve.wait_ge(g_fill, done(b.s))
                carry(dve, passed)
                dve.copy_predicated(sm[0:B, b.u, :], mask[0:B, b.u, :], ps_s[b.u][0:B, 0:CTX]).then_inc(d_sm, 1)

            def maximum(b):
                dve.wait_ge(d_sm, done(b.s))
                dve.tensor_reduce(top[0:B, b.u:b.u + 1], sm[0:B, b.u, :], AX.X, ALU.max).then_inc(d_top, 1)

            def negate(b):
                dve.wait_ge(d_top, done(b.s))
                dve.wait_ge(a_ex, reuse(b.s))
                dve.tensor_scalar(nmax[0:B, b.u:b.u + 1], top[0:B, b.u:b.u + 1], -1.0, None,
                                  ALU.mult).then_inc(d_max, 1)

            def invert(b):
                dve.wait_ge(a_ex, done(b.s))
                dve.reciprocal(inv[0:B, b.u:b.u + 1], sums[0:B, b.u:b.u + 1]).then_inc(d_inv, 1)

            def residual(b):
                dve.wait_ge(s_out, done(b.s))
                dve.wait_ge(d_inv, done(b.s))
                dve.scalar_tensor_tensor(out=X[0:B, b.s, :], in0=ps_o[0:B, 0:D], scalar=inv[0:B, b.u:b.u + 1],
                                         in1=X[0:B, b.s, :], op0=ALU.mult, op1=ALU.add).then_inc(d_x3, 1)

            def stats_x3(b):
                dve.wait_ge(d_x3, done(b.s))
                carry(dve, passed)
                dve.bn_stats(st[0:B, b.u, 1, :], X[0:B, b.s, :]).then_inc(d_st3, 1)

            def aggregate_x3(b):
                dve.wait_ge(d_st3, done(b.s))
                dve.wait_ge(g_ve3, reuse(b.s))
                carry(dve, passed)
                dve.bn_aggr(mv[0:B, b.u, 1, :], st[0:B, b.u, 1, :]).then_inc(d_mv3, 1)

            def norm_x3(b):
                dve.wait_ge(g_rs3, done(b.s))
                dve.wait_ge(s_zT, reuse(b.s))
                dve.wait_ge(a_z, reuse(b.s))
                dve.tensor_scalar(z[0:B, b.u, :], X[0:B, b.s, :], mv[0:B, b.u, 1, 0:1], rs[0:B, b.u, 1:2],
                                  ALU.subtract, ALU.mult).then_inc(d_z, 1)

            pipeline(dve, [(invert, -1), (masked, 1), (residual, -1), (maximum, 1), (stats_x3, -1), (negate, 1),
                           (norm_x2, 3), (aggregate_x3, -1), (combine_first, 4), (combine_second, 4),
                           (stats_x2, 4), (norm_x3, -1), (aggregate_x2, 4)])

        @block.tensor
        def _(pe):
            for x in pe_sems:
                pe.sem_inc(x, CREDIT)

            def turn_y(b):
                pe.wait_ge(d_y, done(b.s))
                for c in range(DC):
                    mm = pe.transpose(ps_yT[:, c * B:(c + 1) * B], y[0:B, b.u, c * P:(c + 1) * P],
                                      keep.ident[0:B, 0:B])
                mm.then_inc(s_yT, 1)

            def query(b):
                pe.wait_ge(a_yT, done(b.s))
                for c in range(DC):
                    for k in range(DC):
                        mm = pe.matmul(ps_q[:, c * B:(c + 1) * B], A[:, k, c * P:(c + 1) * P], yT[:, b.u, k, :],
                                       start=(k == 0), stop=(k == DC - 1))
                mm.then_inc(s_q, 1)

            def scores(b):
                pe.wait_ge(a_q, done(b.s))
                pe.wait_ge(ld_ct[b.u], b.loaded)
                pe.wait_ge(d_sm, reuse(b.s))
                for k in range(DC):
                    mm = pe.matmul(ps_s[b.u][0:B, 0:CTX], qT[:, b.u, k, :], ctxT[:, b.u, k, :],
                                   start=(k == 0), stop=(k == DC - 1))
                mm.then_inc(s_sc, 1)

            def turn_ex(b):
                pe.wait_ge(a_ex, done(b.s))
                for k in range(3):
                    mm = pe.transpose(ps_p[0:CK[k], k * B:(k + 1) * B], ex[0:B, b.u, k * P:k * P + CK[k]],
                                      keep.ident[0:B, 0:B])
                mm.then_inc(s_exT, 1)

            def attend(b):
                pe.wait_ge(a_exT, done(b.s))
                pe.wait_ge(ld_cn[b.u], 2 * b.loaded)
                for c in range(DC):
                    for k in range(3):
                        mm = pe.matmul(ps_av[:, c * B:(c + 1) * B], ctxN[0:CK[k], b.u, k, c * P:(c + 1) * P],
                                       exT[0:CK[k], b.u, k, :], start=(k == 0), stop=(k == 2))
                mm.then_inc(s_av, 1)

            def output(b):
                pe.wait_ge(a_av, done(b.s))
                pe.wait_ge(d_x3, done(b.s - 1))
                for k in range(DC):
                    mm = pe.matmul(ps_o[0:B, 0:D], avT[:, b.u, k, :], wvT[:, k, :],
                                   start=(k == 0), stop=(k == DC - 1))
                mm.then_inc(s_out, 1)

            def turn_z(b):
                pe.wait_ge(d_z, done(b.s))
                pe.wait_ge(a_zT, done(b.s - 1))
                for c in range(DC):
                    mm = pe.transpose(ps_z[:, c * B:(c + 1) * B], z[0:B, b.u, c * P:(c + 1) * P],
                                      keep.ident[0:B, 0:B])
                mm.then_inc(s_zT, 1)

            pipeline(pe, [(turn_y, 2), (turn_ex, 0), (turn_z, -2), (query, 2), (attend, 0), (scores, 2), (output, 0)])


TOK = 4 * B


def second_router(nc, io, keep):
    with ExitStack() as ctx:
        sb = lambda name, shape, dt=F32: ctx.enter_context(nc.sbuf_tensor("f_" + name, shape, dt))
        own = ctx.enter_context(semaphores(nc))
        sem = lambda name: own("f_" + name)
        Y3T = keep.Y3T
        RC = RH // P
        rW1 = keep.rW1
        rW2 = keep.view("rW2").rearrange("p (c e) -> p c e", c=RC)
        rb2 = sb("rb2", [P, E1])
        rh = sb("rh", [P, 2, RC, TOK])
        ps_h = [ctx.enter_context(nc.psum_tensor(f"f_ps_h{k}", [P, 512], F32)) for k in range(RC)]
        ps_l = [ctx.enter_context(nc.psum_tensor(f"f_ps_l{k}", [P, 512], F32)) for k in range(2)]
        ld_b, g_pad = sem("ld_b"), sem("g_pad")
        s_h, s_l, a_h, d_l = sem("h_ps"), sem("l_ps"), sem("h"), sem("l")
        block = ctx.enter_context(nc.Block())
        upto = lambda b, f: RC * b.s + f + 1 + 2 * RC

        @block.sync
        def _(sp):
            sp.dma_start(rb2[:, :], io.rows[:, D:D + E1].to_broadcast([P, E1])).then_inc(ld_b, 16)

        @block.gpsimd
        def _(pool):
            pool.memset(keep.LG[:, :, :], NEG).then_inc(g_pad, 1)

        @block.scalar
        def _(act):
            act.sem_inc(a_h, 2 * RC)

            def gelus(b):
                act.wait_ge(s_l, reuse(b.s))
                for f in range(RC):
                    act.wait_ge(s_h, upto(b, f))
                    act.activation(rh[:, b.u, f, :], ps_h[f][:, 0:TOK], ACT.Gelu,
                                   bias=keep.col("rb1", f)).then_inc(a_h, 1)

            pipeline(act, [(gelus, 0)], S * B // TOK)

        @block.vector
        def _(dve):
            dve.sem_inc(d_l, CREDIT)
            dve.wait_ge(g_pad, 1)
            dve.wait_ge(ld_b, 16)

            def logits(b):
                dve.wait_ge(s_l, done(b.s))
                at = bass.ds(4 * b.s, 4) if b.looped else slice(4 * b.s, 4 * b.s + 4)
                dve.tensor_tensor(keep.LG[0:B, at, 0:E1],
                                  ps_l[b.u][0:B, 0:4 * E1].rearrange("p (k e) -> p k e", e=E1),
                                  rb2[0:B, :].unsqueeze(1).to_broadcast([B, 4, E1]), ALU.add).then_inc(d_l, 1)

            pipeline(dve, [(logits, 0)], S * B // TOK)

        @block.tensor
        def _(pe):
            pe.sem_inc(s_h, 2 * RC)
            pe.sem_inc(s_l, CREDIT)
            pe.wait_ge(keep.ld_rW1, 16)

            def hidden(b):
                at = bass.ds(TOK * b.s, TOK) if b.looped else slice(TOK * b.s, TOK * (b.s + 1))
                for f in range(RC):
                    pe.wait_ge(a_h, upto(b, f - RC))
                    for c in range(DC):
                        mm = pe.matmul(ps_h[f][:, 0:TOK], rW1[:, c, f * P:(f + 1) * P], Y3T[:, c, at],
                                       start=(c == 0), stop=(c == DC - 1))
                    mm.then_inc(s_h, 1)

            def logits(b):
                pe.wait_ge(a_h, upto(b, RC - 1))
                pe.wait_ge(d_l, reuse(b.s))
                for k in range(4):
                    out = ps_l[b.u][0:B, k * E1:(k + 1) * E1]
                    for f in range(RC):
                        mm = pe.matmul(out, rh[:, b.u, f, k * B:(k + 1) * B], rW2[:, f, :],
                                       start=(f == 0), stop=(f == RC - 1))
                mm.then_inc(s_l, 1)

            pipeline(pe, [(hidden, 0), (logits, -1)], S * B // TOK)


def finish(nc, io, keep):
    with ExitStack() as ctx:
        own = ctx.enter_context(semaphores(nc))
        sem = lambda name: own("g_" + name)
        got = ctx.enter_context(nc.sbuf_tensor("g_got", [P, S, 2, D], F32))
        part = ctx.enter_context(nc.sbuf_tensor("g_part", [P, 2, D], F32))
        landed, stored = [sem(f"landed{s}") for s in range(S)], sem("stored")
        d_part, d_out = sem("part"), sem("out")
        block = ctx.enter_context(nc.Block())

        @block.gpsimd
        def _(pool):
            for s in range(S):
                for j in range(2):
                    pool.indirect_dma_start(
                        got[0:B, s, j, :], None, keep.outs1,
                        bass.IndirectOffsetOnAxis(ap=keep.gath[0:B, j, s:s + 1], axis=0),
                        bounds_check=keep.outs1.shape[0] - 1, oob_is_err=True).then_inc(landed[s], 16)

        @block.vector
        def _(dve):
            for s in range(S):
                dve.wait_ge(landed[s], 32)
                if s >= 2:
                    dve.wait_ge(d_out, s - 1)
                dve.scalar_tensor_tensor(out=part[0:B, s % 2, :], in0=got[0:B, s, 0, :],
                                         scalar=keep.W2[0:B, 0, s:s + 1], in1=keep.X[0:B, s, :],
                                         op0=ALU.mult, op1=ALU.add).then_inc(d_part, 1)
                dve.wait_ge(d_part, s + 1)
                dve.scalar_tensor_tensor(out=keep.X[0:B, s, :], in0=got[0:B, s, 1, :],
                                         scalar=keep.W2[0:B, 1, s:s + 1], in1=part[0:B, s % 2, :],
                                         op0=ALU.mult, op1=ALU.add).then_inc(d_out, 1)

        @block.sync
        def _(sp):
            for s in range(S):
                sp.wait_ge(d_out, s + 1)
                sp.dma_start(io.out[s], keep.X[0:B, s, :]).then_inc(stored, 16)
            sp.wait_ge(stored, 16 * S)


COLS = {}
WIDTH = 0
for _name, _w in (("ident", P), ("before", P), ("causal", P), ("kmask", G), ("iota8", G),
                  ("bq", DC), ("bk", DC), ("bv", DC), ("ln1w", DC), ("ln1b", DC), ("ln2w", DC),
                  ("ln2b", DC), ("rb1", RH // P), ("fills", 16), ("thresholds", 5), ("eps", 1),
                  ("router", DC * E0), ("rW2", (RH // P) * E1)):
    COLS[_name] = (WIDTH, _w)
    WIDTH += _w


def laid_out(w):
    f = lambda a: np.ascontiguousarray(a, dtype=a.dtype)
    chunks = lambda a: a.reshape(a.shape[0] // P, P, a.shape[1]).transpose(1, 0, 2)
    L0 = {k[9:]: v for k, v in w.items() if k.startswith("L0_xattn_")}
    F0 = {k[7:]: v for k, v in w.items() if k.startswith("L0_ffn_")}
    L1 = {k[9:]: v for k, v in w.items() if k.startswith("L1_xattn_")}
    F1 = {k[7:]: v for k, v in w.items() if k.startswith("L1_ffn_")}
    p = np.arange(P)
    c = np.zeros((P, WIDTH), np.float32)

    def put(name, a):
        at, n = COLS[name]
        c[:a.shape[0], at:at + n] = a

    put("ident", np.eye(P))
    put("before", p[:, None] < p[None, :])
    put("causal", np.where(p[None, :] % T <= p[:, None] % T, 0.0, NEG))
    put("kmask", p[:, None] // HD == np.arange(G)[None, :])
    put("iota8", np.broadcast_to(np.arange(G), (P, G)))
    put("eps", np.full((P, 1), EPS))
    put("fills", np.broadcast_to(np.arange(16), (P, 16)))
    put("thresholds", np.broadcast_to(TILE1 * np.arange(5), (P, 5)))
    for name, v in (("bq", L0["bq"]), ("bk", L0["bk"]), ("bv", L0["bv"]), ("ln1w", F0["ln1_weight"]),
                    ("ln1b", F0["ln1_bias"]), ("ln2w", F0["ln2_weight"]), ("ln2b", F0["ln2_bias"]),
                    ("rb1", F1["rb1"])):
        put(name, v.reshape(-1, P).T)
    put("router", chunks(F0["router_weight"]).reshape(P, -1))
    put("rW2", chunks(F1["rW2"]).reshape(P, -1))
    qkv = F0["qkv_weight"].reshape(G, QJ + 2, HD, D).transpose(1, 0, 2, 3).reshape(4 * P, D)
    proj = F0["proj_weight"].reshape(D, G, QJ, HD).transpose(2, 1, 3, 0).reshape(D, D)
    return {
        "x": f(w["x"]), "ctx": f(w["ctx_1024"]),
        "ctxT": f(w["ctx_1024"].transpose(0, 2, 1).reshape(S, DC, P, CTX).transpose(0, 2, 1, 3)),
        "mask": f(w["mask_BxS2_ik1"][:, None, :]),
        "consts": c,
        "rows": f(np.concatenate([L0["bo"], F1["rb2"]])[None, :]),
        "w_a": f(np.concatenate([chunks(L0["Wq"]), chunks(L0["Wk"]), chunks(L0["Wv"]),
                                 chunks(L0["Wo"].T)], axis=2)),
        "w_qkvT": f(chunks(qkv.T)),
        "w_projT": f(chunks(proj)),
        "w_e": f(np.concatenate([chunks(L1["Wq"]), chunks(L1["Wk"]), chunks(L1["Wv"].T),
                                 chunks(F1["rW1"])], axis=2)),
        "w_f0": f(np.concatenate([np.stack([chunks(a).reshape(P, -1) for a in F0["moe_w1"]]),
                                  np.stack([chunks(a).reshape(P, -1) for a in F0["moe_w2"]])], axis=2)),
        "w_f1": f(np.concatenate([np.stack([chunks(a).reshape(P, -1) for a in F1["We1"]]),
                                  np.stack([chunks(a).reshape(P, -1) for a in F1["We2"]])], axis=2)),
        "be1": f(F1["be1"].reshape(E1, FC, P).transpose(0, 2, 1)),
        "be2": f(F1["be2"][:, None, :]),
    }



class Kept:
    pass


def two_layers(nc, io):
    keep = Kept()
    with ExitStack() as ctx:
        sb = lambda name, shape, dt=F32: ctx.enter_context(nc.sbuf_tensor(name, shape, dt))
        keep.consts = sb("consts", [P, WIDTH])
        keep.ld_consts = ctx.enter_context(nc.semaphore("ld_consts"))
        view = lambda name: keep.consts[:, COLS[name][0]:sum(COLS[name])]
        keep.view = view
        keep.col = lambda name, c: view(name)[:, c:c + 1]
        keep.ident, keep.kmask = view("ident"), view("kmask")
        keep.half = sb("half", [P, 1])
        keep.zeros = sb("zeros", [P, D])
        dram = lambda name, shape: nc.dram_tensor(name, shape, F32, kind="Internal").ap()
        keep.values = dram("values", (T, B, P))
        keep.slots0, keep.outs0 = dram("slots0", (E0 * CAP, D)), dram("outs0", (E0 * CAP, D))
        keep.slots1, keep.outs1 = dram("slots1", (TILES1 * TILE1, D)), dram("outs1", (TILES1 * TILE1, D))
        keep.zeroed = ctx.enter_context(nc.semaphore("zeroed"))
        keep.ld_proj = ctx.enter_context(nc.semaphore("ld_proj"))
        keep.ld_rW1 = ctx.enter_context(nc.semaphore("ld_rW1"))
        keep.vx_zero = ctx.enter_context(nc.semaphore("vx_zero"))
        keep.X = sb("X", [P, S, D])
        keep.Z = sb("Z", [P, S, D])
        keep.LG = sb("LG", [P, S, G])
        keep.V8 = sb("V8", [P, S, G])
        keep.I8 = sb("I8", [P, S, G], U32)
        keep.W2 = sb("W2", [P, 2, S])
        keep.scat = sb("scat", [P, 2, S], I32)
        keep.gath = sb("gath", [P, 2, S], I32)
        keep.tile_expert = sb("tile_expert", [P, TILES1], I32)
        keep.A = sb("A_e", [P, DC, D])
        keep.wvT = sb("wvT_e", [P, DC, D])
        with ExitStack() as first:
            sb0 = lambda name, shape, dt=F32: first.enter_context(nc.sbuf_tensor(name, shape, dt))
            keep.projT = sb0("projT", [P, QJ, D])
            keep.Y1 = sb0("Y1", [P, S, D])
            keep.Q = sb0("Q", [P, B, QJ, T])
            keep.K = sb0("K", [P, B, T])
            keep.VX = sb0("VX", [P, B, P])
            first_cross_attention(nc, io, keep)
            keep.AT = sb0("AT", [P, QJ, S, B])
            self_attention(nc, io, keep)
            project_and_score(nc, io, keep)
        route(nc, io, keep, False)
        expert_tiles(nc, io, keep, False)
        keep.Y3T = sb("Y3T", [P, DC, S * B])
        keep.rW1 = sb("rW1", [P, DC, RH])
        second_cross_attention(nc, io, keep)
        second_router(nc, io, keep)
        route(nc, io, keep, True)
        expert_tiles(nc, io, keep, True)
        finish(nc, io, keep)


def kernel(**inputs):
    import concourse.bacc as bacc
    from concourse.bass_utils import run_bass_kernel_spmd

    arrays = laid_out({k: np.asarray(v) for k, v in inputs.items()})
    nc = bacc.Bacc("TRN2", target_bir_lowering=False, num_devices=1)
    io = Kept()
    for name, a in arrays.items():
        io.__dict__[name] = nc.dram_tensor(f"in_{name}", a.shape, mybir.dt.from_np(a.dtype),
                                           kind="ExternalInput").ap()
    io.out = nc.dram_tensor("out_0", (S, B, D), F32, kind="ExternalOutput").ap()
    two_layers(nc, io)
    r = run_bass_kernel_spmd(nc, [{f"in_{k}": a for k, a in arrays.items()}], core_ids=[0])
    return r.results[0]["out_0"]
```
